# Optimizing a Trainium2 kernel written in Bass

```python
import numpy as np
import jax
import jax.numpy as jnp

def _softmax(x, axis=-1):
    return jax.nn.softmax(x, axis=axis)

def _gelu(x):
    return jax.nn.gelu(x, approximate=True)

def _silu(x):
    return jax.nn.silu(x)

def _sigmoid(x):
    return jax.nn.sigmoid(x)

def _layernorm(x, axis=-1, eps=1e-05):
    m = jnp.mean(x, axis=axis, keepdims=True)
    v = jnp.var(x, axis=axis, keepdims=True)
    return (x - m) / jnp.sqrt(v + eps)

def _scatter_add(tgt, idx, src, axis=0):
    return tgt.at[idx].add(src)

def _segment_sum(src, seg, n):
    return jax.ops.segment_sum(src, seg, n)
kernel_name = 'mk_audio_tower_d2_tok_audfeat1024_r4_10583d'

def setup_inputs(seed: int=0):
    np.random.seed(seed)
    _w = jnp.asarray

    def _rec_inputs():
        import jax
        import jax.numpy as jnp
        _rk = jax.random.key(seed)
        x = 7.22013e-05 + 1.00017 * jax.random.normal(jax.random.fold_in(_rk, 1), (64, 64, 256), jnp.float32)
        return x
    x = _rec_inputs()

    def _L0_tok_setup():
        import jax, jax.numpy as jnp
        import numpy as np
        PATCH_LEN = 16
        STRIDE = 8
        D_MODEL = 256

        def _patchify(x):
            B, V, T = x.shape
            pad = jnp.broadcast_to(x[:, :, -1:], (B, V, STRIDE))
            xp = jnp.concatenate([x, pad], axis=-1)
            L = (T + STRIDE - PATCH_LEN) // STRIDE + 1
            idx = jnp.arange(L)[:, None] * STRIDE + jnp.arange(PATCH_LEN)[None, :]
            patches = xp[:, :, idx]
            patches = jnp.transpose(patches, (0, 2, 1, 3))
            return patches.reshape(B, L, V * PATCH_LEN)
        key = jax.random.key(seed)
        k0, k1, k2, k3, k4 = jax.random.split(key, 5)
        B, V, T = (32, 64, 1024)
        c_in = V * PATCH_LEN
        x = jax.random.normal(k0, (B, V, T), dtype=jnp.float32)
        s1 = 1.0 / np.sqrt(c_in)
        s2 = 1.0 / np.sqrt(D_MODEL)
        W1 = jax.random.uniform(k1, (c_in, D_MODEL), jnp.float32, -s1, s1)
        b1 = jax.random.uniform(k2, (D_MODEL,), jnp.float32, -s1, s1)
        W2 = jax.random.uniform(k3, (D_MODEL, D_MODEL), jnp.float32, -s2, s2)
        b2 = jax.random.uniform(k4, (D_MODEL,), jnp.float32, -s2, s2)
        return {'x': x, 'W1': W1, 'b1': b1, 'W2': W2, 'b2': b2}
    _L0_tok_all = _L0_tok_setup()
    _L0_tok_in = {k: v for k, v in _L0_tok_all.items() if k in ('W1', 'b1', 'W2', 'b2')}
    del _L0_tok_all

    def _L0_attn_setup():
        import jax, jax.numpy as jnp
        import numpy as np
        B, S, H, NH = (2, 512, 256, 16)
        HD = H // NH
        SCALE = HD ** (-0.5)
        EPS = 1e-05

        def _weight_quant(w):
            scale = 1.0 / jnp.clip(jnp.mean(jnp.abs(w)), 1e-05)
            wq = jnp.clip(jnp.round(w * scale), -1.0, 1.0) / scale
            return w + jax.lax.stop_gradient(wq - w)

        def _act_quant(x):
            scale = 127.0 / jnp.clip(jnp.max(jnp.abs(x), axis=-1, keepdims=True), 1e-05)
            y = jnp.clip(jnp.round(x * scale), -128.0, 127.0) / scale
            return x + jax.lax.stop_gradient(y - x)

        def _bitlinear(x, w):
            mu = jnp.mean(x, axis=(1, 2), keepdims=True)
            var = jnp.var(x, axis=(1, 2), keepdims=True)
            x_norm = (x - mu) * jax.lax.rsqrt(var + EPS)
            return _act_quant(x_norm) @ _weight_quant(w).T
        key = jax.random.key(seed)
        kx, k1, k2, k3, k4 = jax.random.split(key, 5)
        x = jax.random.normal(kx, (B, S, H), dtype=jnp.float32)
        init = 0.02
        w_q = jax.random.normal(k1, (H, H), dtype=jnp.float32) * init
        w_k = jax.random.normal(k2, (H, H), dtype=jnp.float32) * init
        w_v = jax.random.normal(k3, (H, H), dtype=jnp.float32) * init
        w_o = jax.random.normal(k4, (H, H), dtype=jnp.float32) * init
        return {'x': x, 'w_q': w_q, 'w_k': w_k, 'w_v': w_v, 'w_o': w_o}
    _L0_attn_all = _L0_attn_setup()
    _L0_attn_in = {k: v for k, v in _L0_attn_all.items() if k in ('w_q', 'w_k', 'w_v', 'w_o')}
    del _L0_attn_all

    def _L0_ffn_setup():
        import jax, jax.numpy as jnp
        import numpy as np
        EXPERT_NUM = 8
        CAPACITY = 100
        key = jax.random.key(seed)
        k1, k2, k3 = jax.random.split(key, 3)
        B, S, H, E = (8, 512, 256, EXPERT_NUM)
        x = jax.random.normal(k1, (B, S, H), dtype=jnp.float32)
        w_gate = jax.random.normal(k2, (H, E), dtype=jnp.float32) * 0.02
        w_expert = jax.random.normal(k3, (H, H), dtype=jnp.float32) * 0.02
        b_expert = jnp.zeros((H,), dtype=jnp.float32)
        return {'x': x, 'w_gate': w_gate, 'w_expert': w_expert, 'b_expert': b_expert}
    _L0_ffn_all = _L0_ffn_setup()
    _L0_ffn_in = {k: v for k, v in _L0_ffn_all.items() if k in ('w_gate', 'w_expert', 'b_expert')}
    del _L0_ffn_all

    def _L1_attn_setup():
        import jax, jax.numpy as jnp
        import numpy as np
        B, L, D = (2, 2048, 256)
        key = jax.random.key(seed)
        ks = jax.random.split(key, 6)
        x = jax.random.normal(ks[0], (B, L, D), dtype=jnp.float32)
        mag = jnp.abs(jax.random.normal(ks[1], (D,), dtype=jnp.float32))
        ang = (2.0 * np.pi * jnp.arange(D) / D).astype(jnp.float32)
        phazor_real = mag * jnp.cos(ang)
        phazor_imag = mag * jnp.sin(ang)
        phazor_init_real = jax.random.normal(ks[2], (D,), dtype=jnp.float32)
        phazor_init_imag = jax.random.normal(ks[3], (D,), dtype=jnp.float32)
        last_conv_real = jax.random.normal(ks[4], (D,), dtype=jnp.float32)
        last_conv_imag = jax.random.normal(ks[5], (D,), dtype=jnp.float32)
        return {'x': x, 'phazor_real': phazor_real, 'phazor_imag': phazor_imag, 'phazor_init_real': phazor_init_real, 'phazor_init_imag': phazor_init_imag, 'last_conv_real': last_conv_real, 'last_conv_imag': last_conv_imag}
    _L1_attn_all = _L1_attn_setup()
    _L1_attn_in = {k: v for k, v in _L1_attn_all.items() if k in ('phazor_real', 'phazor_imag', 'phazor_init_real', 'phazor_init_imag', 'last_conv_real', 'last_conv_imag')}
    del _L1_attn_all

    def _L1_ffn_setup():
        import jax, jax.numpy as jnp
        import numpy as np
        E = 8
        TOP_K = 2
        DIM = 256
        HID = 512
        key = jax.random.key(seed)
        k1, k2, k3, k4, k5 = jax.random.split(key, 5)
        s = 0.02
        x = jax.random.normal(k1, (2, 512, DIM), dtype=jnp.float32)
        Wg = jax.random.normal(k2, (DIM, E), dtype=jnp.float32) * s
        W1 = jax.random.normal(k3, (E, DIM, HID), dtype=jnp.float32) * s
        W2 = jax.random.normal(k4, (E, DIM, HID), dtype=jnp.float32) * s
        W3 = jax.random.normal(k5, (E, HID, DIM), dtype=jnp.float32) * s
        return {'x': x, 'Wg': Wg, 'W1': W1, 'W2': W2, 'W3': W3}
    _L1_ffn_all = _L1_ffn_setup()
    _L1_ffn_in = {k: v for k, v in _L1_ffn_all.items() if k in ('Wg', 'W1', 'W2', 'W3')}
    del _L1_ffn_all
    return {'x': x, 'L0_tok_W1': _L0_tok_in['W1'], 'L0_tok_b1': _L0_tok_in['b1'], 'L0_tok_W2': _L0_tok_in['W2'], 'L0_tok_b2': _L0_tok_in['b2'], 'L0_attn_w_q': _L0_attn_in['w_q'], 'L0_attn_w_k': _L0_attn_in['w_k'], 'L0_attn_w_v': _L0_attn_in['w_v'], 'L0_attn_w_o': _L0_attn_in['w_o'], 'L0_ffn_w_gate': _L0_ffn_in['w_gate'], 'L0_ffn_w_expert': _L0_ffn_in['w_expert'], 'L0_ffn_b_expert': _L0_ffn_in['b_expert'], 'L1_attn_phazor_real': _L1_attn_in['phazor_real'], 'L1_attn_phazor_imag': _L1_attn_in['phazor_imag'], 'L1_attn_phazor_init_real': _L1_attn_in['phazor_init_real'], 'L1_attn_phazor_init_imag': _L1_attn_in['phazor_init_imag'], 'L1_attn_last_conv_real': _L1_attn_in['last_conv_real'], 'L1_attn_last_conv_imag': _L1_attn_in['last_conv_imag'], 'L1_ffn_Wg': _L1_ffn_in['Wg'], 'L1_ffn_W1': _L1_ffn_in['W1'], 'L1_ffn_W2': _L1_ffn_in['W2'], 'L1_ffn_W3': _L1_ffn_in['W3']}

def reference(x, L0_tok_W1, L0_tok_b1, L0_tok_W2, L0_tok_b2, L0_attn_w_q, L0_attn_w_k, L0_attn_w_v, L0_attn_w_o, L0_ffn_w_gate, L0_ffn_w_expert, L0_ffn_b_expert, L1_attn_phazor_real, L1_attn_phazor_imag, L1_attn_phazor_init_real, L1_attn_phazor_init_imag, L1_attn_last_conv_real, L1_attn_last_conv_imag, L1_ffn_Wg, L1_ffn_W1, L1_ffn_W2, L1_ffn_W3):
    import jax
    import jax.numpy as jnp

    def _L0_tok_ref(x, W1, b1, W2, b2):
        import jax, jax.numpy as jnp
        import numpy as np
        PATCH_LEN = 16
        STRIDE = 8
        D_MODEL = 256

        def _patchify(x):
            B, V, T = x.shape
            pad = jnp.broadcast_to(x[:, :, -1:], (B, V, STRIDE))
            xp = jnp.concatenate([x, pad], axis=-1)
            L = (T + STRIDE - PATCH_LEN) // STRIDE + 1
            idx = jnp.arange(L)[:, None] * STRIDE + jnp.arange(PATCH_LEN)[None, :]
            patches = xp[:, :, idx]
            patches = jnp.transpose(patches, (0, 2, 1, 3))
            return patches.reshape(B, L, V * PATCH_LEN)
        p = _patchify(x)
        h = jax.nn.relu(jnp.einsum('blc,cd->bld', p, W1) + b1)
        out = jnp.einsum('bld,de->ble', h, W2) + b2
        return out

    def _L0_attn_ref(x, w_q, w_k, w_v, w_o):
        import jax, jax.numpy as jnp
        import numpy as np
        B, S, H, NH = (2, 512, 256, 16)
        HD = H // NH
        SCALE = HD ** (-0.5)
        EPS = 1e-05

        def _weight_quant(w):
            scale = 1.0 / jnp.clip(jnp.mean(jnp.abs(w)), 1e-05)
            wq = jnp.clip(jnp.round(w * scale), -1.0, 1.0) / scale
            return w + jax.lax.stop_gradient(wq - w)

        def _act_quant(x):
            scale = 127.0 / jnp.clip(jnp.max(jnp.abs(x), axis=-1, keepdims=True), 1e-05)
            y = jnp.clip(jnp.round(x * scale), -128.0, 127.0) / scale
            return x + jax.lax.stop_gradient(y - x)

        def _bitlinear(x, w):
            mu = jnp.mean(x, axis=(1, 2), keepdims=True)
            var = jnp.var(x, axis=(1, 2), keepdims=True)
            x_norm = (x - mu) * jax.lax.rsqrt(var + EPS)
            return _act_quant(x_norm) @ _weight_quant(w).T
        bsz, seq_len, hidden = x.shape
        q = _bitlinear(x, w_q).reshape(bsz, seq_len, NH, HD).transpose(0, 2, 1, 3)
        k = _bitlinear(x, w_k).reshape(bsz, seq_len, NH, HD).transpose(0, 2, 1, 3)
        v = _bitlinear(x, w_v).reshape(bsz, seq_len, NH, HD).transpose(0, 2, 1, 3)
        scores = jnp.einsum('bhqd,bhkd->bhqk', q, k) * SCALE
        attn = jax.nn.softmax(scores, axis=-1)
        out = jnp.einsum('bhqk,bhkd->bhqd', attn, v)
        out = out.transpose(0, 2, 1, 3).reshape(bsz, seq_len, hidden)
        return _bitlinear(out, w_o)

    def _L0_ffn_ref(x, w_gate, w_expert, b_expert):
        import jax, jax.numpy as jnp
        import numpy as np
        EXPERT_NUM = 8
        CAPACITY = 100
        B, S, H = x.shape
        E, C = (EXPERT_NUM, CAPACITY)
        hs = x.reshape(-1, H)
        logits = hs @ w_gate
        probs = jax.nn.softmax(logits, axis=1)
        best = jnp.argmax(probs, axis=1)
        mask = jax.nn.one_hot(best, E, dtype=jnp.int32)
        gate = jnp.sum(probs * mask.astype(probs.dtype), axis=1)
        locations = jnp.cumsum(mask, axis=0) - 1
        mask = mask * (locations < C).astype(jnp.int32)
        loc_sum = jnp.sum(locations * mask, axis=1)
        new_gates = gate[:, None] * mask.astype(probs.dtype)
        loc_oh = jax.nn.one_hot(loc_sum, C, dtype=probs.dtype)
        combine = new_gates[:, :, None] * loc_oh[:, None, :]
        dispatch = (combine != 0).astype(hs.dtype)
        dispatched = jnp.einsum('tec,th->ech', dispatch, hs).reshape(E * C, H)
        expert_out = dispatched @ w_expert + b_expert
        combined = combine.reshape(-1, E * C) @ expert_out
        return combined.reshape(B, S, H)

    def _L1_attn_ref(x, phazor_real, phazor_imag, phazor_init_real, phazor_init_imag, last_conv_real, last_conv_imag):
        import jax, jax.numpy as jnp
        import numpy as np
        B, L, D = (2, 2048, 256)
        b, length, dim = x.shape
        dtype = x.dtype
        ph = jnp.exp(-(phazor_real * phazor_real + phazor_imag * phazor_imag)) * jnp.exp(1j * jnp.arctan2(phazor_imag, phazor_real))
        prog = jnp.power(ph[None, :], jnp.arange(length)[:, None])
        pinit = phazor_init_real + 1j * phazor_init_imag
        filt = prog * pinit[None, :]
        filt_fft = jnp.fft.fft(filt, n=2 * length, axis=0)
        x_fft = jnp.fft.fft(x.astype(jnp.complex64), n=2 * length, axis=1)
        conv = jnp.fft.ifft(filt_fft[None, :, :] * x_fft, axis=1)[:, :length, :]
        last = (last_conv_real + 1j * last_conv_imag)[None, None, :]
        conv_with_past = conv + last * prog[None, :, :] * ph[None, None, :]
        return conv_with_past.real.astype(dtype)

    def _L1_ffn_ref(x, Wg, W1, W2, W3):
        import jax, jax.numpy as jnp
        import numpy as np
        E = 8
        TOP_K = 2
        DIM = 256
        HID = 512
        B, T, C = x.shape
        xf = x.reshape(-1, C)
        logits = xf @ Wg
        top_w, top_i = jax.lax.top_k(logits, TOP_K)
        top_w = jax.nn.softmax(top_w, axis=-1)
        one_hot = jax.nn.one_hot(top_i, E, dtype=xf.dtype)
        combine = jnp.einsum('nk,nke->ne', top_w, one_hot)
        h = jnp.einsum('nc,ech->enh', xf, W1)
        g = jnp.einsum('nc,ech->enh', xf, W2)
        y = jnp.einsum('enh,ehc->enc', jax.nn.silu(h) * g, W3)
        out = jnp.einsum('enc,ne->nc', y, combine)
        return out.reshape(B, T, C)
    h = _L0_tok_ref(x, L0_tok_W1, L0_tok_b1, L0_tok_W2, L0_tok_b2)
    h = h + _L0_attn_ref(_layernorm(h, axis=-1), L0_attn_w_q, L0_attn_w_k, L0_attn_w_v, L0_attn_w_o)
    h = h + _L0_ffn_ref(_layernorm(h, axis=-1), L0_ffn_w_gate, L0_ffn_w_expert, L0_ffn_b_expert)
    h = h + _L1_attn_ref(_layernorm(h, axis=-1), L1_attn_phazor_real, L1_attn_phazor_imag, L1_attn_phazor_init_real, L1_attn_phazor_init_imag, L1_attn_last_conv_real, L1_attn_last_conv_imag)
    h = h + _L1_ffn_ref(_layernorm(h, axis=-1), L1_ffn_Wg, L1_ffn_W1, L1_ffn_W2, L1_ffn_W3)
    return h

_drawn_inputs = setup_inputs


def setup_inputs(seed=0):
    import zlib

    import numpy as np

    out = dict(_drawn_inputs(seed))
    spreads = {'L0_ffn_b_expert': (0.0, 0.411)}
    factors = {'L0_attn_w_q': 4.425,
     'L0_attn_w_k': 4.028,
     'L1_ffn_Wg': 7.398,
     'L1_ffn_W1': 6.893,
     'L1_ffn_W2': 6.738,
     'L1_ffn_W3': 6.773}
    for name, (base, spread) in spreads.items():
        noise = np.random.default_rng([zlib.crc32(name.encode()), seed]).standard_normal(out[name].shape)
        drawn = base * np.exp(spread * noise) if base else spread * noise
        out[name] = jnp.asarray(drawn.astype(out[name].dtype))
    for name, factor in factors.items():
        out[name] = (out[name] * factor).astype(out[name].dtype)
    return out
```

```python
from contextlib import ExitStack

import concourse.bass as bass
from concourse import mybir

F32 = mybir.dt.float32
BF16 = mybir.dt.bfloat16
I32 = mybir.dt.int32
ALU = mybir.AluOpType
ACT = mybir.ActivationFunctionType
AX = mybir.AxisListType.X


def audio_tower_kernel(
    nc, x, W1, b1, W2, b2, w_q, w_k, w_v, w_o, w_gate, w_expert, b_expert,
    ph_re, ph_im, pi_re, pi_im, lc_re, lc_im, Wg, M1, M2, M3, out,
):
    P = 128
    B, V, T_IN = x.shape
    DM = W1.shape[1]
    CH = DM // P
    STRIDE = 8
    L = T_IN // STRIDE
    NTOK = B * L
    TILES = NTOK // P
    TS = 4
    STEPS = TILES // TS
    SB = B // STEPS
    SN = TS * P
    BT = P // L
    NH = 16
    HD = DM // NH
    DBLK = DM // 32
    VW = HD + 1
    E = w_gate.shape[1]
    DE = DM + E
    CAPACITY = 100
    HID = M1.shape[2]
    HC = HID // P
    EPS = 1e-5
    MAGIC = 12582912.0
    SLOTS = (2 * NTOK + E * (P - 1)) // P
    assert L == 32 and BT == TS and HD == 16 and SLOTS % 2 == 1

    xs = nc.dram_tensor("slot_rows_in", [SLOTS * P, DM], F32, kind="Internal").ap()
    ys = nc.dram_tensor("slot_rows_out", [SLOTS * P, DM], F32, kind="Internal").ap()
    out_rows = out.rearrange("b l d -> (b l) d").rearrange("(t p) d -> p t d", p=P)
    xs_tiles = xs.rearrange("(a p) d -> p a d", p=P)
    ys_tiles = ys.rearrange("(a p) d -> p a d", p=P)

    with ExitStack() as ctx:
        def sb(name, shape, dt=F32):
            return ctx.enter_context(nc.sbuf_tensor(name, shape, dt))

        def sem(name):
            return ctx.enter_context(nc.semaphore(name))

        def part(t, lo, n):
            a = t[:]
            if len(a.shape) > 2:
                a = a.rearrange(" ".join(["p"] + [f"d{i}" for i in range(len(a.shape) - 1)]) + " -> p ("
                                + " ".join(f"d{i}" for i in range(len(a.shape) - 1)) + ")")
            return a[:, lo:lo + n]

        ident_b = sb("ident_b", [P, P], BF16)
        ident = sb("ident", [P, P])
        ones = sb("ones", [P, P])
        ones_b = sb("ones_b", [P, P], BF16)
        tri_b = sb("tri_b", [P, P], BF16)
        batch_mean = sb("batch_mean", [P, P])
        mhalf = sb("mhalf", [P, TS])
        rank_w = sb("rank_w", [P, E])
        slot_no = sb("slot_no", [P, SLOTS])
        reset_t = sb("reset_t", [P, E, TILES])
        ones_e = sb("ones_e", [P, E])
        zrow = sb("zrow", [P, DM])

        W2s = sb("W2s", [P, CH, DM])
        b1c = sb("b1c", [P, CH])
        b2r = sb("b2r", [P, DM])
        WT = sb("WT", [P, CH, 4, DM], BF16)
        WE = sb("WE", [P, CH, DE])
        bE = sb("bE", [P, DE])
        Wgs = sb("Wgs", [P, CH, E])
        M1s = sb("M1s", [P, E, CH, HID])
        M2s = sb("M2s", [P, E, CH, HID])
        M3s = sb("M3s", [P, E, HC, DM])
        wm = sb("wm", [P, 4])
        wmi = sb("wmi", [P, 4])
        wsum = sb("wsum", [P, 4])

        H = sb("H", [P, TILES, DM])
        EO = sb("EO", [P, TILES, DE])
        x1 = sb("x1", [P, TS, DM])
        xq = sb("xq", [P, TS, DM], BF16)
        xqT = sb("xqT", [P, CH, SN], BF16)
        oq = sb("oq", [P, TS, DM], BF16)
        oqT = sb("oqT", [P, CH, SN], BF16)
        qtok = sb("qtok", [P, TS, DM])
        ktok = sb("ktok", [P, TS, DBLK, 2, 2, HD])
        vtok = sb("vtok", [P, TS, NH, VW])
        QT = sb("QT", [P, TS, DBLK, 32])
        KT = sb("KT", [P, TS, DBLK, 64])
        Vp = sb("Vp", [P, BT, NH, VW])
        Eb = sb("Eb", [P, 2, NH, 32])
        PT = sb("PT", [P, 2, NH, 32])
        O = sb("O", [P, TS, DM])

        X4 = EO
        W1s = part(EO, 4 * DE, STRIDE * DM).rearrange("p (r d) -> p r d", r=STRIDE)
        h1T = part(EO, 12 * DE, CH * SN).rearrange("p (c n) -> p c n", c=CH)
        xin = part(M3s, 0, 2 * SB * T_IN).rearrange("p (u b t) -> p u b t", u=2, b=SB)
        xT = part(x1, 0, CH * SN).rearrange("p (c n) -> p c n", c=CH)
        wraw = part(KT, 0, 4 * CH * DM).rearrange("p (w n) -> p w n", w=4)
        wter = PT[:].rearrange("p a h k -> p (a h k)").bitcast(BF16).rearrange("p (w c n) -> p w c n", w=4, c=CH)
        RT = part(qtok, 0, CH * SN)
        uR = part(ktok, 0, CH * SN)
        uI = part(ktok, CH * SN, CH * SN)
        ra = part(Eb, 0, 8 * TILES * E).rearrange("p (s t e) -> p s t e", s=8, t=TILES)
        cmp = part(PT, 0, SLOTS * E).rearrange("p (a e) -> p a e", e=E)
        xrow = part(KT, 0, 2 * DM).rearrange("p (u d) -> p u d", u=2)
        xrT = part(KT, 2 * DM, 2 * DM).rearrange("p (u c n) -> p u c n", u=2, c=CH)
        actT = part(KT, 4 * DM, 2 * HID).rearrange("p (u c n) -> p u c n", u=2, c=HC)
        sil = part(QT, 0, 2 * HID).rearrange("p (u n) -> p u n", u=2)
        yrow = part(O, 0, 2 * DM).rearrange("p (u d) -> p u d", u=2)
        back = [part(m, 0, TILES * DM).rearrange("p (t d) -> p t d", t=TILES) for m in (M1s, M2s)]

        def stats(n):
            return {k: sb(f"{k}_{n}", s) for k, s in dict(
                st=[P, TS, 6], mv=[P, TS, 2], ve=[P, TS], rstd=[P, TS], bs=[P, 2, TS], bv=[P, 2, TS], bve=[P, TS],
                rsb=[P, TS], am=[P, TS], sa=[P, TS], s=[P, TS], sw=[P, 4, TS]).items()}

        SB1, SD, SE = stats("in"), stats("att"), stats("ssm")
        mx = sb("mx", [P, 2, NH])
        rec = sb("rec", [P, TS, NH])
        vec = sb("vec", [P, 6, CH])
        sv = sb("sv", [P, 20, CH])
        CT = sb("CT", [P, CH, L + 1])
        ST = sb("ST", [P, CH, L + 1])
        Wr = sb("Wr", [P, CH, L])
        Wi = sb("Wi", [P, CH, L])
        tmpT = sb("tmpT", [P, 4, CH, L])
        lg = sb("lg", [P, TILES, E])
        rs = sb("rs", [P, 10, TILES])
        cum = sb("cum", [P, 2, E, TILES])
        mask_b = sb("mask_b", [P, TILES, E], BF16)
        pos_i = sb("pos_i", [P, 2, TILES], I32)
        tb = sb("tb", [P, 6, E])
        exf = sb("exf", [P, SLOTS])
        exi = sb("exi", [P, SLOTS], I32)

        psum = ctx.enter_context(nc.psum_tensor("psum", [P, 8, 512], F32))
        bank = [psum[:, i, :] for i in range(8)]

        def banks(i):
            return psum[:, i:i + 2, :].rearrange("p a b -> p (a b)")

        d_w1, d_x0, d_x1, d_w2, d_b, d_att, d_we = (
            sem(n) for n in "d_w1 d_x0 d_x1 d_w2 d_b d_att d_we".split())
        d_vec, d_moe, d_m3, d_zero, d_vp, d_xs, d_out = (
            sem(n) for n in "d_vec d_moe d_m3 d_zero d_vp d_xs d_out".split())
        d_slot0, d_slot1, d_ys0, d_ys1 = (
            sem(n) for n in "d_slot0 d_slot1 d_ys0 d_ys1".split())
        g_const, g_pow, g_ui, g_uc = (
            sem(n) for n in "g_const g_pow g_ui g_uc".split())
        v_chain, v_h, v_ask, v_y, v_xq, v_ob, v_oq = (
            sem(n) for n in "v_chain v_h v_ask v_y v_xq v_ob v_oq".split())
        v_hd, v_x2, v_sc, v_qk, v_sub, v_pt, v_o = (
            sem(n) for n in "v_hd v_x2 v_sc v_qk v_sub v_pt v_o".split())
        v_wabs, v_wt, v_xc, v_ur, v_yc, v_x4, v_mask = (
            sem(n) for n in "v_wabs v_wt v_xc v_ur v_yc v_x4 v_mask".split())
        v_mask2, v_cum, v_slots, v_exp, v_act, v_xx, v_eo = (
            sem(n) for n in "v_mask2 v_cum v_slots v_exp v_act v_xx v_eo".split())
        v_hfin, v_ra = (
            sem(n) for n in "v_hfin v_ra".split())
        p_wsum, p_wt, p_l1, p_l2, p_bv, p_xt, p_qkv = (
            sem(n) for n in "p_wsum p_wt p_l1 p_l2 p_bv p_xt p_qkv".split())
        p_s, p_pv, p_ob, p_ot, p_o, p_x2, p_e = (
            sem(n) for n in "p_s p_pv p_ob p_ot p_o p_x2 p_e".split())
        p_cum, p_cum2, p_x3, p_y3, p_x4, p_lg, p_xr = (
            sem(n) for n in "p_cum p_cum2 p_x3 p_y3 p_x4 p_lg p_xr".split())
        p_up, p_at, p_dn = (
            sem(n) for n in "p_up p_at p_dn".split())
        a_wt, a_pad, a_h1, a_xt, a_qkv, a_exp, a_ot = (
            sem(n) for n in "a_wt a_pad a_h1 a_xt a_qkv a_exp a_ot".split())
        a_x2, a_x3, a_x4, a_lg, a_gate, a_r, a_xr = (
            sem(n) for n in "a_x2 a_x3 a_x4 a_lg a_gate a_r a_xr".split())
        a_sil, a_at, a_y = (
            sem(n) for n in "a_sil a_at a_y".split())

        d_back = [sem(f"d_back{t}") for t in range(TILES)]

        block = ctx.enter_context(nc.Block())

        def wait(eng, s, n):
            if n > 0:
                eng.wait_ge(s, n)

        def done(slot, lag):
            return max(0, min(STEPS, slot - lag + 1))

        def step_of(slot, lag):
            i = slot - lag
            return i if 0 <= i < STEPS else None

        A_LAG, B_LAG, C_LAG, D_LAG = 0, 1, 2, 3
        SLOTS_OF_STEPS = STEPS + D_LAG

        @block.sync
        def _(sp):
            w1_v = W1.rearrange("(v s r) d -> s v r d", s=2, r=STRIDE)
            xv = x.rearrange("b v t -> v b t")

            def load_x(i):
                s_x = (d_x0, d_x1)[i % 2]
                sp.dma_start(xin[0:64, i % 2], xv[:, SB * i:SB * (i + 1), :]).then_inc(s_x, 16)
                sp.dma_start(xin[64:128, i % 2, :, 0:T_IN - STRIDE],
                             xv[:, SB * i:SB * (i + 1), STRIDE:T_IN]).then_inc(s_x, 16)

            for s in range(2):
                sp.dma_start(W1s[64 * s:64 * s + 64], w1_v[s]).then_inc(d_w1, 16)
            load_x(0)
            for n, w in enumerate((w_q, w_k, w_v, w_o)):
                sp.dma_start(wraw[:, n, :].rearrange("p (c i) -> p c i", c=CH),
                             w.rearrange("(c p) i -> p c i", p=P)).then_inc(d_att, 16)
            sp.dma_start(W2s[:], W2.rearrange("(c p) d -> p c d", p=P)).then_inc(d_w2, 16)
            load_x(1)
            sp.dma_start(WE[:, :, 0:DM], w_expert.rearrange("(c p) d -> p c d", p=P)).then_inc(d_we, 16)
            sp.dma_start(WE[:, :, DM:], w_gate.rearrange("(c p) d -> p c d", p=P)).then_inc(d_we, 16)
            sp.dma_start(Wgs[:], Wg.rearrange("(c p) d -> p c d", p=P)).then_inc(d_we, 16)
            for i in range(2, STEPS):
                sp.wait_ge(p_l1, CH * (i - 1))
                load_x(i)
            sp.dma_start(M1s[:], M1.rearrange("e (c p) h -> p e c h", p=P)).then_inc(d_moe, 16)
            sp.dma_start(M2s[:], M2.rearrange("e (c p) h -> p e c h", p=P)).then_inc(d_moe, 16)
            sp.wait_ge(g_const, 1)
            sp.dma_start(xs_tiles, zrow[:].rearrange("p (a d) -> p a d", a=1).to_broadcast([P, SLOTS, DM])
                         ).then_inc(d_zero, 16)
            for i in range(STEPS):
                sp.wait_ge(a_qkv, TS * (i + 1))
                if i > 0:
                    sp.wait_ge(p_pv, BT * i)
                if i == STEPS - 1:
                    sp.wait_ge(p_l1, CH * STEPS)
                    sp.dma_start(M3s[:], M3.rearrange("e (c p) d -> p e c d", p=P)).then_inc(d_m3, 16)
                for b in range(BT):
                    for t in range(TS):
                        sp.dma_start(Vp[32 * t:32 * t + 32, b].rearrange("k h n -> k (h n)"),
                                     vtok[32 * b:32 * b + 32, t].rearrange("k h n -> k (h n)")).then_inc(d_vp, 16)
            sp.wait_ge(d_xs, 16 * 2 * TILES)
            sp.wait_ge(a_x4, STEPS)
            sp.wait_ge(p_s, BT * STEPS)
            slot_in, slot_out = (d_slot0, d_slot1), (d_ys0, d_ys1)

            def load_slot(j, u, used):
                if used is not None:
                    sp.wait_ge(p_xr, used)
                sp.dma_start(xrow[:, u, :], xs_tiles[:, bass.ds(j, 1), :].rearrange("p a d -> p (a d)")
                             ).then_inc(slot_in[u], 16)

            def store_slot(j, u):
                sp.wait_ge(a_y, j + 1)
                sp.dma_start(ys_tiles[:, bass.ds(j, 1), :].rearrange("p a d -> p (a d)"), yrow[:, u, :]
                             ).then_inc(slot_out[u], 16)

            load_slot(0, 0, None)
            load_slot(1, 1, None)
            load_slot(2, 0, 1)
            store_slot(0, 0)
            with sp.Fori(0, (SLOTS - 3) // 2) as t:
                load_slot(2 * t + 3, 1, 2 * t + 2)
                store_slot(2 * t + 1, 1)
                load_slot(2 * t + 4, 0, 2 * t + 3)
                store_slot(2 * t + 2, 0)
            store_slot(SLOTS - 2, 1)
            store_slot(SLOTS - 1, 0)
            for t in range(TILES):
                sp.wait_ge(v_hfin, t + 1)
                sp.dma_start(out_rows[:, t, :], H[:, t, :]).then_inc(d_out, 16)
            sp.wait_ge(d_out, 16 * TILES)

        @block.gpsimd
        def _(pool):
            gp = nc.gpsimd
            gp.memset(zrow[:], 0.0).then_inc(g_const, 1)
            for t, v in ((ident_b, 0.0), (ident, 0.0), (tri_b, 1.0), (batch_mean, 1.0 / L), (ones_e, 1.0),
                         (ones, 1.0), (ones_b, 1.0), (mhalf, -0.5), (reset_t, 1.0)):
                gp.memset(t[:], v).then_inc(g_const, 1)
            gp.memset(bE[:, DM:], 0.0).then_inc(g_const, 1)
            gp.iota(rank_w[:], pattern=[[-1, E]], base=E, channel_multiplier=0,
                    allow_small_or_imprecise_dtypes=True).then_inc(g_const, 1)
            gp.iota(slot_no[:], pattern=[[1, SLOTS]], base=0, channel_multiplier=0,
                    allow_small_or_imprecise_dtypes=True).then_inc(g_const, 1)
            pool.wait_ge(g_const, 13)
            for t in (ident_b, ident):
                gp.affine_select(out=t[:], in_=t[:], compare_op=ALU.not_equal, fill=1.0, base=0,
                                 pattern=[[-1, P]], channel_multiplier=1).then_inc(g_const, 1)
            gp.affine_select(out=tri_b[:], in_=tri_b[:], compare_op=ALU.is_ge, fill=0.0, base=0,
                             pattern=[[1, P]], channel_multiplier=-1).then_inc(g_const, 1)
            bm = batch_mean[:].rearrange("p (a b) -> p a b", b=L)
            gp.affine_select(out=bm, in_=bm, compare_op=ALU.is_ge, fill=0.0, base=0,
                             pattern=[[-L, BT], [0, L]], channel_multiplier=1).then_inc(g_const, 1)
            pool.wait_ge(g_const, 17)
            gp.affine_select(out=bm, in_=bm, compare_op=ALU.is_ge, fill=0.0, base=L - 1,
                             pattern=[[L, BT], [0, L]], channel_multiplier=-1).then_inc(g_const, 1)
            gp.memset(reset_t[:, :, 0:1], 0.0).then_inc(g_const, 1)
            gp.memset(ktok[:], 0.0).then_inc(g_const, 1)
            gp.memset(vtok[:], 1.0).then_inc(g_const, 1)

            asked = [0]

            def power(dst, src):
                asked[0] += 1
                pool.wait_ge(v_ask, asked[0])
                gp.tensor_tensor(dst, src, mhalf[:, 0:src.shape[-1]], ALU.pow).then_inc(g_pow, 1)

            power(sv[:, 3, :], sv[:, 2, :])
            for slot in range(SLOTS_OF_STEPS):
                if step_of(slot, D_LAG) is not None:
                    power(SD["rsb"][:], SD["bve"][:])
                if step_of(slot, B_LAG) is not None:
                    power(SB1["rstd"][:], SB1["ve"][:])
                    power(SB1["rsb"][:], SB1["bve"][:])
                if step_of(slot, D_LAG) is not None:
                    power(SD["rstd"][:], SD["ve"][:])

            for i in range(STEPS):
                power(SE["rstd"][:], SE["ve"][:])
                pool.wait_ge(a_x3, i + 1)
                gp.tensor_tensor(uI.rearrange("p (c b l) -> p c b l", c=CH, l=L),
                                 xT.rearrange("p c (b l) -> p c b l", l=L),
                                 Wi[:].rearrange("p c (a l) -> p c a l", a=1).to_broadcast([P, CH, SB, L]),
                                 ALU.mult).then_inc(g_ui, 1)
                pool.wait_ge(v_ur, i + 1)
                gp.tensor_tensor(uR.rearrange("p (c b l) -> p c b l", c=CH, l=L),
                                 uR.rearrange("p (c b l) -> p c b l", c=CH, l=L),
                                 CT[:, :, 0:L].rearrange("p c (a l) -> p c a l", a=1).to_broadcast([P, CH, SB, L]),
                                 ALU.mult).then_inc(g_uc, 1)
                power(SE["rstd"][:], SE["ve"][:])
            pool.wait_ge(d_zero, 16)
            pool.wait_ge(v_slots, 1)
            for k in range(2):
                for t in range(TILES):
                    gp.indirect_dma_start(xs, bass.IndirectOffsetOnAxis(ap=pos_i[:, k, t:t + 1], axis=0),
                                          X4[:, t, 0:DM], None).then_inc(d_xs, 16)
            pool.wait_ge(d_ys0, 16 * ((SLOTS + 1) // 2))
            pool.wait_ge(d_ys1, 16 * (SLOTS // 2))
            pool.wait_ge(p_dn, SLOTS)
            for t in range(TILES):
                for k in range(2):
                    gp.indirect_dma_start(back[k][:, t, :], None, ys,
                                          bass.IndirectOffsetOnAxis(ap=pos_i[:, k, t:t + 1], axis=0)
                                          ).then_inc(d_back[t], 16)

        @block.scalar
        def _(act):
            a = nc.scalar
            def pad(i):
                act.wait_ge((d_x0, d_x1)[i % 2], 32 * (i // 2 + 1))
                a.activation(xin[64:128, i % 2, :, T_IN - STRIDE:T_IN],
                             xin[64:128, i % 2, :, T_IN - STRIDE - 1:T_IN - STRIDE].to_broadcast([64, SB, STRIDE]),
                             ACT.Copy).then_inc(a_pad, 1)

            for n, v in enumerate((ph_re, ph_im, pi_re, pi_im, lc_re, lc_im)):
                act.dma_start(vec[:, n, :], v.rearrange("(c p) -> p c", p=P),
                              allow_slow_non_contiguous=True).then_inc(d_vec, 16)
            act.dma_start(b1c[:], b1.rearrange("(c p) -> p c", p=P), allow_slow_non_contiguous=True).then_inc(d_b, 16)
            act.dma_start(b2r[:], b2.partition_broadcast(P)).then_inc(d_b, 16)
            act.dma_start(bE[:, 0:DM], b_expert.partition_broadcast(P)).then_inc(d_b, 16)
            act.wait_ge(v_exp, 1)
            a.activation(sv[:, 4, :], sv[:, 5, :], ACT.Exp, scale=-1.0).then_inc(a_r, 1)
            pad(0)
            for c in range(CH):
                act.wait_ge(p_wt, c + 1)
                a.activation(WT[:, c].rearrange("p w d -> p (w d)"), bank[4 + c].bitcast(BF16), ACT.Copy
                             ).then_inc(a_wt, 1)
            act.wait_ge(d_b, 48)

            for slot in range(SLOTS_OF_STEPS):
                iA, iB, iC, iD = (step_of(slot, lag) for lag in (A_LAG, B_LAG, C_LAG, D_LAG))
                if iA is not None:
                    for c in range(CH):
                        act.wait_ge(p_l1, CH * iA + c + 1)
                        wait(act, p_l2, TS * iA)
                        a.activation(h1T[:, c, :], bank[c], ACT.Relu, bias=b1c[:, c:c + 1]).then_inc(a_h1, 1)
                    if iA + 1 < STEPS:
                        pad(iA + 1)
                if iD is not None:
                    act.wait_ge(p_ot, iD + 1)
                    wait(act, p_o, TS * iD)
                    a.activation(oqT[:].rearrange("p c n -> p (c n)"), bank[3].bitcast(BF16), ACT.Copy).then_inc(a_ot, 1)
                if iB is not None:
                    act.wait_ge(p_xt, iB + 1)
                    wait(act, p_qkv, TS * iB)
                    a.activation(xqT[:].rearrange("p c n -> p (c n)"), bank[4].bitcast(BF16), ACT.Copy).then_inc(a_xt, 1)
                    act.wait_ge(v_sc, iB + 1)
                    wait(act, v_qk, iB)
                    wait(act, d_vp, 16 * BT * TS * iB)
                    if iB == 0:
                        act.wait_ge(g_const, 21)
                    for t in range(TS):
                        act.wait_ge(p_qkv, TS * iB + t + 1)
                        qk = bank[(3, 5)[t % 2]]
                        a.activation(qtok[:, t, :], qk[:, 0:DM], ACT.Copy, scale=SB1["sw"][:, 0, t:t + 1])
                        for h in range(2):
                            a.activation(ktok[:, t, :, h, h, :],
                                         qk[:, DM:2 * DM].rearrange("p (n h d) -> p n h d", h=2, d=HD)[:, :, h, :],
                                         ACT.Copy, scale=SB1["sw"][:, 1, t:t + 1])
                        a.activation(vtok[:, t, :, 0:HD],
                                     bank[(2, 4)[t % 2]][:, 0:DM].rearrange("p (h d) -> p h d", d=HD),
                                     ACT.Copy, scale=SB1["sw"][:, 2, t:t + 1]).then_inc(a_qkv, 1)
                if iD is not None:
                    act.wait_ge(p_x2, iD + 1)
                    wait(act, v_xq, done(slot, B_LAG))
                    a.activation(xT.rearrange("p c n -> p (c n)"), banks(4), ACT.Copy).then_inc(a_x2, 1)
                if iC is not None:
                    for b in range(BT):
                        act.wait_ge(v_sub, BT * iC + b + 1)
                        e = Eb[:, b % 2]
                        a.activation(e, e, ACT.Exp).then_inc(a_exp, 1)
            act.wait_ge(v_xx, 1)
            a.activation(ra[:, 5], ra[:, 3], ACT.Exp).then_inc(a_gate, 1)
            for i in range(STEPS):
                act.wait_ge(p_x3, i + 1)
                wait(act, g_ui, i)
                a.activation(xT.rearrange("p c n -> p (c n)"), banks(0), ACT.Copy).then_inc(a_x3, 1)
                act.wait_ge(p_x4, i + 1)
                act.wait_ge(v_ur, i + 1)
                act.wait_ge(g_ui, i + 1)
                a.activation(xT.rearrange("p c n -> p (c n)"), banks(4), ACT.Copy).then_inc(a_x4, 1)
            act.wait_ge(v_ra, 1)
            a.activation(rs[:, 4, :], rs[:, 3, :], ACT.Exp).then_inc(a_lg, 1)

            def slot_rows(j, u):
                act.wait_ge(p_xr, j + 1)
                a.activation(xrT[:, u].rearrange("p c n -> p (c n)"), bank[u][:, 0:DM], ACT.Copy).then_inc(a_xr, 1)

            def slot_silu(j, u):
                act.wait_ge(p_up, j + 1)
                a.activation(sil[:, u, :], bank[2], ACT.Silu).then_inc(a_sil, 1)

            def slot_act(j, u):
                act.wait_ge(p_at, j + 1)
                a.activation(actT[:, u].rearrange("p c n -> p (c n)"), bank[4 + u], ACT.Copy).then_inc(a_at, 1)

            def slot_out(j, u, stored):
                act.wait_ge(p_dn, j + 1)
                if stored is not None:
                    act.wait_ge((d_ys0, d_ys1)[u], stored)
                a.activation(yrow[:, u, :], bank[6 + u][:, 0:DM], ACT.Copy).then_inc(a_y, 1)

            slot_rows(0, 0)
            slot_silu(0, 0)
            slot_rows(1, 1)
            slot_silu(1, 1)
            slot_act(0, 0)
            slot_out(0, 0, None)
            slot_rows(2, 0)
            slot_silu(2, 0)
            slot_act(1, 1)
            slot_out(1, 1, None)
            with act.Fori(1, (SLOTS - 1) // 2) as t:
                slot_rows(2 * t + 1, 1)
                slot_silu(2 * t + 1, 1)
                slot_act(2 * t, 0)
                slot_out(2 * t, 0, 16 * t)
                slot_rows(2 * t + 2, 0)
                slot_silu(2 * t + 2, 0)
                slot_act(2 * t + 1, 1)
                slot_out(2 * t + 1, 1, 16 * t)
            slot_act(SLOTS - 1, 0)
            slot_out(SLOTS - 1, 0, 16 * (SLOTS // 2))

        @block.vector
        def _(dve):
            v = nc.vector
            chain = [0]

            def ln(ins):
                chain[0] += 1
                ins.then_inc(v_chain, 1)

            def own():
                dve.wait_ge(v_chain, chain[0])

            asked = [0]

            def ask(ins):
                asked[0] += 1
                ins.then_inc(v_ask, 1)

            def answered():
                dve.wait_ge(g_pow, asked[0])

            dve.wait_ge(d_att, 64)
            v.tensor_reduce(wsum[:], wraw, AX, ALU.add, apply_absolute_value=True).then_inc(v_wabs, 1)
            dve.wait_ge(d_vec, 96)
            pr, pim = vec[:, 0, :], vec[:, 1, :]
            t = [sv[:, k, :] for k in range(20)]
            ln(v.tensor_tensor(t[5], pr, pr, ALU.mult))
            ln(v.tensor_tensor(t[6], pim, pim, ALU.mult))
            ln(v.tensor_scalar(t[7], pr, -1.0, None, ALU.mult))
            ln(v.tensor_scalar(t[8], pim, -1.0, None, ALU.mult))
            own()
            v.tensor_tensor(t[5], t[5], t[6], ALU.add).then_inc(v_exp, 1)
            ln(v.tensor_tensor(t[7], t[7], pr, ALU.max))
            ln(v.tensor_tensor(t[8], t[8], pim, ALU.max))
            own()
            ln(v.tensor_tensor(t[9], t[7], t[8], ALU.max))
            own()
            ln(v.tensor_scalar(t[10], t[9], 0.0, None, ALU.is_equal))
            own()
            ln(v.tensor_tensor(t[9], t[9], t[10], ALU.add))
            own()
            ln(v.reciprocal(t[11], t[9]))
            own()
            ln(v.tensor_tensor(t[12], pr, t[11], ALU.mult))
            ln(v.tensor_tensor(t[13], pim, t[11], ALU.mult))
            own()
            ln(v.tensor_tensor(t[12], t[12], t[10], ALU.add))
            own()
            ln(v.tensor_tensor(t[14], t[12], t[12], ALU.mult))
            ln(v.tensor_tensor(t[15], t[13], t[13], ALU.mult))
            own()
            ask(v.tensor_tensor(t[2], t[14], t[15], ALU.add))
            answered()
            ln(v.memset(CT[:, :, 0:1], 1.0))
            ln(v.memset(ST[:, :, 0:1], 0.0))
            one = lambda a_: a_.rearrange("p (c a) -> p c a", a=1)
            ln(v.tensor_tensor(CT[:, :, 1:2], one(t[12]), one(t[3]), ALU.mult))
            ln(v.tensor_tensor(ST[:, :, 1:2], one(t[13]), one(t[3]), ALU.mult))
            own()
            n = 1
            while n < L:
                cn = CT[:, :, n:n + 1].to_broadcast([P, CH, n])
                sn = ST[:, :, n:n + 1].to_broadcast([P, CH, n])
                q = [tmpT[:, k, :, 0:n] for k in range(4)]
                ln(v.tensor_tensor(q[0], CT[:, :, 1:n + 1], cn, ALU.mult))
                ln(v.tensor_tensor(q[1], ST[:, :, 1:n + 1], sn, ALU.mult))
                ln(v.tensor_tensor(q[2], CT[:, :, 1:n + 1], sn, ALU.mult))
                ln(v.tensor_tensor(q[3], ST[:, :, 1:n + 1], cn, ALU.mult))
                own()
                ln(v.tensor_tensor(CT[:, :, n + 1:2 * n + 1], q[0], q[1], ALU.subtract))
                ln(v.tensor_tensor(ST[:, :, n + 1:2 * n + 1], q[2], q[3], ALU.add))
                own()
                n *= 2
            q = [tmpT[:, k] for k in range(4)]
            bc = lambda k: one(vec[:, k, :]).to_broadcast([P, CH, L])
            ln(v.tensor_tensor(q[0], CT[:, :, 0:L], bc(2), ALU.mult))
            ln(v.tensor_tensor(q[1], ST[:, :, 0:L], bc(3), ALU.mult))
            ln(v.tensor_tensor(q[2], CT[:, :, 0:L], bc(3), ALU.mult))
            ln(v.tensor_tensor(q[3], ST[:, :, 0:L], bc(2), ALU.mult))
            own()
            ln(v.tensor_tensor(Wr[:], q[0], q[1], ALU.add))
            ln(v.tensor_tensor(Wi[:], q[2], q[3], ALU.subtract))
            own()
            c1, s1 = CT[:, :, 1:2], ST[:, :, 1:2]
            ln(v.tensor_tensor(one(t[14]), one(vec[:, 4, :]), c1, ALU.mult))
            ln(v.tensor_tensor(one(t[15]), one(vec[:, 5, :]), s1, ALU.mult))
            ln(v.tensor_tensor(one(t[16]), one(vec[:, 4, :]), s1, ALU.mult))
            ln(v.tensor_tensor(one(t[17]), one(vec[:, 5, :]), c1, ALU.mult))
            own()
            ln(v.tensor_tensor(t[14], t[14], t[15], ALU.subtract))
            ln(v.tensor_tensor(t[16], t[16], t[17], ALU.add))
            own()
            dve.wait_ge(a_r, 1)
            ln(v.tensor_tensor(t[18], t[14], t[4], ALU.mult))
            ln(v.tensor_tensor(t[19], t[16], t[4], ALU.mult))
            dve.wait_ge(p_wsum, 1)
            ln(v.tensor_scalar(wm[:], bank[6][:, 0:4], 1.0 / (DM * DM), 1e-5, ALU.mult, ALU.max))
            own()
            ln(v.reciprocal(wmi[:], wm[:]))
            own()
            for w in range(4):
                ln(v.tensor_scalar(wraw[:, w, :], wraw[:, w, :], wmi[:, w:w + 1], MAGIC, ALU.mult, ALU.add))
            own()
            allw = wraw.rearrange("p w n -> p (w n)")
            ln(v.tensor_scalar(allw, allw, MAGIC, 1.0, ALU.subtract, ALU.min))
            own()
            v.tensor_scalar(wter.rearrange("p w c n -> p (w c n)"), allw, -1.0, None, ALU.max).then_inc(v_wt, 1)

            def norm_stats(S, rows):
                for t_ in range(TS):
                    ln(v.bn_stats(S["st"][:, t_, :], rows(t_)))
                own()
                for t_ in range(TS):
                    ln(v.bn_aggr(S["mv"][:, t_, :], S["st"][:, t_, :]))
                own()

            def ask_rstd(S):
                ask(v.tensor_scalar(S["ve"][:], S["mv"][:, :, 1], EPS, None, ALU.add))

            def scales(S, rows, weights):
                ln(v.tensor_reduce(S["am"][:], rows, AX, ALU.max, apply_absolute_value=True))
                answered()
                own()
                ln(v.tensor_tensor(S["am"][:], S["am"][:], S["rsb"][:], ALU.mult))
                own()
                ln(v.tensor_scalar(S["sa"][:], S["am"][:], 1e-5, 1.0 / 127.0, ALU.max, ALU.mult))
                own()
                ln(v.reciprocal(S["s"][:], S["sa"][:]))
                for n_, (w_, extra) in enumerate(weights):
                    ln(v.tensor_scalar(S["sw"][:, n_, :], S["sa"][:], wm[:, w_:w_ + 1], extra, ALU.mult, ALU.mult))
                own()
                ln(v.tensor_tensor(S["s"][:], S["s"][:], S["rsb"][:], ALU.mult))
                own()

            for slot in range(SLOTS_OF_STEPS):
                iA, iB, iC, iD = (step_of(slot, lag) for lag in (A_LAG, B_LAG, C_LAG, D_LAG))
                if iD is not None:
                    norm_stats(SD, lambda t_: O[:, t_, :])
                    mean, var = SD["mv"][:, :, 0], SD["mv"][:, :, 1]
                    ln(v.tensor_copy(SD["bs"][:, 0, :], mean))
                    ln(v.tensor_tensor(SD["st"][:, :, 0], mean, mean, ALU.mult))
                    own()
                    v.tensor_tensor(SD["bs"][:, 1, :], SD["st"][:, :, 0], var, ALU.add).then_inc(v_ob, 1)
                if iB is not None:
                    i = iB
                    dve.wait_ge(v_h, TS * (i + 1))
                    wait(dve, p_e, TS * done(slot - 1, D_LAG))
                    norm_stats(SB1, lambda t_: H[:, TS * i + t_, :])
                if iD is not None:
                    dve.wait_ge(p_ob, iD + 1)
                    ln(v.tensor_copy(SD["bv"][:].rearrange("p a t -> p (a t)"), bank[3][:, 0:2 * TS]))
                    own()
                    mu, e2 = SD["bv"][:, 0, :], SD["bv"][:, 1, :]
                    ln(v.tensor_tensor(SD["am"][:], mu, mu, ALU.mult))
                    own()
                    ln(v.tensor_tensor(e2, e2, SD["am"][:], ALU.subtract))
                    own()
                    ask(v.tensor_scalar(SD["bve"][:], e2, 0.0, EPS, ALU.max, ALU.add))
                    for t_ in range(TS):
                        ln(v.tensor_scalar(O[:, t_, :], O[:, t_, :], mu[:, t_:t_ + 1], None, ALU.subtract))
                    own()
                    scales(SD, O[:], [(3, 1.0)])
                    for t_ in range(TS):
                        ln(v.tensor_scalar(O[:, t_, :], O[:, t_, :], SD["s"][:, t_:t_ + 1], MAGIC, ALU.mult, ALU.add))
                    own()
                    wait(dve, p_ot, iD)
                    v.tensor_scalar(oq[:], O[:], MAGIC, 127.0, ALU.subtract, ALU.min).then_inc(v_oq, 1)
                if iB is not None:
                    ask_rstd(SB1)
                    answered()
                    mean, var, r_ = SB1["mv"][:, :, 0], SB1["mv"][:, :, 1], SB1["rstd"]
                    ln(v.tensor_tensor(SB1["bs"][:, 1, :], var, r_[:], ALU.mult))
                    own()
                    v.tensor_tensor(SB1["bs"][:, 0, :], SB1["bs"][:, 1, :], r_[:], ALU.mult).then_inc(v_y, 1)
                    for t_ in range(TS):
                        ln(v.tensor_scalar(x1[:, t_, :], H[:, TS * iB + t_, :], mean[:, t_:t_ + 1], r_[:, t_:t_ + 1],
                                           ALU.subtract, ALU.mult))
                    dve.wait_ge(p_bv, iB + 1)
                    ask(v.tensor_scalar(SB1["bve"][:], bank[2][:, 0:TS], EPS, None, ALU.add))
                    own()
                    wait(dve, a_qkv, TS * iB)
                    scales(SB1, x1[:], [(0, HD ** -0.5), (1, 1.0), (2, 1.0)])
                    for t_ in range(TS):
                        ln(v.tensor_scalar(x1[:, t_, :], x1[:, t_, :], SB1["s"][:, t_:t_ + 1], MAGIC, ALU.mult, ALU.add))
                    own()
                    v.engine_nop().then_inc(v_sc, 1)
                    wait(dve, p_xt, iB)
                    v.tensor_scalar(xq[:], x1[:], MAGIC, 127.0, ALU.subtract, ALU.min).then_inc(v_xq, 1)
                if iA is not None:
                    dve.wait_ge(d_b, 48)
                    for t_ in range(TS):
                        dve.wait_ge(p_l2, TS * iA + 2 * (t_ // 2) + 2)
                        v.tensor_tensor(H[:, TS * iA + t_, :], bank[6 + t_ // 2][:, DM * (t_ % 2):DM * (t_ % 2 + 1)],
                                        b2r[:], ALU.add).then_inc(v_h, 1)
                if iD is not None:
                    for t_ in range(TS):
                        dve.wait_ge(p_o, TS * iD + 2 * (t_ // 2) + 2)
                        hrow = H[:, TS * iD + t_, :]
                        ln(v.scalar_tensor_tensor(hrow, bank[6 + t_ // 2][:, DM * (t_ % 2):DM * (t_ % 2 + 1)],
                                                  SD["sw"][:, 0, t_:t_ + 1], hrow, ALU.mult, ALU.add))
                    own()
                    v.engine_nop().then_inc(v_hd, 1)
                    norm_stats(SD, lambda t_: H[:, TS * iD + t_, :])
                    ask_rstd(SD)
                    answered()
                    for t_ in range(TS):
                        r = v.tensor_scalar(O[:, t_, :], H[:, TS * iD + t_, :], SD["mv"][:, t_, 0:1],
                                            SD["rstd"][:, t_:t_ + 1], ALU.subtract, ALU.mult)
                    r.then_inc(v_x2, 1)
                if iC is not None:
                    def minus_max(b):
                        m = mx[:, b % 2, :]
                        s_ = bank[b % 2].rearrange("p (h k) -> p h k", k=32)
                        dve.wait_ge(p_s, BT * iC + b + 1)
                        ln(v.tensor_reduce(m, s_, AX, ALU.max))
                        own()
                        wait(dve, v_pt, BT * iC + b - 1)
                        v.tensor_tensor(Eb[:, b % 2], s_, m.rearrange("p (h a) -> p h a", a=1).to_broadcast([P, NH, 32]),
                                        ALU.subtract).then_inc(v_sub, 1)

                    def turn(b):
                        dve.wait_ge(a_exp, BT * iC + b + 1)
                        wait(dve, p_pv, BT * iC + b - 1)
                        v.transpose(PT[:, b % 2].rearrange("p h k -> p (h k)"), Eb[:, b % 2].rearrange("p h k -> p (h k)")
                                    ).then_inc(v_pt, 1)

                    minus_max(0)
                    minus_max(1)
                    turn(0)
                    minus_max(2)
                    turn(1)
                    minus_max(3)
                if iD is not None:
                    for t_ in range(TS):
                        dve.wait_ge(p_e, TS * iD + t_ + 1)
                        v.tensor_tensor(EO[:, TS * iD + t_, :], bank[6 + t_ % 2][:, 0:DE], bE[:], ALU.add
                                        ).then_inc(v_eo, 1)
                if iC is not None:
                    turn(2)
                    turn(3)
                if iB is not None:
                    dve.wait_ge(a_qkv, TS * (iB + 1))
                    wait(dve, p_s, BT * iB)
                    if iB == 0:
                        dve.wait_ge(p_wt, CH)
                    v.transpose(QT[:].rearrange("p t n k -> p (t n k)"), qtok[:].rearrange("p t d -> p (t d)"))
                    v.transpose(KT[:].rearrange("p t n k -> p (t n k)"),
                                ktok[:].rearrange("p t n a b d -> p (t n a b d)")).then_inc(v_qk, 1)
                if iC is not None:
                    dve.wait_ge(p_pv, BT * (iC + 1))
                    wait(dve, p_x2, done(slot, D_LAG))
                    for t_ in range(TS):
                        o = bank[2 + t_][:, 0:NH * VW].rearrange("p (h n) -> p h n", n=VW)
                        ln(v.reciprocal(rec[:, t_, :].rearrange("p (h a) -> p h a", a=1), o[:, :, HD:VW]))
                    own()
                    for t_ in range(TS):
                        o = bank[2 + t_][:, 0:NH * VW].rearrange("p (h n) -> p h n", n=VW)
                        ln(v.tensor_tensor(O[:, t_, :].rearrange("p (h d) -> p h d", d=HD), o[:, :, 0:HD],
                                           rec[:, t_, :].rearrange("p (h a) -> p h a", a=1).to_broadcast([P, NH, HD]),
                                           ALU.mult))
                    own()
                    v.engine_nop().then_inc(v_o, 1)

            te = lambda a_: a_.rearrange("p (t a) -> p t a", a=1).to_broadcast([P, TILES, E])
            rw = rank_w[:].rearrange("p (a e) -> p a e", a=1).to_broadcast([P, TILES, E])

            def best(logits, m, tie, oh, s1_, s2_):
                ln(v.tensor_reduce(m, logits, AX, ALU.max))
                own()
                ln(v.tensor_tensor(s1_, logits, te(m), ALU.is_equal))
                own()
                ln(v.tensor_tensor(s2_, s1_, rw, ALU.mult))
                own()
                ln(v.tensor_reduce(tie, s2_, AX, ALU.max))
                own()
                ln(v.tensor_tensor(oh, s2_, te(tie), ALU.is_equal))
                own()

            def queue_places(signal, ready, total):
                dve.wait_ge(ready, 1)
                ct = cum[:, 0]
                ln(v.tensor_copy(ct, bank[7][:, 0:TILES * E].rearrange("p (t e) -> p e t", e=E)))
                own()
                ln(v.tensor_tensor_scan(cum[:, 1].rearrange("p e t -> p (e t)"), reset_t[:].rearrange("p e t -> p (e t)"),
                                        ct.rearrange("p e t -> p (e t)"), 0.0, ALU.mult, ALU.add))
                own()
                ln(v.tensor_tensor(ct, cum[:, 1], ct, ALU.subtract))
                own()
                ln(v.tensor_tensor(ra[:, 7], bank[6][:, 0:TILES * E].rearrange("p (t e) -> p t e", e=E),
                                   ct.rearrange("p e t -> p t e"), ALU.add))
                own()

            dve.wait_ge(v_eo, TILES)
            dve.wait_ge(v_pt, BT * STEPS)
            dve.wait_ge(g_const, 21)
            ln(v.tensor_copy(lg[:], EO[:, :, DM:DE]))
            own()
            best(lg[:], rs[:, 0, :], rs[:, 1, :], ra[:, 0], ra[:, 1], ra[:, 2])
            v.tensor_copy(mask_b[:], ra[:, 0]).then_inc(v_mask, 1)
            ln(v.tensor_tensor(ra[:, 3], lg[:], te(rs[:, 0, :]), ALU.subtract))
            own()
            v.engine_nop().then_inc(v_xx, 1)
            queue_places(None, p_cum, None)
            ln(v.tensor_scalar(ra[:, 4], ra[:, 7], float(CAPACITY), None, ALU.is_le))
            own()
            ln(v.tensor_tensor(ra[:, 4], ra[:, 4], ra[:, 0], ALU.mult))
            own()
            ln(v.tensor_reduce(rs[:, 2, :], ra[:, 4], AX, ALU.add))
            dve.wait_ge(a_gate, 1)
            ln(v.tensor_reduce(rs[:, 5, :], ra[:, 5], AX, ALU.add))
            own()
            ln(v.reciprocal(rs[:, 6, :], rs[:, 5, :]))
            own()
            ln(v.tensor_tensor(rs[:, 7, :], rs[:, 6, :], rs[:, 2, :], ALU.mult))
            ln(v.memset(RT, 0.0))
            own()
            rt = RT.rearrange("p (c b l) -> p c b l", c=CH, l=L)
            for c in range(CH):
                ln(v.tensor_scalar(rt[:, c, :, 1:L], rt[:, c, :, 1:L], t[4][:, c:c + 1], None, ALU.add))
            own()
            for i in range(STEPS):
                for t_ in range(TS):
                    n = TS * i + t_
                    ln(v.scalar_tensor_tensor(H[:, n, :], EO[:, n, 0:DM], rs[:, 7, n:n + 1], H[:, n, :], ALU.mult, ALU.add))
                own()
                norm_stats(SE, lambda t_: H[:, TS * i + t_, :])
                ask_rstd(SE)
                answered()
                wait(dve, p_x3, i)
                for t_ in range(TS):
                    r = v.tensor_scalar(O[:, t_, :], H[:, TS * i + t_, :], SE["mv"][:, t_, 0:1],
                                        SE["rstd"][:, t_:t_ + 1], ALU.subtract, ALU.mult)
                r.then_inc(v_xc, 1)
                dve.wait_ge(a_x3, i + 1)
                wait(dve, p_y3, i)
                cbl = lambda a_: a_.rearrange("p (c b l) -> p c b l", c=CH, l=L)
                tab = lambda a_: a_.rearrange("p c (a l) -> p c a l", a=1).to_broadcast([P, CH, SB, L])
                ln(v.tensor_tensor(cbl(uR), xT.rearrange("p c (b l) -> p c b l", l=L), tab(Wr[:]), ALU.mult))
                own()
                for c in range(CH):
                    ln(v.tensor_scalar(cbl(uR)[:, c, :, 0], cbl(uR)[:, c, :, 0], t[18][:, c:c + 1], None, ALU.add))
                own()
                v.tensor_tensor_scan(uR, RT, uR, 0.0, ALU.mult, ALU.add).then_inc(v_ur, 1)
                dve.wait_ge(g_ui, i + 1)
                for c in range(CH):
                    ln(v.tensor_scalar(cbl(uI)[:, c, :, 0], cbl(uI)[:, c, :, 0], t[19][:, c:c + 1], None, ALU.add))
                own()
                ln(v.tensor_tensor_scan(uI, RT, uI, 0.0, ALU.mult, ALU.add))
                own()
                ln(v.tensor_tensor(cbl(uI), cbl(uI), tab(ST[:, :, 0:L]), ALU.mult))
                own()
                dve.wait_ge(g_uc, i + 1)
                v.tensor_tensor(uR, uR, uI, ALU.subtract).then_inc(v_yc, 1)
                dve.wait_ge(p_y3, i + 1)
                hh = H[:, TS * i:TS * (i + 1), :].rearrange("p t d -> p (t d)")
                ln(v.tensor_tensor(hh, hh, banks(2), ALU.add))
                own()
                norm_stats(SE, lambda t_: H[:, TS * i + t_, :])
                ask_rstd(SE)
                answered()
                for t_ in range(TS):
                    n = TS * i + t_
                    r = v.tensor_scalar(X4[:, n, 0:DM], H[:, n, :], SE["mv"][:, t_, 0:1],
                                        SE["rstd"][:, t_:t_ + 1], ALU.subtract, ALU.mult)
                r.then_inc(v_x4, 1)
                dve.wait_ge(p_lg, i + 1)
                ln(v.tensor_copy(lg[:, TS * i:TS * (i + 1), :], bank[6][:, 0:TS * E].rearrange("p (t e) -> p t e", e=E)))

            own()
            best(lg[:], rs[:, 0, :], rs[:, 1, :], ra[:, 0], ra[:, 1], ra[:, 2])
            ln(v.scalar_tensor_tensor(ra[:, 3], ra[:, 0], -1e30, lg[:], ALU.mult, ALU.add))
            own()
            best(ra[:, 3], rs[:, 2, :], rs[:, 1, :], ra[:, 4], ra[:, 1], ra[:, 2])
            v.tensor_tensor(mask_b[:], ra[:, 0], ra[:, 4], ALU.add).then_inc(v_mask2, 1)
            v.tensor_tensor(rs[:, 3, :], rs[:, 2, :], rs[:, 0, :], ALU.subtract).then_inc(v_ra, 1)
            queue_places(None, p_cum2, None)
            cnt = cum[:, 1, :, TILES - 1]
            ln(v.tensor_scalar(tb[:, 0, :], cnt, float(P - 1), 1.0 / P, ALU.add, ALU.mult))
            own()
            ln(v.tensor_scalar(tb[:, 0, :], tb[:, 0, :], 0.5 - 1.0 / (2 * P), MAGIC, ALU.subtract, ALU.add))
            own()
            ln(v.tensor_scalar(tb[:, 0, :], tb[:, 0, :], MAGIC, None, ALU.subtract))
            own()
            ln(v.tensor_tensor_scan(tb[:, 1, :], ones_e[:], tb[:, 0, :], 0.0, ALU.mult, ALU.add))
            own()
            ln(v.tensor_tensor(tb[:, 2, :], tb[:, 1, :], tb[:, 0, :], ALU.subtract))
            own()
            ln(v.tensor_scalar(tb[:, 3, :], tb[:, 2, :], float(P), -1.0, ALU.mult, ALU.add))
            own()
            eb = lambda a_, n_: a_.rearrange("p (a e) -> p a e", a=1).to_broadcast([P, n_, E])
            ln(v.tensor_tensor(ra[:, 7], ra[:, 7], eb(tb[:, 3, :], TILES), ALU.add))
            own()
            for k, oh in enumerate((ra[:, 0], ra[:, 4])):
                ln(v.tensor_tensor(ra[:, 5 + k], ra[:, 7], oh, ALU.mult))
            own()
            for k in range(2):
                ln(v.tensor_reduce(rs[:, 5 + k, :], ra[:, 5 + k], AX, ALU.add))
            own()
            v.tensor_copy(pos_i[:], rs[:, 5:7, :]).then_inc(v_slots, 1)
            ln(v.tensor_tensor(cmp, eb(tb[:, 1, :], SLOTS),
                               slot_no[:].rearrange("p (s a) -> p s a", a=1).to_broadcast([P, SLOTS, E]), ALU.is_le))
            own()
            ln(v.tensor_reduce(exf[:], cmp, AX, ALU.add))
            own()
            v.tensor_scalar(exi[:], exf[:], float(E - 1), None, ALU.min).then_inc(v_cum, 1)
            dve.wait_ge(a_lg, 1)
            ln(v.tensor_scalar(rs[:, 7, :], rs[:, 4, :], 1.0, None, ALU.add))
            own()
            ln(v.reciprocal(rs[:, 8, :], rs[:, 7, :]))
            own()
            ln(v.tensor_tensor(rs[:, 9, :], rs[:, 8, :], rs[:, 4, :], ALU.mult))
            own()

            def slot_gate(j, u):
                dve.wait_ge(a_sil, j + 1)
                v.tensor_tensor(sil[:, u, :], sil[:, u, :], bank[3], ALU.mult).then_inc(v_act, 1)

            slot_gate(0, 0)
            with dve.Fori(0, (SLOTS - 1) // 2) as t_:
                slot_gate(2 * t_ + 1, 1)
                slot_gate(2 * t_ + 2, 0)
            for n in range(TILES):
                dve.wait_ge(d_back[n], 32)
                ln(v.scalar_tensor_tensor(H[:, n, :], back[0][:, n, :], rs[:, 8, n:n + 1], H[:, n, :], ALU.mult, ALU.add))
                own()
                v.scalar_tensor_tensor(H[:, n, :], back[1][:, n, :], rs[:, 9, n:n + 1], H[:, n, :], ALU.mult, ALU.add
                                       ).then_inc(v_hfin, 1)

        @block.tensor
        def _(pe):
            mm = nc.tensor.matmul
            tr = nc.tensor.transpose
            pe.wait_ge(g_const, 21)
            pe.wait_ge(v_wabs, 1)
            mm(bank[6][:, 0:4], ones[:], wsum[:], start=True, stop=True).then_inc(p_wsum, 1)

            def layer1(i, c):
                if c == 0:
                    if i == 0:
                        pe.wait_ge(d_w1, 32)
                    pe.wait_ge(a_pad, i + 1)
                    pe.wait_ge((d_x0, d_x1)[i % 2], 32 * (i // 2 + 1))
                wait(pe, a_h1, CH * (i - 1) + c + 1)
                wait(pe, v_sub, BT * done(i - 1, C_LAG))
                for r in range(STRIDE):
                    last = mm(bank[c], W1s[:, r, P * c:P * (c + 1)],
                              xin[:, i % 2].rearrange("p b (l s) -> p b l s", s=STRIDE)[:, :, :, r],
                              start=(r == 0), stop=(r == STRIDE - 1))
                last.then_inc(p_l1, 1)

            def layer2(i, slot):
                pe.wait_ge(a_h1, CH * (i + 1))
                if i == 0:
                    pe.wait_ge(d_w2, 16)
                    pe.wait_ge(v_wt, 1)
                wait(pe, v_h, TS * i)
                wait(pe, v_eo, TS * done(slot - 1, D_LAG))
                for t in range(TS):
                    for c in range(CH):
                        last = mm(bank[6 + t // 2][:, DM * (t % 2):DM * (t % 2 + 1)], h1T[:, c, P * t:P * (t + 1)],
                                  W2s[:, c, :], start=(c == 0), stop=(c == CH - 1))
                    last.then_inc(p_l2, 1)

            for slot in range(SLOTS_OF_STEPS):
                iA, iB, iC, iD = (step_of(slot, lag) for lag in (A_LAG, B_LAG, C_LAG, D_LAG))
                if iA is not None:
                    layer1(iA, 0)
                if iD is not None:
                    pe.wait_ge(v_ob, iD + 1)
                    pe.wait_ge(v_o, done(slot - 1, C_LAG))
                    mm(bank[3][:, 0:2 * TS], batch_mean[:], SD["bs"][:].rearrange("p a t -> p (a t)"),
                       start=True, stop=True).then_inc(p_ob, 1)
                if iB is not None:
                    pe.wait_ge(v_y, iB + 1)
                    wait(pe, v_o, done(slot - 1, C_LAG))
                    mm(bank[2][:, 0:TS], batch_mean[:], SB1["bs"][:, 0, :], start=True, stop=True).then_inc(p_bv, 1)
                if iA is not None:
                    layer1(iA, 1)
                if iD is not None:
                    pe.wait_ge(v_oq, iD + 1)
                    for c in range(CH):
                        for t in range(TS):
                            last = tr(bank[3].bitcast(BF16)[:, SN * c + P * t:SN * c + P * (t + 1)],
                                      oq[:, t, P * c:P * (c + 1)], ident_b[:])
                    last.then_inc(p_ot, 1)
                if iB is not None:
                    pe.wait_ge(v_xq, iB + 1)
                    for c in range(CH):
                        for t in range(TS):
                            last = tr(bank[4].bitcast(BF16)[:, SN * c + P * t:SN * c + P * (t + 1)],
                                      xq[:, t, P * c:P * (c + 1)], ident_b[:])
                    last.then_inc(p_xt, 1)
                if iA == 0:
                    pe.wait_ge(v_wt, 1)
                    for c in range(CH):
                        for w in range(4):
                            for o in range(CH):
                                last = tr(bank[4 + c].bitcast(BF16)[:, DM * w + P * o:DM * w + P * (o + 1)],
                                          wter[:, w, o, P * c:P * (c + 1)], ident_b[:])
                        last.then_inc(p_wt, 1)
                if iA is not None:
                    layer2(iA, slot)
                if iD is not None:
                    pe.wait_ge(a_ot, iD + 1)
                    wait(pe, v_h, TS * done(slot, A_LAG))
                    wait(pe, v_eo, TS * done(slot - 1, D_LAG))
                    for t in range(TS):
                        for c in range(CH):
                            last = mm(bank[6 + t // 2][:, DM * (t % 2):DM * (t % 2 + 1)], oqT[:, c, P * t:P * (t + 1)],
                                      WT[:, c, 3, :], start=(c == 0), stop=(c == CH - 1))
                        last.then_inc(p_o, 1)
                if iB is not None:
                    if iB == 0:
                        pe.wait_ge(a_wt, CH)
                    pe.wait_ge(a_xt, iB + 1)
                    wait(pe, a_ot, done(slot, D_LAG))
                    pe.wait_ge(v_xq, iB + 1)
                    for t in range(TS):
                        wait(pe, a_qkv, TS * iB + t - 1)
                        for c in range(CH):
                            mm(bank[(3, 5)[t % 2]], xqT[:, c, P * t:P * (t + 1)],
                               WT[:, c, 0:2, :].rearrange("p w d -> p (w d)"), start=(c == 0), stop=(c == CH - 1))
                        for c in range(CH):
                            last = mm(bank[(2, 4)[t % 2]][:, 0:DM], xqT[:, c, P * t:P * (t + 1)],
                                      WT[:, c, 2, :], start=(c == 0), stop=(c == CH - 1))
                        last.then_inc(p_qkv, 1)
                if iD is not None:
                    pe.wait_ge(v_x2, iD + 1)
                    wait(pe, a_qkv, TS * done(slot, B_LAG))
                    for c in range(CH):
                        for t in range(TS):
                            last = tr(bank[4 + c][:, P * t:P * (t + 1)], O[:, t, P * c:P * (c + 1)], ident[:])
                    last.then_inc(p_x2, 1)
                if iC is not None:
                    pe.wait_ge(v_qk, iC + 1)
                    pe.wait_ge(a_h1, CH * done(slot, A_LAG))
                    for b in range(BT):
                        wait(pe, v_sub, BT * iC + b - 1)
                        for n in range(DBLK):
                            for t in range(TS):
                                last = mm(bank[b % 2][32 * t:32 * t + 32, 64 * n:64 * n + 64],
                                          QT[32 * b:32 * b + 32, t, n, :], KT[32 * b:32 * b + 32, t, n, :],
                                          start=True, stop=True)
                        last.then_inc(p_s, 1)
                if iD is not None:
                    pe.wait_ge(a_x2, iD + 1)
                    if iD == 0:
                        pe.wait_ge(d_we, 48)
                    pe.wait_ge(v_hd, iD + 1)
                    for t in range(TS):
                        wait(pe, v_eo, TS * iD + t - 1)
                        for c in range(CH):
                            last = mm(bank[6 + t % 2][:, 0:DE], xT[:, c, P * t:P * (t + 1)], WE[:, c, :],
                                      start=(c == 0), stop=(c == CH - 1))
                        last.then_inc(p_e, 1)
                if iC is not None:
                    pe.wait_ge(d_vp, 16 * BT * TS * (iC + 1))
                    wait(pe, a_x2, done(slot, D_LAG))
                    for b in range(BT):
                        pe.wait_ge(v_pt, BT * iC + b + 1)
                        for h in range(NH):
                            for t in range(TS):
                                last = mm(bank[2 + t][32 * b:32 * b + 32, VW * h:VW * (h + 1)],
                                          PT[32 * t:32 * t + 32, b % 2, h, :], Vp[32 * t:32 * t + 32, b, h, :],
                                          start=True, stop=True)
                        last.then_inc(p_pv, 1)

            def places(ready, signal):
                pe.wait_ge(ready, 1)
                mk = mask_b[:].rearrange("p t e -> p (t e)")
                mm(bank[6][:, 0:TILES * E], tri_b[:], mk, start=True, stop=True)
                mm(bank[7][:, 0:TILES * E], ones_b[:], mk, start=True, stop=True).then_inc(signal, 1)

            pe.wait_ge(v_eo, TILES)
            places(v_mask, p_cum)
            for i in range(STEPS):
                pe.wait_ge(v_xc, i + 1)
                for c in range(CH):
                    for t in range(TS):
                        last = tr(bank[c][:, P * t:P * (t + 1)], O[:, t, P * c:P * (c + 1)], ident[:])
                last.then_inc(p_x3, 1)
                pe.wait_ge(v_yc, i + 1)
                for t in range(TS):
                    for c in range(CH):
                        last = tr(banks(2)[:, DM * t + P * c:DM * t + P * (c + 1)],
                                  uR[:, SN * c + P * t:SN * c + P * (t + 1)], ident[:])
                last.then_inc(p_y3, 1)
                pe.wait_ge(v_x4, i + 1)
                for c in range(CH):
                    for t in range(TS):
                        last = tr(bank[4 + c][:, P * t:P * (t + 1)], X4[:, TS * i + t, P * c:P * (c + 1)], ident[:])
                last.then_inc(p_x4, 1)
                pe.wait_ge(a_x4, i + 1)
                for t in range(TS):
                    for c in range(CH):
                        last = mm(bank[6][:, E * t:E * (t + 1)], xT[:, c, P * t:P * (t + 1)], Wgs[:, c, :],
                                  start=(c == 0), stop=(c == CH - 1))
                last.then_inc(p_lg, 1)
            places(v_mask2, p_cum2)
            pe.wait_ge(v_cum, 1)
            pe.wait_ge(d_moe, 32)
            pe.wait_ge(d_m3, 16)
            slot_in = (d_slot0, d_slot1)

            def slot_up(j, u, loads):
                pe.wait_ge(slot_in[u], loads)
                for c in range(CH):
                    last = tr(bank[u][:, P * c:P * (c + 1)], xrow[:, u, P * c:P * (c + 1)], ident[:])
                last.then_inc(p_xr, 1)
                e = pe.value_load(exi[0:1, bass.ds(j, 1)], min_val=0, max_val=E - 1)
                pe.wait_ge(a_xr, j + 1)
                for w, z in ((M1s, bank[2]), (M2s, bank[3])):
                    if w is M1s and not (isinstance(j, int) and j == 0):
                        pe.wait_ge(a_sil, j)
                    if w is M2s and not (isinstance(j, int) and j == 0):
                        pe.wait_ge(v_act, j)
                    for c in range(CH):
                        last = mm(z, xrT[:, u, c, :], w[:, bass.ds(e, 1), c, :].rearrange("p a h -> p (a h)"),
                                  start=(c == 0), stop=(c == CH - 1))
                last.then_inc(p_up, 1)
                return e

            def slot_down(j, u):
                pe.wait_ge(v_act, j + 1)
                if not (isinstance(j, int) and j < 2):
                    pe.wait_ge(a_y, j - 1)
                for c in range(HC):
                    last = tr(bank[4 + u][:, P * c:P * (c + 1)], sil[:, u, P * c:P * (c + 1)], ident[:])
                last.then_inc(p_at, 1)
                e = pe.value_load(exi[0:1, bass.ds(j, 1)], min_val=0, max_val=E - 1)
                pe.wait_ge(a_at, j + 1)
                for c in range(HC):
                    last = mm(bank[6 + u][:, 0:DM], actT[:, u, c, :], M3s[:, bass.ds(e, 1), c, :].rearrange("p a d -> p (a d)"),
                              start=(c == 0), stop=(c == HC - 1))
                last.then_inc(p_dn, 1)

            slot_up(0, 0, 16)
            slot_up(1, 1, 16)
            slot_down(0, 0)
            slot_up(2, 0, 32)
            slot_down(1, 1)
            with pe.Fori(1, (SLOTS - 1) // 2) as t:
                slot_up(2 * t + 1, 1, 16 * t + 16)
                slot_down(2 * t, 0)
                slot_up(2 * t + 2, 0, 16 * t + 32)
                slot_down(2 * t + 1, 1)
            slot_down(SLOTS - 1, 0)


_INS = ['x', 'L0_tok_W1', 'L0_tok_b1', 'L0_tok_W2', 'L0_tok_b2', 'L0_attn_w_q', 'L0_attn_w_k', 'L0_attn_w_v',
        'L0_attn_w_o', 'L0_ffn_w_gate', 'L0_ffn_w_expert', 'L0_ffn_b_expert', 'L1_attn_phazor_real',
        'L1_attn_phazor_imag', 'L1_attn_phazor_init_real', 'L1_attn_phazor_init_imag', 'L1_attn_last_conv_real',
        'L1_attn_last_conv_imag', 'L1_ffn_Wg', 'L1_ffn_W1', 'L1_ffn_W2', 'L1_ffn_W3']
_OUTS = [((64, 32, 256), 'float32')]


def kernel(**inputs):
    import numpy as _np
    import concourse.bacc as _bacc
    from concourse import mybir as _mybir
    from concourse.bass_utils import run_bass_kernel_spmd as _run

    nc = _bacc.Bacc("TRN2", target_bir_lowering=False, num_devices=1)
    arrays, args = {}, []
    for name in _INS:
        a = _np.ascontiguousarray(inputs[name])
        arrays[f"in_{name}_dram"] = a
        args.append(nc.dram_tensor(f"in_{name}_dram", a.shape, _mybir.dt.from_np(a.dtype), kind="ExternalInput").ap())
    for i, (shape, dtype) in enumerate(_OUTS):
        dt = _mybir.dt.from_np(_np.dtype(dtype))
        args.append(nc.dram_tensor(f"out_{i}_dram", shape, dt, kind="ExternalOutput").ap())
    audio_tower_kernel(nc, *args)
    r = _run(nc, [arrays], core_ids=[0])
    got = tuple(r.results[0][f"out_{i}_dram"] for i in range(len(_OUTS)))
    return got[0]
```

```python
from contextlib import ExitStack

import concourse.bass as bass
from concourse import mybir

F32 = mybir.dt.float32
BF16 = mybir.dt.bfloat16
I32 = mybir.dt.int32
ALU = mybir.AluOpType
ACT = mybir.ActivationFunctionType
AX = mybir.AxisListType.X


def audio_tower_kernel(
    nc, x, W1, b1, W2, b2, w_q, w_k, w_v, w_o, w_gate, w_expert, b_expert,
    ph_re, ph_im, pi_re, pi_im, lc_re, lc_im, Wg, M1, M2, M3, out,
):
    P = 128
    B, V, T_IN = x.shape
    DM = W1.shape[1]
    CH = DM // P
    STRIDE = 8
    L = T_IN // STRIDE
    NTOK = B * L
    TILES = NTOK // P
    TS = 4
    STEPS = TILES // TS
    SB = B // STEPS
    SN = TS * P
    BT = P // L
    NH = 16
    HD = DM // NH
    DBLK = DM // 32
    VW = HD + 1
    E = w_gate.shape[1]
    DE = DM + E
    CAPACITY = 100
    HID = M1.shape[2]
    HC = HID // P
    EPS = 1e-5
    MAGIC = 12582912.0
    SLOTS = (2 * NTOK + E * (P - 1)) // P
    PEEL = 3
    assert L == 32 and BT == TS and HD == 16 and SLOTS % 2 == 1

    xs = nc.dram_tensor("mixture_rows_in", [NTOK, DM], F32, kind="Internal").ap()
    ys = nc.dram_tensor("mixture_rows_out", [2 * NTOK + SLOTS * P, DM], F32, kind="Internal").ap()
    out_rows = out.rearrange("b l d -> (b l) d").rearrange("(t p) d -> p t d", p=P)
    xs_tiles = xs.rearrange("(t p) d -> p t d", p=P)
    ys_tiles = ys[0:2 * NTOK, :].rearrange("(k t p) d -> p k t d", p=P, k=2)

    with ExitStack() as ctx:
        def sb(name, shape, dt=F32):
            return ctx.enter_context(nc.sbuf_tensor(name, shape, dt))

        def sem(name):
            return ctx.enter_context(nc.semaphore(name))

        def part(t, lo, n):
            a = t[:]
            if len(a.shape) > 2:
                a = a.rearrange(" ".join(["p"] + [f"d{i}" for i in range(len(a.shape) - 1)]) + " -> p ("
                                + " ".join(f"d{i}" for i in range(len(a.shape) - 1)) + ")")
            return a[:, lo:lo + n]

        ident_b = sb("ident_b", [P, P], BF16)
        ident = sb("ident", [P, P])
        ones = sb("ones", [P, P])
        ones_b = sb("ones_b", [P, P], BF16)
        tri_b = sb("tri_b", [P, P], BF16)
        batch_mean = sb("batch_mean", [P, P])
        mhalf = sb("mhalf", [P, TS])
        rank_w = sb("rank_w", [P, E])
        slot_no = sb("slot_no", [P, SLOTS])
        reset_t = sb("reset_t", [P, E, TILES])
        ones_e = sb("ones_e", [P, E])
        row_no = sb("row_no", [P, P])
        row_p = sb("row_p", [P, 1])
        tile_no = sb("tile_no", [P, 2, TILES])
        unread = sb("unread", [P, SLOTS])

        W2s = sb("W2s", [P, CH, DM])
        b1c = sb("b1c", [P, CH])
        b2r = sb("b2r", [P, DM])
        WT = sb("WT", [P, CH, 4, DM], BF16)
        WE = sb("WE", [P, CH, DE])
        bE = sb("bE", [P, DE])
        Wgs = sb("Wgs", [P, CH, E])
        M1s = sb("M1s", [P, E, CH, HID])
        M2s = sb("M2s", [P, E, CH, HID])
        M3s = sb("M3s", [P, E, HC, DM])
        wm = sb("wm", [P, 4])
        wmi = sb("wmi", [P, 4])
        wsum = sb("wsum", [P, 4])

        H = sb("H", [P, TILES, DM])
        EO = sb("EO", [P, TILES, DE])
        x1 = sb("x1", [P, TS, DM])
        xq = sb("xq", [P, TS, DM], BF16)
        xqT = sb("xqT", [P, CH, SN], BF16)
        oq = sb("oq", [P, TS, DM], BF16)
        oqT = sb("oqT", [P, CH, SN], BF16)
        qtok = sb("qtok", [P, TS, DM])
        ktok = sb("ktok", [P, TS, DBLK, 2, 2, HD])
        vtok = sb("vtok", [P, TS, NH, VW])
        QT = sb("QT", [P, TS, DBLK, 32])
        KT = sb("KT", [P, TS, DBLK, 64])
        Eb = sb("Eb", [P, 2, NH, 32])
        PT = sb("PT", [P, 2, NH, 32])
        O = sb("O", [P, TS, DM])

        X4 = EO
        W1s = part(EO, 4 * DE, STRIDE * DM).rearrange("p (r d) -> p r d", r=STRIDE)
        h1T = part(EO, 12 * DE, CH * SN).rearrange("p (c n) -> p c n", c=CH)
        xin = part(M3s, 0, 2 * SB * T_IN).rearrange("p (u b t) -> p u b t", u=2, b=SB)
        Vx = part(M1s, 0, BT * TS * NH * VW).rearrange("p (b t h n) -> p b t h n", b=BT, t=TS, h=NH)
        xT = part(x1, 0, CH * SN).rearrange("p (c n) -> p c n", c=CH)
        wraw = part(KT, 0, 4 * CH * DM).rearrange("p (w n) -> p w n", w=4)
        wter = PT[:].rearrange("p a h k -> p (a h k)").bitcast(BF16).rearrange("p (w c n) -> p w c n", w=4, c=CH)
        RT = part(qtok, 0, CH * SN)
        uR = part(ktok, 0, CH * SN)
        uI = part(ktok, CH * SN, CH * SN)
        ra = part(Eb, 0, 8 * TILES * E).rearrange("p (s t e) -> p s t e", s=8, t=TILES)
        cmp = part(PT, 0, SLOTS * E).rearrange("p (a e) -> p a e", e=E)
        in_row = part(KT, 0, TILES * P).bitcast(BF16).rearrange("p (k t m) -> p k t m", k=2, t=TILES)
        oh_w = SLOTS * 2 * TILES // 2
        in_slot, in_tile, in_part = (
            part(ktok, n * oh_w, oh_w).bitcast(BF16).rearrange("p (k t a) -> p k t a", k=2, t=TILES)
            for n in range(3))
        xrow = part(KT, 0, 2 * DM).rearrange("p (u d) -> p u d", u=2)
        xrT = part(KT, 2 * DM, 2 * DM).rearrange("p (u c n) -> p u c n", u=2, c=CH)
        actT = part(KT, 4 * DM, 2 * HID).rearrange("p (u c n) -> p u c n", u=2, c=HC)
        x4T = part(QT, 0, CH * SN).rearrange("p (c n) -> p c n", c=CH)
        sil = part(QT, 0, 2 * HID).rearrange("p (u n) -> p u n", u=2)
        yrow = part(O, 0, 2 * DM).rearrange("p (u d) -> p u d", u=2)
        back = [part(m, 0, TILES * DM).rearrange("p (t d) -> p t d", t=TILES) for m in (M1s, M2s)]

        def stats(n):
            return {k: sb(f"{k}_{n}", s) for k, s in dict(
                st=[P, TS, 6], mv=[P, TS, 2], ve=[P, TS], rstd=[P, TS], bs=[P, 2, TS], bv=[P, 2, TS], bve=[P, TS],
                rsb=[P, TS], am=[P, TS], sa=[P, TS], s=[P, TS], sw=[P, 4, TS]).items()}

        SB1, SD, SE = stats("in"), stats("att"), stats("ssm")
        SR = SB1
        mx = sb("mx", [P, 2, NH])
        rec = sb("rec", [P, TS, NH])
        vec = sb("vec", [P, 6, CH])
        sv = sb("sv", [P, 20, CH])
        CT = sb("CT", [P, CH, L + 1])
        ST = sb("ST", [P, CH, L + 1])
        Wr = sb("Wr", [P, CH, L])
        Wi = sb("Wi", [P, CH, L])
        tmpT = sb("tmpT", [P, 4, CH, L])
        lg = sb("lg", [P, TILES, E])
        rs = sb("rs", [P, 10, TILES])
        cum = sb("cum", [P, 2, E, TILES])
        mask_b = sb("mask_b", [P, TILES, E], BF16)
        slot_of = sb("slot_of", [P, 3, 2, TILES])
        src_f = sb("src_f", [P, 4, SLOTS])
        src_i = sb("src_i", [P, SLOTS], I32)
        dst_i = sb("dst_i", [P, SLOTS], I32)
        tb = sb("tb", [P, 6, E])
        exf = sb("exf", [P, SLOTS])
        exi = sb("exi", [P, SLOTS], I32)

        psum = ctx.enter_context(nc.psum_tensor("psum", [P, 8, 512], F32))
        bank = [psum[:, i, :] for i in range(8)]

        def banks(i):
            return psum[:, i:i + 2, :].rearrange("p a b -> p (a b)")

        d_w1, d_x0, d_x1, d_w2, d_b, d_att, d_we = (
            sem(n) for n in "d_w1 d_x0 d_x1 d_w2 d_b d_att d_we".split())
        d_vec, d_moe, d_m3, d_vp, d_xs, d_out = (
            sem(n) for n in "d_vec d_moe d_m3 d_vp d_xs d_out".split())
        d_slot0, d_slot1, d_ys0, d_ys1 = (
            sem(n) for n in "d_slot0 d_slot1 d_ys0 d_ys1".split())
        g_const, g_pow, g_ui, g_uc = (
            sem(n) for n in "g_const g_pow g_ui g_uc".split())
        v_chain, v_h, v_ask, v_y, v_xq, v_ob, v_oq = (
            sem(n) for n in "v_chain v_h v_ask v_y v_xq v_ob v_oq".split())
        v_hd, v_x2, v_sc, v_qk, v_sub, v_pt, v_o = (
            sem(n) for n in "v_hd v_x2 v_sc v_qk v_sub v_pt v_o".split())
        v_wabs, v_wt, v_xc, v_ur, v_yc, v_x4, v_mask = (
            sem(n) for n in "v_wabs v_wt v_xc v_ur v_yc v_x4 v_mask".split())
        v_mask2, v_exp_no, v_exp, v_act, v_xx, v_eo = (
            sem(n) for n in "v_mask2 v_exp_no v_exp v_act v_xx v_eo".split())
        v_hfin, v_ra = (
            sem(n) for n in "v_hfin v_ra".split())
        p_wsum, p_wt, p_l1, p_l2, p_bv, p_xt, p_qkv = (
            sem(n) for n in "p_wsum p_wt p_l1 p_l2 p_bv p_xt p_qkv".split())
        p_s, p_pv, p_ob, p_ot, p_o, p_x2, p_e = (
            sem(n) for n in "p_s p_pv p_ob p_ot p_o p_x2 p_e".split())
        p_cum, p_cum2, p_x3, p_y3, p_x4, p_lg, p_xr = (
            sem(n) for n in "p_cum p_cum2 p_x3 p_y3 p_x4 p_lg p_xr".split())
        p_up_h, p_up_g, p_at, p_dn = (
            sem(n) for n in "p_up_h p_up_g p_at p_dn".split())
        a_wt, a_pad, a_h1, a_xt, a_qkv, a_exp, a_ot = (
            sem(n) for n in "a_wt a_pad a_h1 a_xt a_qkv a_exp a_ot".split())
        a_x2, a_x3, a_x4, a_lg, a_gate, a_r, a_xr = (
            sem(n) for n in "a_x2 a_x3 a_x4 a_lg a_gate a_r a_xr".split())
        a_sil, a_at, a_y = (
            sem(n) for n in "a_sil a_at a_y".split())

        d_back = [sem(f"d_back{t}") for t in range(STEPS)]
        v_hot, v_row, v_src, g_tile, a_part, p_tab = (
            sem(n) for n in "v_hot v_row v_src g_tile a_part p_tab".split())

        block = ctx.enter_context(nc.Block())

        def wait(eng, s, n):
            if n > 0:
                eng.wait_ge(s, n)

        def done(slot, lag):
            return max(0, min(STEPS, slot - lag + 1))

        def step_of(slot, lag):
            i = slot - lag
            return i if 0 <= i < STEPS else None

        A_LAG, B_LAG, C_LAG, D_LAG = 0, 1, 2, 3
        SLOTS_OF_STEPS = STEPS + D_LAG
        N_LAG, S_LAG, R_LAG = 0, 1, 2

        @block.sync
        def _(sp):
            w1_v = W1.rearrange("(v s r) d -> s v r d", s=2, r=STRIDE)
            xv = x.rearrange("b v t -> v b t")

            def load_x(i):
                s_x = (d_x0, d_x1)[i % 2]
                sp.dma_start(xin[0:64, i % 2], xv[:, SB * i:SB * (i + 1), :]).then_inc(s_x, 16)
                sp.dma_start(xin[64:128, i % 2, :, 0:T_IN - STRIDE],
                             xv[:, SB * i:SB * (i + 1), STRIDE:T_IN]).then_inc(s_x, 16)

            for s in range(2):
                sp.dma_start(W1s[64 * s:64 * s + 64], w1_v[s]).then_inc(d_w1, 16)
            load_x(0)
            for n, w in enumerate((w_q, w_k, w_v, w_o)):
                sp.dma_start(wraw[:, n, :].rearrange("p (c i) -> p c i", c=CH),
                             w.rearrange("(c p) i -> p c i", p=P)).then_inc(d_att, 16)
            sp.dma_start(W2s[:], W2.rearrange("(c p) d -> p c d", p=P)).then_inc(d_w2, 16)
            load_x(1)
            sp.dma_start(WE[:, :, 0:DM], w_expert.rearrange("(c p) d -> p c d", p=P)).then_inc(d_we, 16)
            sp.dma_start(WE[:, :, DM:], w_gate.rearrange("(c p) d -> p c d", p=P)).then_inc(d_we, 16)
            sp.dma_start(Wgs[:], Wg.rearrange("(c p) d -> p c d", p=P)).then_inc(d_we, 16)
            for i in range(2, STEPS):
                sp.wait_ge(p_l1, CH * (i - 1))
                load_x(i)
            sp.wait_ge(g_const, 22)
            for i in range(STEPS):
                sp.wait_ge(a_qkv, TS * (i + 1))
                if i > 0:
                    sp.wait_ge(p_pv, BT * i)
                for b in range(BT):
                    for t in range(TS):
                        sp.dma_start(Vx[32 * t:32 * t + 32, b, t].rearrange("k h n -> k (h n)"),
                                     vtok[32 * b:32 * b + 32, t].rearrange("k h n -> k (h n)")).then_inc(d_vp, 16)
                if i == 1:
                    sp.dma_start(M2s[:], M2.rearrange("e (c p) h -> p e c h", p=P)).then_inc(d_moe, 16)
            sp.wait_ge(p_pv, BT * STEPS)
            sp.dma_start(M1s[:], M1.rearrange("e (c p) h -> p e c h", p=P)).then_inc(d_moe, 16)
            sp.wait_ge(p_l1, CH * STEPS)
            sp.dma_start(M3s[:], M3.rearrange("e (c p) d -> p e c d", p=P)).then_inc(d_m3, 16)
            for i in range(STEPS):
                sp.wait_ge(v_x4, i + 1)
                sp.dma_start(xs_tiles[:, TS * i:TS * (i + 1), :], X4[:, TS * i:TS * (i + 1), 0:DM]).then_inc(d_xs, 16)
            sp.wait_ge(d_ys0, 16 * ((SLOTS + 1) // 2))
            sp.wait_ge(d_ys1, 16 * (SLOTS // 2))
            sp.wait_ge(p_dn, SLOTS)
            for i in range(STEPS):
                for k in range(2):
                    sp.dma_start(back[k][:, TS * i:TS * (i + 1), :], ys_tiles[:, k, TS * i:TS * (i + 1), :]
                                 ).then_inc(d_back[i], 16)
            for t in range(TILES):
                sp.wait_ge(v_hfin, t + 1)
                sp.dma_start(out_rows[:, t, :], H[:, t, :]).then_inc(d_out, 16)
            sp.wait_ge(d_out, 16 * TILES)

        @block.gpsimd
        def _(pool):
            gp = nc.gpsimd
            gp.iota(row_no[:], pattern=[[1, P]], base=0, channel_multiplier=0,
                    allow_small_or_imprecise_dtypes=True).then_inc(g_const, 1)
            for t, v in ((ident_b, 0.0), (ident, 0.0), (tri_b, 1.0), (batch_mean, 1.0 / L), (ones_e, 1.0),
                         (ones, 1.0), (ones_b, 1.0), (mhalf, -0.5), (reset_t, 1.0)):
                gp.memset(t[:], v).then_inc(g_const, 1)
            gp.memset(bE[:, DM:], 0.0).then_inc(g_const, 1)
            gp.iota(rank_w[:], pattern=[[-1, E]], base=E, channel_multiplier=0,
                    allow_small_or_imprecise_dtypes=True).then_inc(g_const, 1)
            gp.iota(slot_no[:], pattern=[[1, SLOTS]], base=0, channel_multiplier=0,
                    allow_small_or_imprecise_dtypes=True).then_inc(g_const, 1)
            pool.wait_ge(g_const, 13)
            for t in (ident_b, ident):
                gp.affine_select(out=t[:], in_=t[:], compare_op=ALU.not_equal, fill=1.0, base=0,
                                 pattern=[[-1, P]], channel_multiplier=1).then_inc(g_const, 1)
            gp.affine_select(out=tri_b[:], in_=tri_b[:], compare_op=ALU.is_ge, fill=0.0, base=0,
                             pattern=[[1, P]], channel_multiplier=-1).then_inc(g_const, 1)
            bm = batch_mean[:].rearrange("p (a b) -> p a b", b=L)
            gp.affine_select(out=bm, in_=bm, compare_op=ALU.is_ge, fill=0.0, base=0,
                             pattern=[[-L, BT], [0, L]], channel_multiplier=1).then_inc(g_const, 1)
            pool.wait_ge(g_const, 17)
            gp.affine_select(out=bm, in_=bm, compare_op=ALU.is_ge, fill=0.0, base=L - 1,
                             pattern=[[L, BT], [0, L]], channel_multiplier=-1).then_inc(g_const, 1)
            gp.memset(reset_t[:, :, 0:1], 0.0).then_inc(g_const, 1)
            gp.memset(ktok[:], 0.0).then_inc(g_const, 1)
            gp.memset(vtok[:], 1.0).then_inc(g_const, 1)
            gp.memset(Vx, 0.0).then_inc(g_const, 1)
            gp.iota(row_p[:], pattern=[[0, 1]], base=0, channel_multiplier=1,
                    allow_small_or_imprecise_dtypes=True).then_inc(g_const, 1)
            gp.iota(tile_no[:], pattern=[[TILES, 2], [1, TILES]], base=1, channel_multiplier=0,
                    allow_small_or_imprecise_dtypes=True).then_inc(g_const, 1)
            gp.iota(unread[:], pattern=[[P, SLOTS]], base=2 * NTOK + P, channel_multiplier=1,
                    allow_small_or_imprecise_dtypes=True).then_inc(g_const, 1)

            asked = [0]

            def power(dst, src):
                asked[0] += 1
                pool.wait_ge(v_ask, asked[0])
                gp.tensor_tensor(dst, src, mhalf[:, 0:src.shape[-1]], ALU.pow).then_inc(g_pow, 1)

            power(sv[:, 3, :], sv[:, 2, :])
            for slot in range(SLOTS_OF_STEPS):
                if step_of(slot, D_LAG) is not None:
                    power(SD["rsb"][:], SD["bve"][:])
                if step_of(slot, B_LAG) is not None:
                    power(SB1["rstd"][:], SB1["ve"][:])
                    power(SB1["rsb"][:], SB1["bve"][:])
                if step_of(slot, D_LAG) is not None:
                    power(SD["rstd"][:], SD["ve"][:])

            for slot in range(STEPS + R_LAG):
                iN, iS, iR = (step_of(slot, lag) for lag in (N_LAG, S_LAG, R_LAG))
                if iS is not None:
                    pool.wait_ge(a_x3, iS + 1)
                    wait(pool, v_yc, iS)
                    gp.tensor_tensor(uI.rearrange("p (c b l) -> p c b l", c=CH, l=L),
                                     xT.rearrange("p c (b l) -> p c b l", l=L),
                                     Wi[:].rearrange("p c (a l) -> p c a l", a=1).to_broadcast([P, CH, SB, L]),
                                     ALU.mult).then_inc(g_ui, 1)
                if iR is not None:
                    power(SR["rstd"][:], SR["ve"][:])
                if iN is not None:
                    power(SE["rstd"][:], SE["ve"][:])
                if iS is not None:
                    pool.wait_ge(v_ur, iS + 1)
                    gp.tensor_tensor(uR.rearrange("p (c b l) -> p c b l", c=CH, l=L),
                                     uR.rearrange("p (c b l) -> p c b l", c=CH, l=L),
                                     CT[:, :, 0:L].rearrange("p c (a l) -> p c a l", a=1).to_broadcast([P, CH, SB, L]),
                                     ALU.mult).then_inc(g_uc, 1)
            pool.wait_ge(v_hot, 1)
            gp.tensor_tensor(in_tile, in_slot,
                             tile_no[:].rearrange("p k (t a) -> p k t a", a=1).to_broadcast([P, 2, TILES, SLOTS]),
                             ALU.mult).then_inc(g_tile, 1)
            pool.wait_ge(d_xs, 16 * STEPS)
            pool.wait_ge(v_src, 1)

            def fetch(j):
                wait(pool, p_xr, j - 1)
                gp.indirect_dma_start(xrow[:, j % 2, :], None, xs,
                                      bass.IndirectOffsetOnAxis(ap=src_i[:, j:j + 1], axis=0)
                                      ).then_inc((d_slot0, d_slot1)[j % 2], 16)

            def deliver(j):
                pool.wait_ge(a_y, j + 1)
                gp.indirect_dma_start(ys, bass.IndirectOffsetOnAxis(ap=dst_i[:, j:j + 1], axis=0),
                                      yrow[:, j % 2, :], None).then_inc((d_ys0, d_ys1)[j % 2], 16)

            for j in range(3):
                fetch(j)
            for j in range(SLOTS):
                if j + 3 < SLOTS:
                    fetch(j + 3)
                deliver(j)

        @block.scalar
        def _(act):
            a = nc.scalar
            def pad(i):
                act.wait_ge((d_x0, d_x1)[i % 2], 32 * (i // 2 + 1))
                a.activation(xin[64:128, i % 2, :, T_IN - STRIDE:T_IN],
                             xin[64:128, i % 2, :, T_IN - STRIDE - 1:T_IN - STRIDE].to_broadcast([64, SB, STRIDE]),
                             ACT.Copy).then_inc(a_pad, 1)

            for n, v in enumerate((ph_re, ph_im, pi_re, pi_im, lc_re, lc_im)):
                act.dma_start(vec[:, n, :], v.rearrange("(c p) -> p c", p=P),
                              allow_slow_non_contiguous=True).then_inc(d_vec, 16)
            act.dma_start(b1c[:], b1.rearrange("(c p) -> p c", p=P), allow_slow_non_contiguous=True).then_inc(d_b, 16)
            act.dma_start(b2r[:], b2.partition_broadcast(P)).then_inc(d_b, 16)
            act.dma_start(bE[:, 0:DM], b_expert.partition_broadcast(P)).then_inc(d_b, 16)
            pad(0)
            act.wait_ge(v_exp, 1)
            a.activation(sv[:, 4, :], sv[:, 5, :], ACT.Exp, scale=-1.0).then_inc(a_r, 1)
            for c in range(CH):
                act.wait_ge(p_wt, c + 1)
                a.activation(WT[:, c].rearrange("p w d -> p (w d)"), bank[4 + c].bitcast(BF16), ACT.Copy
                             ).then_inc(a_wt, 1)
            act.wait_ge(d_b, 48)

            def exps(i, batches):
                for b in batches:
                    act.wait_ge(v_sub, BT * i + b + 1)
                    a.activation(Eb[:, b % 2], Eb[:, b % 2], ACT.Exp).then_inc(a_exp, 1)

            for slot in range(SLOTS_OF_STEPS):
                iA, iB, iC, iD = (step_of(slot, lag) for lag in (A_LAG, B_LAG, C_LAG, D_LAG))
                if iA is not None:
                    for c in range(CH):
                        act.wait_ge(p_l1, CH * iA + c + 1)
                        wait(act, p_l2, TS * iA)
                        a.activation(h1T[:, c, :], bank[c], ACT.Relu, bias=b1c[:, c:c + 1]).then_inc(a_h1, 1)
                    if iA + 1 < STEPS:
                        pad(iA + 1)
                if iD is not None:
                    act.wait_ge(p_ot, iD + 1)
                    wait(act, p_o, TS * iD)
                    a.activation(oqT[:].rearrange("p c n -> p (c n)"), bank[3].bitcast(BF16), ACT.Copy).then_inc(a_ot, 1)
                if iB is not None:
                    act.wait_ge(p_xt, iB + 1)
                    wait(act, p_qkv, TS * iB)
                    a.activation(xqT[:].rearrange("p c n -> p (c n)"), bank[4].bitcast(BF16), ACT.Copy).then_inc(a_xt, 1)
                if iC is not None:
                    exps(iC, range(0, 2))
                if iB is not None:
                    act.wait_ge(v_sc, iB + 1)
                    wait(act, v_qk, iB)
                    wait(act, d_vp, 16 * BT * TS * iB)
                    if iB == 0:
                        act.wait_ge(g_const, 21)
                    for t in range(TS):
                        act.wait_ge(p_qkv, TS * iB + t + 1)
                        qk = bank[(3, 5)[t % 2]]
                        a.activation(qtok[:, t, :], qk[:, 0:DM], ACT.Copy, scale=SB1["sw"][:, 0, t:t + 1])
                        for h in range(2):
                            a.activation(ktok[:, t, :, h, h, :],
                                         qk[:, DM:2 * DM].rearrange("p (n h d) -> p n h d", h=2, d=HD)[:, :, h, :],
                                         ACT.Copy, scale=SB1["sw"][:, 1, t:t + 1])
                        a.activation(vtok[:, t, :, 0:HD],
                                     bank[(2, 4)[t % 2]][:, 0:DM].rearrange("p (h d) -> p h d", d=HD),
                                     ACT.Copy, scale=SB1["sw"][:, 2, t:t + 1]).then_inc(a_qkv, 1)
                if iD is not None:
                    act.wait_ge(p_x2, iD + 1)
                    wait(act, v_xq, done(slot, B_LAG))
                    a.activation(xT.rearrange("p c n -> p (c n)"), banks(0), ACT.Copy).then_inc(a_x2, 1)
                if iC is not None:
                    exps(iC, range(2, BT))
            act.wait_ge(v_xx, 1)
            a.activation(ra[:, 5], ra[:, 3], ACT.Exp).then_inc(a_gate, 1)
            for slot in range(STEPS + R_LAG):
                iN, iS, iR = (step_of(slot, lag) for lag in (N_LAG, S_LAG, R_LAG))
                if iR is not None:
                    act.wait_ge(p_x4, iR + 1)
                    wait(act, p_lg, iR)
                    a.activation(x4T.rearrange("p c n -> p (c n)"), banks(4), ACT.Copy).then_inc(a_x4, 1)
                if iN is not None:
                    act.wait_ge(p_x3, iN + 1)
                    wait(act, v_ur, iN)
                    wait(act, g_ui, iN)
                    a.activation(xT.rearrange("p c n -> p (c n)"), banks(0), ACT.Copy).then_inc(a_x3, 1)
            act.wait_ge(v_ra, 1)
            a.activation(rs[:, 4, :], rs[:, 3, :], ACT.Exp).then_inc(a_lg, 1)
            act.wait_ge(v_hot, 1)
            a.activation(in_part, in_slot, ACT.Copy, scale=row_p[:, 0:1]).then_inc(a_part, 1)

            def slot_rows(j, u):
                act.wait_ge(p_xr, j + 1)
                a.activation(xrT[:, u].rearrange("p c n -> p (c n)"), bank[u][:, 0:DM], ACT.Copy).then_inc(a_xr, 1)

            def slot_silu(j, u):
                act.wait_ge(p_up_h, j + 1)
                a.activation(sil[:, u, :], bank[2], ACT.Silu).then_inc(a_sil, 1)

            def slot_act(j, u):
                act.wait_ge(p_at, j + 1)
                a.activation(actT[:, u].rearrange("p c n -> p (c n)"), bank[4 + u], ACT.Copy).then_inc(a_at, 1)

            def slot_out(j, u, stored):
                act.wait_ge(p_dn, j + 1)
                if stored is not None:
                    act.wait_ge((d_ys0, d_ys1)[u], stored)
                a.activation(yrow[:, u, :], bank[6 + u][:, 0:DM], ACT.Copy).then_inc(a_y, 1)

            def slot_step(j, u, stored):
                slot_act(j, u)
                if not isinstance(j, int) or j + 2 < SLOTS:
                    slot_rows(j + 2, u)
                if not isinstance(j, int) or j + 1 < SLOTS:
                    slot_silu(j + 1, 1 - u)
                slot_out(j, u, stored)

            slot_rows(0, 0)
            slot_rows(1, 1)
            slot_silu(0, 0)
            for j in range(PEEL):
                slot_step(j, j % 2, 16 * (j // 2) or None)
            with act.Fori(0, (SLOTS - 2 - PEEL) // 2) as t:
                slot_step(2 * t + PEEL, 1, 16 * t + 16)
                slot_step(2 * t + PEEL + 1, 0, 16 * t + 32)
            for j in range(SLOTS - 2, SLOTS):
                slot_step(j, j % 2, 16 * (j // 2))

        @block.vector
        def _(dve):
            v = nc.vector
            chain = [0]

            def ln(ins):
                chain[0] += 1
                ins.then_inc(v_chain, 1)

            def own():
                dve.wait_ge(v_chain, chain[0])

            asked = [0]

            def ask(ins):
                asked[0] += 1
                ins.then_inc(v_ask, 1)

            def answered(later=0):
                dve.wait_ge(g_pow, asked[0] - later)

            dve.wait_ge(d_att, 64)
            v.tensor_reduce(wsum[:], wraw, AX, ALU.add, apply_absolute_value=True).then_inc(v_wabs, 1)
            dve.wait_ge(d_vec, 96)
            pr, pim = vec[:, 0, :], vec[:, 1, :]
            t = [sv[:, k, :] for k in range(20)]
            ln(v.tensor_tensor(t[5], pr, pr, ALU.mult))
            ln(v.tensor_tensor(t[6], pim, pim, ALU.mult))
            ln(v.tensor_scalar(t[7], pr, -1.0, None, ALU.mult))
            ln(v.tensor_scalar(t[8], pim, -1.0, None, ALU.mult))
            own()
            v.tensor_tensor(t[5], t[5], t[6], ALU.add).then_inc(v_exp, 1)
            ln(v.tensor_tensor(t[7], t[7], pr, ALU.max))
            ln(v.tensor_tensor(t[8], t[8], pim, ALU.max))
            own()
            ln(v.tensor_tensor(t[9], t[7], t[8], ALU.max))
            own()
            ln(v.tensor_scalar(t[10], t[9], 0.0, None, ALU.is_equal))
            own()
            ln(v.tensor_tensor(t[9], t[9], t[10], ALU.add))
            own()
            ln(v.reciprocal(t[11], t[9]))
            own()
            ln(v.tensor_tensor(t[12], pr, t[11], ALU.mult))
            ln(v.tensor_tensor(t[13], pim, t[11], ALU.mult))
            own()
            ln(v.tensor_tensor(t[12], t[12], t[10], ALU.add))
            own()
            ln(v.tensor_tensor(t[14], t[12], t[12], ALU.mult))
            ln(v.tensor_tensor(t[15], t[13], t[13], ALU.mult))
            own()
            ask(v.tensor_tensor(t[2], t[14], t[15], ALU.add))
            answered()
            ln(v.memset(CT[:, :, 0:1], 1.0))
            ln(v.memset(ST[:, :, 0:1], 0.0))
            one = lambda a_: a_.rearrange("p (c a) -> p c a", a=1)
            ln(v.tensor_tensor(CT[:, :, 1:2], one(t[12]), one(t[3]), ALU.mult))
            ln(v.tensor_tensor(ST[:, :, 1:2], one(t[13]), one(t[3]), ALU.mult))
            own()
            n = 1
            while n < L:
                cn = CT[:, :, n:n + 1].to_broadcast([P, CH, n])
                sn = ST[:, :, n:n + 1].to_broadcast([P, CH, n])
                q = [tmpT[:, k, :, 0:n] for k in range(4)]
                ln(v.tensor_tensor(q[0], CT[:, :, 1:n + 1], cn, ALU.mult))
                ln(v.tensor_tensor(q[1], ST[:, :, 1:n + 1], sn, ALU.mult))
                ln(v.tensor_tensor(q[2], CT[:, :, 1:n + 1], sn, ALU.mult))
                ln(v.tensor_tensor(q[3], ST[:, :, 1:n + 1], cn, ALU.mult))
                own()
                ln(v.tensor_tensor(CT[:, :, n + 1:2 * n + 1], q[0], q[1], ALU.subtract))
                ln(v.tensor_tensor(ST[:, :, n + 1:2 * n + 1], q[2], q[3], ALU.add))
                own()
                n *= 2
            q = [tmpT[:, k] for k in range(4)]
            bc = lambda k: one(vec[:, k, :]).to_broadcast([P, CH, L])
            ln(v.tensor_tensor(q[0], CT[:, :, 0:L], bc(2), ALU.mult))
            ln(v.tensor_tensor(q[1], ST[:, :, 0:L], bc(3), ALU.mult))
            ln(v.tensor_tensor(q[2], CT[:, :, 0:L], bc(3), ALU.mult))
            ln(v.tensor_tensor(q[3], ST[:, :, 0:L], bc(2), ALU.mult))
            own()
            ln(v.tensor_tensor(Wr[:], q[0], q[1], ALU.add))
            ln(v.tensor_tensor(Wi[:], q[2], q[3], ALU.subtract))
            own()
            c1, s1 = CT[:, :, 1:2], ST[:, :, 1:2]
            ln(v.tensor_tensor(one(t[14]), one(vec[:, 4, :]), c1, ALU.mult))
            ln(v.tensor_tensor(one(t[15]), one(vec[:, 5, :]), s1, ALU.mult))
            ln(v.tensor_tensor(one(t[16]), one(vec[:, 4, :]), s1, ALU.mult))
            ln(v.tensor_tensor(one(t[17]), one(vec[:, 5, :]), c1, ALU.mult))
            own()
            ln(v.tensor_tensor(t[14], t[14], t[15], ALU.subtract))
            ln(v.tensor_tensor(t[16], t[16], t[17], ALU.add))
            own()
            dve.wait_ge(a_r, 1)
            ln(v.tensor_tensor(t[18], t[14], t[4], ALU.mult))
            ln(v.tensor_tensor(t[19], t[16], t[4], ALU.mult))
            dve.wait_ge(p_wsum, 1)
            ln(v.tensor_scalar(wm[:], bank[6][:, 0:4], 1.0 / (DM * DM), 1e-5, ALU.mult, ALU.max))
            own()
            ln(v.reciprocal(wmi[:], wm[:]))
            own()
            for w in range(4):
                ln(v.tensor_scalar(wraw[:, w, :], wraw[:, w, :], wmi[:, w:w + 1], MAGIC, ALU.mult, ALU.add))
            own()
            allw = wraw.rearrange("p w n -> p (w n)")
            ln(v.tensor_scalar(allw, allw, MAGIC, 1.0, ALU.subtract, ALU.min))
            own()
            v.tensor_scalar(wter.rearrange("p w c n -> p (w c n)"), allw, -1.0, None, ALU.max).then_inc(v_wt, 1)

            def norm_stats(S, rows):
                for t_ in range(TS):
                    ln(v.bn_stats(S["st"][:, t_, :], rows(t_)))
                own()
                for t_ in range(TS):
                    ln(v.bn_aggr(S["mv"][:, t_, :], S["st"][:, t_, :]))
                own()

            def ask_rstd(S):
                ask(v.tensor_scalar(S["ve"][:], S["mv"][:, :, 1], EPS, None, ALU.add))

            def scales(S, rows, weights):
                ln(v.tensor_reduce(S["am"][:], rows, AX, ALU.max, apply_absolute_value=True))
                answered()
                own()
                ln(v.tensor_tensor(S["am"][:], S["am"][:], S["rsb"][:], ALU.mult))
                own()
                ln(v.tensor_scalar(S["sa"][:], S["am"][:], 1e-5, 1.0 / 127.0, ALU.max, ALU.mult))
                own()
                ln(v.reciprocal(S["s"][:], S["sa"][:]))
                for n_, (w_, extra) in enumerate(weights):
                    ln(v.tensor_scalar(S["sw"][:, n_, :], S["sa"][:], wm[:, w_:w_ + 1], extra, ALU.mult, ALU.mult))
                own()
                ln(v.tensor_tensor(S["s"][:], S["s"][:], S["rsb"][:], ALU.mult))
                own()

            def minus_max(i, b):
                m = mx[:, b % 2, :]
                s_ = bank[b % 2].rearrange("p (h k) -> p h k", k=32)
                dve.wait_ge(p_s, BT * i + b + 1)
                ln(v.tensor_reduce(m, s_, AX, ALU.max))
                own()
                wait(dve, v_pt, BT * i + b - 1)
                v.tensor_tensor(Eb[:, b % 2], s_, m.rearrange("p (h a) -> p h a", a=1).to_broadcast([P, NH, 32]),
                                ALU.subtract).then_inc(v_sub, 1)

            def turn(i, b):
                dve.wait_ge(a_exp, BT * i + b + 1)
                wait(dve, p_pv, BT * i + b - 1)
                v.transpose(PT[:, b % 2].rearrange("p h k -> p (h k)"), Eb[:, b % 2].rearrange("p h k -> p (h k)")
                            ).then_inc(v_pt, 1)

            for slot in range(SLOTS_OF_STEPS):
                iA, iB, iC, iD = (step_of(slot, lag) for lag in (A_LAG, B_LAG, C_LAG, D_LAG))
                if iD is not None:
                    norm_stats(SD, lambda t_: O[:, t_, :])
                    mean, var = SD["mv"][:, :, 0], SD["mv"][:, :, 1]
                    ln(v.tensor_copy(SD["bs"][:, 0, :], mean))
                    ln(v.tensor_tensor(SD["st"][:, :, 0], mean, mean, ALU.mult))
                    own()
                    v.tensor_tensor(SD["bs"][:, 1, :], SD["st"][:, :, 0], var, ALU.add).then_inc(v_ob, 1)
                if iB is not None:
                    i = iB
                    dve.wait_ge(v_h, TS * (i + 1))
                    wait(dve, p_e, TS * done(slot - 1, D_LAG))
                    norm_stats(SB1, lambda t_: H[:, TS * i + t_, :])
                if iD is not None:
                    dve.wait_ge(p_ob, iD + 1)
                    ln(v.tensor_copy(SD["bv"][:].rearrange("p a t -> p (a t)"), bank[3][:, 0:2 * TS]))
                    own()
                    mu, e2 = SD["bv"][:, 0, :], SD["bv"][:, 1, :]
                    ln(v.tensor_tensor(SD["am"][:], mu, mu, ALU.mult))
                    own()
                    ln(v.tensor_tensor(e2, e2, SD["am"][:], ALU.subtract))
                    own()
                    ask(v.tensor_scalar(SD["bve"][:], e2, 0.0, EPS, ALU.max, ALU.add))
                    for t_ in range(TS):
                        ln(v.tensor_scalar(O[:, t_, :], O[:, t_, :], mu[:, t_:t_ + 1], None, ALU.subtract))
                    own()
                    scales(SD, O[:], [(3, 1.0)])
                    for t_ in range(TS):
                        ln(v.tensor_scalar(O[:, t_, :], O[:, t_, :], SD["s"][:, t_:t_ + 1], MAGIC, ALU.mult, ALU.add))
                    own()
                    wait(dve, p_ot, iD)
                    v.tensor_scalar(oq[:], O[:], MAGIC, 127.0, ALU.subtract, ALU.min).then_inc(v_oq, 1)
                if iB is not None:
                    ask_rstd(SB1)
                    answered()
                    mean, var, r_ = SB1["mv"][:, :, 0], SB1["mv"][:, :, 1], SB1["rstd"]
                    ln(v.tensor_tensor(SB1["bs"][:, 1, :], var, r_[:], ALU.mult))
                    own()
                    v.tensor_tensor(SB1["bs"][:, 0, :], SB1["bs"][:, 1, :], r_[:], ALU.mult).then_inc(v_y, 1)
                    for t_ in range(TS):
                        ln(v.tensor_scalar(x1[:, t_, :], H[:, TS * iB + t_, :], mean[:, t_:t_ + 1], r_[:, t_:t_ + 1],
                                           ALU.subtract, ALU.mult))
                    dve.wait_ge(p_bv, iB + 1)
                    ask(v.tensor_scalar(SB1["bve"][:], bank[2][:, 0:TS], EPS, None, ALU.add))
                    own()
                    wait(dve, a_qkv, TS * iB)
                    scales(SB1, x1[:], [(0, HD ** -0.5), (1, 1.0), (2, 1.0)])
                    for t_ in range(TS):
                        ln(v.tensor_scalar(x1[:, t_, :], x1[:, t_, :], SB1["s"][:, t_:t_ + 1], MAGIC, ALU.mult, ALU.add))
                    own()
                    v.engine_nop().then_inc(v_sc, 1)
                    wait(dve, p_xt, iB)
                    v.tensor_scalar(xq[:], x1[:], MAGIC, 127.0, ALU.subtract, ALU.min).then_inc(v_xq, 1)
                if iC is not None:
                    minus_max(iC, 0)
                    minus_max(iC, 1)
                if iA is not None:
                    dve.wait_ge(d_b, 48)
                    for t_ in range(TS):
                        dve.wait_ge(p_l2, TS * iA + 2 * (t_ // 2) + 2)
                        v.tensor_tensor(H[:, TS * iA + t_, :], bank[6 + t_ // 2][:, DM * (t_ % 2):DM * (t_ % 2 + 1)],
                                        b2r[:], ALU.add).then_inc(v_h, 1)
                if iC is not None:
                    turn(iC, 0)
                    turn(iC, 1)
                if iD is not None:
                    for t_ in range(TS):
                        dve.wait_ge(p_o, TS * iD + 2 * (t_ // 2) + 2)
                        hrow = H[:, TS * iD + t_, :]
                        ln(v.scalar_tensor_tensor(hrow, bank[6 + t_ // 2][:, DM * (t_ % 2):DM * (t_ % 2 + 1)],
                                                  SD["sw"][:, 0, t_:t_ + 1], hrow, ALU.mult, ALU.add))
                    own()
                    v.engine_nop().then_inc(v_hd, 1)
                    norm_stats(SD, lambda t_: H[:, TS * iD + t_, :])
                    ask_rstd(SD)
                if iC is not None:
                    minus_max(iC, 2)
                    minus_max(iC, 3)
                if iD is not None:
                    answered()
                    for t_ in range(TS):
                        r = v.tensor_scalar(O[:, t_, :], H[:, TS * iD + t_, :], SD["mv"][:, t_, 0:1],
                                            SD["rstd"][:, t_:t_ + 1], ALU.subtract, ALU.mult)
                    r.then_inc(v_x2, 1)
                if iC is not None:
                    turn(iC, 2)
                    turn(iC, 3)
                if iB is not None:
                    dve.wait_ge(a_qkv, TS * (iB + 1))
                    wait(dve, p_s, BT * iB)
                    if iB == 0:
                        dve.wait_ge(p_wt, CH)
                    v.transpose(QT[:].rearrange("p t n k -> p (t n k)"), qtok[:].rearrange("p t d -> p (t d)"))
                    v.transpose(KT[:].rearrange("p t n k -> p (t n k)"),
                                ktok[:].rearrange("p t n a b d -> p (t n a b d)")).then_inc(v_qk, 1)
                if iD is not None:
                    for t_ in range(TS):
                        dve.wait_ge(p_e, TS * iD + t_ + 1)
                        v.tensor_tensor(EO[:, TS * iD + t_, :], bank[6 + t_ % 2][:, 0:DE], bE[:], ALU.add
                                        ).then_inc(v_eo, 1)
                if iC is not None:
                    dve.wait_ge(p_pv, BT * (iC + 1))
                    wait(dve, p_x2, done(slot, D_LAG))
                    HB = NH // 4
                    rows = [bank[2 + k][:, 0:HB * TS * VW].rearrange("p (h t n) -> p h t n", h=HB, t=TS)
                            for k in range(4)]
                    recs = [rec[:, :, HB * k:HB * (k + 1)].rearrange("p t (h a) -> p h t a", a=1) for k in range(4)]
                    for k in range(4):
                        ln(v.reciprocal(recs[k], rows[k][:, :, :, HD:VW]))
                    own()
                    for k in range(4):
                        ln(v.tensor_tensor(O[:, :, HB * HD * k:HB * HD * (k + 1)].rearrange("p t (h d) -> p h t d", d=HD),
                                           rows[k][:, :, :, 0:HD], recs[k].to_broadcast([P, HB, TS, HD]), ALU.mult))
                    own()
                    v.engine_nop().then_inc(v_o, 1)

            te = lambda a_: a_.rearrange("p (t a) -> p t a", a=1).to_broadcast([P, TILES, E])
            rw = rank_w[:].rearrange("p (a e) -> p a e", a=1).to_broadcast([P, TILES, E])

            def best(logits, m, tie, oh, s1_, s2_):
                ln(v.tensor_reduce(m, logits, AX, ALU.max))
                own()
                ln(v.tensor_tensor(s1_, logits, te(m), ALU.is_equal))
                own()
                ln(v.tensor_tensor(s2_, s1_, rw, ALU.mult))
                own()
                ln(v.tensor_reduce(tie, s2_, AX, ALU.max))
                own()
                ln(v.tensor_tensor(oh, s2_, te(tie), ALU.is_equal))
                own()

            def queue_places(signal, ready, total):
                dve.wait_ge(ready, 1)
                ct = cum[:, 0]
                ln(v.tensor_copy(ct, bank[7][:, 0:TILES * E].rearrange("p (t e) -> p e t", e=E)))
                own()
                ln(v.tensor_tensor_scan(cum[:, 1].rearrange("p e t -> p (e t)"), reset_t[:].rearrange("p e t -> p (e t)"),
                                        ct.rearrange("p e t -> p (e t)"), 0.0, ALU.mult, ALU.add))
                own()
                ln(v.tensor_tensor(ct, cum[:, 1], ct, ALU.subtract))
                own()
                ln(v.tensor_tensor(ra[:, 7], bank[6][:, 0:TILES * E].rearrange("p (t e) -> p t e", e=E),
                                   ct.rearrange("p e t -> p t e"), ALU.add))
                own()

            dve.wait_ge(v_eo, TILES)
            dve.wait_ge(v_pt, BT * STEPS)
            dve.wait_ge(g_const, 21)
            ln(v.tensor_copy(lg[:], EO[:, :, DM:DE]))
            own()
            best(lg[:], rs[:, 0, :], rs[:, 1, :], ra[:, 0], ra[:, 1], ra[:, 2])
            v.tensor_copy(mask_b[:], ra[:, 0]).then_inc(v_mask, 1)
            ln(v.tensor_tensor(ra[:, 3], lg[:], te(rs[:, 0, :]), ALU.subtract))
            own()
            v.engine_nop().then_inc(v_xx, 1)
            queue_places(None, p_cum, None)
            ln(v.tensor_scalar(ra[:, 4], ra[:, 7], float(CAPACITY), None, ALU.is_le))
            own()
            ln(v.tensor_tensor(ra[:, 4], ra[:, 4], ra[:, 0], ALU.mult))
            own()
            ln(v.tensor_reduce(rs[:, 2, :], ra[:, 4], AX, ALU.add))
            dve.wait_ge(a_gate, 1)
            ln(v.tensor_reduce(rs[:, 5, :], ra[:, 5], AX, ALU.add))
            own()
            ln(v.reciprocal(rs[:, 6, :], rs[:, 5, :]))
            own()
            ln(v.tensor_tensor(rs[:, 7, :], rs[:, 6, :], rs[:, 2, :], ALU.mult))
            ln(v.memset(RT, 0.0))
            own()
            rt = RT.rearrange("p (c b l) -> p c b l", c=CH, l=L)
            for c in range(CH):
                ln(v.tensor_scalar(rt[:, c, :, 1:L], rt[:, c, :, 1:L], t[4][:, c:c + 1], None, ALU.add))
            own()
            cbl = lambda a_: a_.rearrange("p (c b l) -> p c b l", c=CH, l=L)
            tab = lambda a_: a_.rearrange("p c (a l) -> p c a l", a=1).to_broadcast([P, CH, SB, L])
            for slot in range(STEPS + R_LAG):
                iN, iS, iR = (step_of(slot, lag) for lag in (N_LAG, S_LAG, R_LAG))
                if iR is not None:
                    dve.wait_ge(p_y3, iR + 1)
                    hh = H[:, TS * iR:TS * (iR + 1), :].rearrange("p t d -> p (t d)")
                    ln(v.tensor_tensor(hh, hh, banks(2), ALU.add))
                    own()
                    norm_stats(SR, lambda t_: H[:, TS * iR + t_, :])
                    ask_rstd(SR)
                if iN is not None:
                    for t_ in range(TS):
                        n = TS * iN + t_
                        ln(v.scalar_tensor_tensor(H[:, n, :], EO[:, n, 0:DM], rs[:, 7, n:n + 1], H[:, n, :],
                                                  ALU.mult, ALU.add))
                    own()
                    norm_stats(SE, lambda t_: H[:, TS * iN + t_, :])
                    ask_rstd(SE)
                if iS is not None:
                    dve.wait_ge(a_x3, iS + 1)
                    wait(dve, p_y3, iS)
                    ln(v.tensor_tensor(cbl(uR), xT.rearrange("p c (b l) -> p c b l", l=L), tab(Wr[:]), ALU.mult))
                    own()
                    for c in range(CH):
                        ln(v.tensor_scalar(cbl(uR)[:, c, :, 0], cbl(uR)[:, c, :, 0], t[18][:, c:c + 1], None, ALU.add))
                    own()
                    v.tensor_tensor_scan(uR, RT, uR, 0.0, ALU.mult, ALU.add).then_inc(v_ur, 1)
                if iR is not None:
                    answered(later=0 if iN is None else 1)
                    for t_ in range(TS):
                        n = TS * iR + t_
                        r = v.tensor_scalar(X4[:, n, 0:DM], H[:, n, :], SR["mv"][:, t_, 0:1],
                                            SR["rstd"][:, t_:t_ + 1], ALU.subtract, ALU.mult)
                    r.then_inc(v_x4, 1)
                if iN is not None:
                    answered()
                    wait(dve, p_x3, iN)
                    for t_ in range(TS):
                        r = v.tensor_scalar(O[:, t_, :], H[:, TS * iN + t_, :], SE["mv"][:, t_, 0:1],
                                            SE["rstd"][:, t_:t_ + 1], ALU.subtract, ALU.mult)
                    r.then_inc(v_xc, 1)
                if iS is not None:
                    dve.wait_ge(g_ui, iS + 1)
                    for c in range(CH):
                        ln(v.tensor_scalar(cbl(uI)[:, c, :, 0], cbl(uI)[:, c, :, 0], t[19][:, c:c + 1], None, ALU.add))
                    own()
                    ln(v.tensor_tensor_scan(uI, RT, uI, 0.0, ALU.mult, ALU.add))
                    own()
                    ln(v.tensor_tensor(cbl(uI), cbl(uI), tab(ST[:, :, 0:L]), ALU.mult))
                    own()
                    dve.wait_ge(g_uc, iS + 1)
                    v.tensor_tensor(uR, uR, uI, ALU.subtract).then_inc(v_yc, 1)
                if iR is not None:
                    dve.wait_ge(p_lg, iR + 1)
                    ln(v.tensor_copy(lg[:, TS * iR:TS * (iR + 1), :],
                                     bank[6][:, 0:TS * E].rearrange("p (t e) -> p t e", e=E)))

            own()
            best(lg[:], rs[:, 0, :], rs[:, 1, :], ra[:, 0], ra[:, 1], ra[:, 2])
            ln(v.scalar_tensor_tensor(ra[:, 3], ra[:, 0], -1e30, lg[:], ALU.mult, ALU.add))
            own()
            best(ra[:, 3], rs[:, 2, :], rs[:, 1, :], ra[:, 4], ra[:, 1], ra[:, 2])
            v.tensor_tensor(mask_b[:], ra[:, 0], ra[:, 4], ALU.add).then_inc(v_mask2, 1)
            v.tensor_tensor(rs[:, 3, :], rs[:, 2, :], rs[:, 0, :], ALU.subtract).then_inc(v_ra, 1)
            queue_places(None, p_cum2, None)
            cnt = cum[:, 1, :, TILES - 1]
            ln(v.tensor_scalar(tb[:, 0, :], cnt, float(P - 1), 1.0 / P, ALU.add, ALU.mult))
            own()
            ln(v.tensor_scalar(tb[:, 0, :], tb[:, 0, :], 0.5 - 1.0 / (2 * P), MAGIC, ALU.subtract, ALU.add))
            own()
            ln(v.tensor_scalar(tb[:, 0, :], tb[:, 0, :], MAGIC, None, ALU.subtract))
            own()
            ln(v.tensor_tensor_scan(tb[:, 1, :], ones_e[:], tb[:, 0, :], 0.0, ALU.mult, ALU.add))
            own()
            ln(v.tensor_tensor(tb[:, 2, :], tb[:, 1, :], tb[:, 0, :], ALU.subtract))
            own()
            ln(v.tensor_scalar(tb[:, 3, :], tb[:, 2, :], float(P), -1.0, ALU.mult, ALU.add))
            own()
            eb = lambda a_, n_: a_.rearrange("p (a e) -> p a e", a=1).to_broadcast([P, n_, E])
            ln(v.tensor_tensor(ra[:, 7], ra[:, 7], eb(tb[:, 3, :], TILES), ALU.add))
            own()
            for k, oh in enumerate((ra[:, 0], ra[:, 4])):
                ln(v.tensor_tensor(ra[:, 5 + k], ra[:, 7], oh, ALU.mult))
            own()
            for k in range(2):
                ln(v.tensor_reduce(rs[:, 5 + k, :], ra[:, 5 + k], AX, ALU.add))
            own()
            place, tile_of, row_of = (slot_of[:, n] for n in range(3))
            ln(v.tensor_scalar(place, rs[:, 5:7, :], (P - 1) / 2, 1.0 / P, ALU.subtract, ALU.mult))
            own()
            ln(v.tensor_scalar(place, place, MAGIC, None, ALU.add))
            own()
            ln(v.tensor_scalar(tile_of, place, MAGIC, None, ALU.subtract))
            own()
            kt = lambda a_, n_: a_.rearrange("p k (t a) -> p k t a", a=1).to_broadcast([P, 2, TILES, n_])
            v.tensor_tensor(in_slot, kt(tile_of, SLOTS),
                            slot_no[:].rearrange("p (k t s) -> p k t s", k=1, t=1).to_broadcast([P, 2, TILES, SLOTS]),
                            ALU.is_equal).then_inc(v_hot, 1)
            ln(v.scalar_tensor_tensor(row_of, tile_of, -float(P), rs[:, 5:7, :], ALU.mult, ALU.add))
            own()
            for k in range(2):
                v.tensor_tensor(in_row[:, k], kt(row_of, P)[:, k],
                                row_no[:].rearrange("p (t s) -> p t s", t=1).to_broadcast([P, TILES, P]),
                                ALU.is_equal).then_inc(v_row, 1)
            ln(v.tensor_tensor(cmp, eb(tb[:, 1, :], SLOTS),
                               slot_no[:].rearrange("p (s a) -> p s a", a=1).to_broadcast([P, SLOTS, E]), ALU.is_le))
            own()
            ln(v.tensor_reduce(exf[:], cmp, AX, ALU.add))
            own()
            v.tensor_scalar(exi[:], exf[:], float(E - 1), None, ALU.min).then_inc(v_exp_no, 1)
            dve.wait_ge(p_tab, 1)
            tile1, row = (bank[5 - n][:, 0:SLOTS] for n in range(2))
            f = [src_f[:, n, :] for n in range(4)]
            ln(v.tensor_scalar(f[0], tile1, float(P), -float(P), ALU.mult, ALU.add))
            ln(v.tensor_scalar(f[1], tile1, TILES + 0.5, -float(NTOK), ALU.is_gt, ALU.mult))
            ln(v.scalar_tensor_tensor(f[2], tile1, 0.5, unread[:], ALU.is_lt, ALU.mult))
            own()
            ln(v.tensor_tensor(f[0], f[0], row, ALU.add))
            own()
            ln(v.tensor_tensor(f[1], f[1], f[0], ALU.add))
            ln(v.tensor_tensor(f[2], f[2], f[0], ALU.add))
            own()
            ln(v.tensor_scalar(src_i[:], f[1], 0.0, None, ALU.max))
            ln(v.tensor_copy(dst_i[:], f[2]))
            own()
            v.engine_nop().then_inc(v_src, 1)
            dve.wait_ge(a_lg, 1)
            ln(v.tensor_scalar(rs[:, 7, :], rs[:, 4, :], 1.0, None, ALU.add))
            own()
            ln(v.reciprocal(rs[:, 8, :], rs[:, 7, :]))
            own()
            ln(v.tensor_tensor(rs[:, 9, :], rs[:, 8, :], rs[:, 4, :], ALU.mult))
            own()

            def slot_gate(j, u):
                dve.wait_ge(a_sil, j + 1)
                dve.wait_ge(p_up_g, j + 1)
                v.tensor_tensor(sil[:, u, :], sil[:, u, :], bank[3], ALU.mult).then_inc(v_act, 1)

            slot_gate(0, 0)
            with dve.Fori(0, (SLOTS - 1) // 2) as t_:
                slot_gate(2 * t_ + 1, 1)
                slot_gate(2 * t_ + 2, 0)
            for n in range(TILES):
                dve.wait_ge(d_back[n // TS], 32)
                ln(v.scalar_tensor_tensor(H[:, n, :], back[0][:, n, :], rs[:, 8, n:n + 1], H[:, n, :], ALU.mult, ALU.add))
                own()
                v.scalar_tensor_tensor(H[:, n, :], back[1][:, n, :], rs[:, 9, n:n + 1], H[:, n, :], ALU.mult, ALU.add
                                       ).then_inc(v_hfin, 1)

        @block.tensor
        def _(pe):
            mm = nc.tensor.matmul
            tr = nc.tensor.transpose
            def layer1(i, c):
                if c == 0:
                    if i == 0:
                        pe.wait_ge(d_w1, 32)
                    pe.wait_ge(a_pad, i + 1)
                    pe.wait_ge((d_x0, d_x1)[i % 2], 32 * (i // 2 + 1))
                wait(pe, a_h1, CH * (i - 1) + c + 1)
                wait(pe, v_sub, BT * done(i - 1, C_LAG))
                wait(pe, a_x2, done(i - 1, D_LAG))
                for r in range(STRIDE):
                    last = mm(bank[c], W1s[:, r, P * c:P * (c + 1)],
                              xin[:, i % 2].rearrange("p b (l s) -> p b l s", s=STRIDE)[:, :, :, r],
                              start=(r == 0), stop=(r == STRIDE - 1))
                last.then_inc(p_l1, 1)

            def layer2(i, slot):
                pe.wait_ge(a_h1, CH * (i + 1))
                if i == 0:
                    pe.wait_ge(d_w2, 16)
                    pe.wait_ge(v_wt, 1)
                wait(pe, v_h, TS * i)
                wait(pe, v_eo, TS * done(slot - 1, D_LAG))
                for t in range(TS):
                    for c in range(CH):
                        last = mm(bank[6 + t // 2][:, DM * (t % 2):DM * (t % 2 + 1)], h1T[:, c, P * t:P * (t + 1)],
                                  W2s[:, c, :], start=(c == 0), stop=(c == CH - 1))
                    last.then_inc(p_l2, 1)

            def scores(i, slot, batches):
                pe.wait_ge(v_qk, i + 1)
                pe.wait_ge(a_h1, CH * done(slot, A_LAG))
                wait(pe, a_x2, done(slot - 1, D_LAG))
                for b in batches:
                    wait(pe, v_sub, BT * i + b - 1)
                    for n in range(DBLK):
                        for t in range(TS):
                            last = mm(bank[b % 2][32 * t:32 * t + 32, 64 * n:64 * n + 64],
                                      QT[32 * b:32 * b + 32, t, n, :], KT[32 * b:32 * b + 32, t, n, :],
                                      start=True, stop=True)
                    last.then_inc(p_s, 1)

            def values(i, slot, batches):
                pe.wait_ge(d_vp, 16 * BT * TS * (i + 1))
                wait(pe, a_qkv, TS * done(slot, B_LAG))
                for b in batches:
                    pe.wait_ge(v_pt, BT * i + b + 1)
                    for h in range(NH):
                        w = TS * VW
                        last = mm(bank[2 + h // 4][32 * b:32 * b + 32, w * (h % 4):w * (h % 4 + 1)],
                                  PT[:, b % 2, h, :], Vx[:, b, :, h, :], start=True, stop=True)
                    last.then_inc(p_pv, 1)

            for slot in range(SLOTS_OF_STEPS):
                iA, iB, iC, iD = (step_of(slot, lag) for lag in (A_LAG, B_LAG, C_LAG, D_LAG))
                if iA is not None:
                    layer1(iA, 0)
                elif iC is not None:
                    scores(iC, slot, range(0, 2))
                if iA == 0:
                    pe.wait_ge(g_const, 21)
                    pe.wait_ge(v_wabs, 1)
                    mm(bank[6][:, 0:4], ones[:], wsum[:], start=True, stop=True).then_inc(p_wsum, 1)
                if iD is not None:
                    pe.wait_ge(v_ob, iD + 1)
                    pe.wait_ge(v_o, done(slot - 1, C_LAG))
                    mm(bank[3][:, 0:2 * TS], batch_mean[:], SD["bs"][:].rearrange("p a t -> p (a t)"),
                       start=True, stop=True).then_inc(p_ob, 1)
                if iB is not None:
                    pe.wait_ge(v_y, iB + 1)
                    wait(pe, v_o, done(slot - 1, C_LAG))
                    mm(bank[2][:, 0:TS], batch_mean[:], SB1["bs"][:, 0, :], start=True, stop=True).then_inc(p_bv, 1)
                if iA is not None:
                    layer1(iA, 1)
                if iA == 0:
                    pe.wait_ge(v_wt, 1)
                    for c in range(CH):
                        for w in range(4):
                            for o in range(CH):
                                last = tr(bank[4 + c].bitcast(BF16)[:, DM * w + P * o:DM * w + P * (o + 1)],
                                          wter[:, w, o, P * c:P * (c + 1)], ident_b[:])
                        last.then_inc(p_wt, 1)
                if iA is not None:
                    layer2(iA, slot)
                    if iC is not None:
                        scores(iC, slot, range(0, 2))
                if iD is not None:
                    pe.wait_ge(v_oq, iD + 1)
                    for c in range(CH):
                        for t in range(TS):
                            last = tr(bank[3].bitcast(BF16)[:, SN * c + P * t:SN * c + P * (t + 1)],
                                      oq[:, t, P * c:P * (c + 1)], ident_b[:])
                    last.then_inc(p_ot, 1)
                if iB is not None:
                    pe.wait_ge(v_xq, iB + 1)
                    for c in range(CH):
                        for t in range(TS):
                            last = tr(bank[4].bitcast(BF16)[:, SN * c + P * t:SN * c + P * (t + 1)],
                                      xq[:, t, P * c:P * (c + 1)], ident_b[:])
                    last.then_inc(p_xt, 1)
                if iD is not None:
                    pe.wait_ge(a_ot, iD + 1)
                    wait(pe, v_h, TS * done(slot, A_LAG))
                    wait(pe, v_eo, TS * done(slot - 1, D_LAG))
                    for t in range(TS):
                        for c in range(CH):
                            last = mm(bank[6 + t // 2][:, DM * (t % 2):DM * (t % 2 + 1)], oqT[:, c, P * t:P * (t + 1)],
                                      WT[:, c, 3, :], start=(c == 0), stop=(c == CH - 1))
                        last.then_inc(p_o, 1)
                if iB is not None:
                    if iB == 0:
                        pe.wait_ge(a_wt, CH)
                    pe.wait_ge(a_xt, iB + 1)
                    wait(pe, a_ot, done(slot, D_LAG))
                    pe.wait_ge(v_xq, iB + 1)
                    for t in range(TS):
                        wait(pe, a_qkv, TS * iB + t - 1)
                        for c in range(CH):
                            mm(bank[(3, 5)[t % 2]], xqT[:, c, P * t:P * (t + 1)],
                               WT[:, c, 0:2, :].rearrange("p w d -> p (w d)"), start=(c == 0), stop=(c == CH - 1))
                        for c in range(CH):
                            last = mm(bank[(2, 4)[t % 2]][:, 0:DM], xqT[:, c, P * t:P * (t + 1)],
                                      WT[:, c, 2, :], start=(c == 0), stop=(c == CH - 1))
                        last.then_inc(p_qkv, 1)
                if iC is not None:
                    scores(iC, slot, range(2, BT))
                if iC is not None:
                    values(iC, slot, range(0, 2))
                if iD is not None:
                    pe.wait_ge(v_x2, iD + 1)
                    wait(pe, v_sub, BT * done(slot, C_LAG))
                    for c in range(CH):
                        for t in range(TS):
                            last = tr(bank[c][:, P * t:P * (t + 1)], O[:, t, P * c:P * (c + 1)], ident[:])
                    last.then_inc(p_x2, 1)
                if iC is not None:
                    values(iC, slot, range(2, BT))
                if iD is not None:
                    pe.wait_ge(a_x2, iD + 1)
                    if iD == 0:
                        pe.wait_ge(d_we, 48)
                    pe.wait_ge(v_hd, iD + 1)
                    for t in range(TS):
                        wait(pe, v_eo, TS * iD + t - 1)
                        for c in range(CH):
                            last = mm(bank[6 + t % 2][:, 0:DE], xT[:, c, P * t:P * (t + 1)], WE[:, c, :],
                                      start=(c == 0), stop=(c == CH - 1))
                        last.then_inc(p_e, 1)

            def places(ready, signal):
                pe.wait_ge(ready, 1)
                mk = mask_b[:].rearrange("p t e -> p (t e)")
                mm(bank[6][:, 0:TILES * E], tri_b[:], mk, start=True, stop=True)
                mm(bank[7][:, 0:TILES * E], ones_b[:], mk, start=True, stop=True).then_inc(signal, 1)

            pe.wait_ge(v_eo, TILES)
            places(v_mask, p_cum)
            for slot in range(STEPS + R_LAG):
                iN, iS, iR = (step_of(slot, lag) for lag in (N_LAG, S_LAG, R_LAG))
                if iR is not None:
                    pe.wait_ge(v_x4, iR + 1)
                    for c in range(CH):
                        for t in range(TS):
                            last = tr(bank[4 + c][:, P * t:P * (t + 1)], X4[:, TS * iR + t, P * c:P * (c + 1)], ident[:])
                    last.then_inc(p_x4, 1)
                if iN is not None:
                    pe.wait_ge(v_xc, iN + 1)
                    wait(pe, a_x3, iN)
                    for c in range(CH):
                        for t in range(TS):
                            last = tr(bank[c][:, P * t:P * (t + 1)], O[:, t, P * c:P * (c + 1)], ident[:])
                    last.then_inc(p_x3, 1)
                if iR is not None:
                    pe.wait_ge(a_x4, iR + 1)
                    for t in range(TS):
                        for c in range(CH):
                            last = mm(bank[6][:, E * t:E * (t + 1)], x4T[:, c, P * t:P * (t + 1)], Wgs[:, c, :],
                                      start=(c == 0), stop=(c == CH - 1))
                    last.then_inc(p_lg, 1)
                if iS is not None:
                    pe.wait_ge(v_yc, iS + 1)
                    for t in range(TS):
                        for c in range(CH):
                            last = tr(banks(2)[:, DM * t + P * c:DM * t + P * (c + 1)],
                                      uR[:, SN * c + P * t:SN * c + P * (t + 1)], ident[:])
                    last.then_inc(p_y3, 1)
            places(v_mask2, p_cum2)
            pe.wait_ge(g_tile, 1)
            pe.wait_ge(a_part, 1)
            for k in range(2):
                pe.wait_ge(v_row, k + 1)
                for t in range(TILES):
                    for n, what in enumerate((in_tile, in_part)):
                        last = mm(bank[5 - n][:, 0:SLOTS], in_row[:, k, t, :], what[:, k, t, :],
                                  start=(k == 0 and t == 0), stop=(k == 1 and t == TILES - 1))
            last.then_inc(p_tab, 1)
            pe.wait_ge(v_exp_no, 1)
            pe.wait_ge(d_moe, 32)
            pe.wait_ge(d_m3, 16)
            slot_in = (d_slot0, d_slot1)

            def slot_rows(j, u, loads):
                pe.wait_ge(slot_in[u], loads)
                for c in range(CH):
                    last = tr(bank[u][:, P * c:P * (c + 1)], xrow[:, u, P * c:P * (c + 1)], ident[:])
                last.then_inc(p_xr, 1)

            def slot_up(j, u):
                e = pe.value_load(exi[0:1, bass.ds(j, 1)], min_val=0, max_val=E - 1)
                pe.wait_ge(a_xr, j + 1)
                for w, z, signal in ((M1s, bank[2], p_up_h), (M2s, bank[3], p_up_g)):
                    for c in range(CH):
                        last = mm(z, xrT[:, u, c, :], w[:, bass.ds(e, 1), c, :].rearrange("p a h -> p (a h)"),
                                  start=(c == 0), stop=(c == CH - 1))
                    last.then_inc(signal, 1)

            def slot_act(j, u):
                pe.wait_ge(v_act, j + 1)
                for c in range(HC):
                    last = tr(bank[4 + u][:, P * c:P * (c + 1)], sil[:, u, P * c:P * (c + 1)], ident[:])
                last.then_inc(p_at, 1)

            def slot_down(j, u):
                e = pe.value_load(exi[0:1, bass.ds(j, 1)], min_val=0, max_val=E - 1)
                pe.wait_ge(a_at, j + 1)
                if not (isinstance(j, int) and j < 2):
                    pe.wait_ge(a_y, j - 1)
                for c in range(HC):
                    last = mm(bank[6 + u][:, 0:DM], actT[:, u, c, :],
                              M3s[:, bass.ds(e, 1), c, :].rearrange("p a d -> p (a d)"),
                              start=(c == 0), stop=(c == HC - 1))
                last.then_inc(p_dn, 1)

            def slot_step(j, u, loads):
                slot_act(j, u)
                if not isinstance(j, int) or j + 2 < SLOTS:
                    slot_rows(j + 2, u, loads)
                if not isinstance(j, int) or j + 1 < SLOTS:
                    slot_up(j + 1, 1 - u)
                slot_down(j, u)

            slot_rows(0, 0, 16)
            slot_rows(1, 1, 16)
            slot_up(0, 0)
            for j in range(PEEL):
                slot_step(j, j % 2, 16 * ((j + 2) // 2 + 1))
            with pe.Fori(0, (SLOTS - 2 - PEEL) // 2) as t:
                slot_step(2 * t + PEEL, 1, 16 * t + 48)
                slot_step(2 * t + PEEL + 1, 0, 16 * t + 64)
            for j in range(SLOTS - 2, SLOTS):
                slot_step(j, j % 2, None)


_INS = ['x', 'L0_tok_W1', 'L0_tok_b1', 'L0_tok_W2', 'L0_tok_b2', 'L0_attn_w_q', 'L0_attn_w_k', 'L0_attn_w_v',
        'L0_attn_w_o', 'L0_ffn_w_gate', 'L0_ffn_w_expert', 'L0_ffn_b_expert', 'L1_attn_phazor_real',
        'L1_attn_phazor_imag', 'L1_attn_phazor_init_real', 'L1_attn_phazor_init_imag', 'L1_attn_last_conv_real',
        'L1_attn_last_conv_imag', 'L1_ffn_Wg', 'L1_ffn_W1', 'L1_ffn_W2', 'L1_ffn_W3']
_OUTS = [((64, 32, 256), 'float32')]


def kernel(**inputs):
    import numpy as _np
    import concourse.bacc as _bacc
    from concourse import mybir as _mybir
    from concourse.bass_utils import run_bass_kernel_spmd as _run

    nc = _bacc.Bacc("TRN2", target_bir_lowering=False, num_devices=1)
    arrays, args = {}, []
    for name in _INS:
        a = _np.ascontiguousarray(inputs[name])
        arrays[f"in_{name}_dram"] = a
        args.append(nc.dram_tensor(f"in_{name}_dram", a.shape, _mybir.dt.from_np(a.dtype), kind="ExternalInput").ap())
    for i, (shape, dtype) in enumerate(_OUTS):
        dt = _mybir.dt.from_np(_np.dtype(dtype))
        args.append(nc.dram_tensor(f"out_{i}_dram", shape, dt, kind="ExternalOutput").ap())
    audio_tower_kernel(nc, *args)
    r = _run(nc, [arrays], core_ids=[0])
    got = tuple(r.results[0][f"out_{i}_dram"] for i in range(len(_OUTS)))
    return got[0]
```

```python
from contextlib import ExitStack

import concourse.bass as bass
from concourse import mybir

F32 = mybir.dt.float32
BF16 = mybir.dt.bfloat16
I32 = mybir.dt.int32
ALU = mybir.AluOpType
ACT = mybir.ActivationFunctionType
AX = mybir.AxisListType.X


def audio_tower_kernel(
    nc, x, W1, b1, W2, b2, w_q, w_k, w_v, w_o, w_gate, w_expert, b_expert,
    ph_re, ph_im, pi_re, pi_im, lc_re, lc_im, Wg, M1, M2, M3, out,
):
    P = 128
    B, V, T_IN = x.shape
    DM = W1.shape[1]
    CH = DM // P
    STRIDE = 8
    L = T_IN // STRIDE
    NTOK = B * L
    TILES = NTOK // P
    TS = 4
    STEPS = TILES // TS
    SB = B // STEPS
    SN = TS * P
    BT = P // L
    NH = 16
    HD = DM // NH
    DBLK = DM // 32
    VW = HD + 1
    E = w_gate.shape[1]
    DE = DM + E
    CAPACITY = 100
    HID = M1.shape[2]
    HC = HID // P
    EPS = 1e-5
    MAGIC = 12582912.0
    SLOTS = (2 * NTOK + E * (P - 1)) // P
    PEEL = 3
    assert L == 32 and BT == TS and HD == 16 and SLOTS % 2 == 1

    xs = nc.dram_tensor("mixture_rows_in", [NTOK, DM], F32, kind="Internal").ap()
    ys = nc.dram_tensor("mixture_rows_out", [2 * NTOK + SLOTS * P, DM], F32, kind="Internal").ap()
    out_rows = out.rearrange("b l d -> (b l) d").rearrange("(t p) d -> p t d", p=P)
    xs_tiles = xs.rearrange("(t p) d -> p t d", p=P)
    ys_tiles = ys[0:2 * NTOK, :].rearrange("(k t p) d -> p k t d", p=P, k=2)

    with ExitStack() as ctx:
        def sb(name, shape, dt=F32):
            return ctx.enter_context(nc.sbuf_tensor(name, shape, dt))

        def sem(name):
            return ctx.enter_context(nc.semaphore(name))

        def part(t, lo, n):
            a = t[:]
            if len(a.shape) > 2:
                a = a.rearrange(" ".join(["p"] + [f"d{i}" for i in range(len(a.shape) - 1)]) + " -> p ("
                                + " ".join(f"d{i}" for i in range(len(a.shape) - 1)) + ")")
            return a[:, lo:lo + n]

        ident_b = sb("ident_b", [P, P], BF16)
        ident = sb("ident", [P, P])
        ones = sb("ones", [P, P])
        ones_b = sb("ones_b", [P, P], BF16)
        tri_b = sb("tri_b", [P, P], BF16)
        batch_mean = sb("batch_mean", [P, P])
        mhalf = sb("mhalf", [P, TS])
        rank_w = sb("rank_w", [P, E])
        slot_no = sb("slot_no", [P, SLOTS])
        reset_t = sb("reset_t", [P, E, TILES])
        ones_e = sb("ones_e", [P, E])
        row_no = sb("row_no", [P, P])
        row_p = sb("row_p", [P, 1])
        tile_no = sb("tile_no", [P, 2, TILES])
        unread = sb("unread", [P, SLOTS])

        W2s = sb("W2s", [P, CH, DM])
        b1c = sb("b1c", [P, CH])
        b2r = sb("b2r", [P, DM])
        WT = sb("WT", [P, CH, 4, DM], BF16)
        WE = sb("WE", [P, CH, DE])
        bE = sb("bE", [P, DM])
        Wgs = sb("Wgs", [P, CH, E])
        M1s = sb("M1s", [P, E, CH, HID])
        M2s = sb("M2s", [P, E, CH, HID])
        M3s = sb("M3s", [P, E, HC, DM])
        wm = sb("wm", [P, 4])
        wmi = sb("wmi", [P, 4])
        wsum = sb("wsum", [P, 4])

        H = sb("H", [P, TILES, DM])
        EO = sb("EO", [P, TILES, DE])
        x1 = sb("x1", [P, TS, DM])
        xq = sb("xq", [P, TS, DM], BF16)
        xqT = sb("xqT", [P, CH, SN], BF16)
        oq = sb("oq", [P, TS, DM], BF16)
        oqT = sb("oqT", [P, CH, SN], BF16)
        qtok = sb("qtok", [P, TS, DM])
        ktok = sb("ktok", [P, 2, TS * DM])
        head_mask = sb("head_mask", [P, 2])
        head_sum = sb("head_sum", [P, P // HD])
        vtok = sb("vtok", [P, TS, NH, VW])
        QT = sb("QT", [P, TS, DBLK, 32])
        KT = sb("KT", [P, TS, DBLK, 64])
        Eb = sb("Eb", [P, 2, NH, 32])
        PT = sb("PT", [P, 2, NH, 32])
        O = sb("O", [P, TS, DM])

        X4 = EO
        W1s = part(EO, 4 * DE, STRIDE * DM).rearrange("p (r d) -> p r d", r=STRIDE)
        h1T = part(EO, 12 * DE, CH * SN).rearrange("p (c n) -> p c n", c=CH)
        xin = part(M3s, 0, 2 * SB * T_IN).rearrange("p (u b t) -> p u b t", u=2, b=SB)
        Vx = part(M1s, 0, BT * TS * NH * VW).rearrange("p (b t h n) -> p b t h n", b=BT, t=TS, h=NH)
        xT = part(x1, 0, CH * SN).rearrange("p (c n) -> p c n", c=CH)
        wraw = part(KT, 0, 4 * CH * DM).rearrange("p (w n) -> p w n", w=4)
        wter = PT[:].rearrange("p a h k -> p (a h k)").bitcast(BF16).rearrange("p (w c n) -> p w c n", w=4, c=CH)
        RT = part(qtok, 0, CH * SN)
        uR = [part(ktok, u * CH * SN, CH * SN) for u in range(2)]
        uI = [part(KT, u * CH * SN, CH * SN) for u in range(2)]
        ra = part(Eb, 0, 8 * TILES * E).rearrange("p (s t e) -> p s t e", s=8, t=TILES)
        cmp = part(PT, 0, SLOTS * E).rearrange("p (a e) -> p a e", e=E)
        in_row = part(KT, 0, TILES * P).bitcast(BF16).rearrange("p (k t m) -> p k t m", k=2, t=TILES)
        oh_w = SLOTS * 2 * TILES // 2
        in_slot, in_tile, in_part = (
            part(ktok, n * oh_w, oh_w).bitcast(BF16).rearrange("p (k t a) -> p k t a", k=2, t=TILES)
            for n in range(3))
        xrow = part(KT, 0, 2 * DM).rearrange("p (u d) -> p u d", u=2)
        xrT = part(KT, 2 * DM, 2 * DM).rearrange("p (u c n) -> p u c n", u=2, c=CH)
        actT = part(KT, 4 * DM, 2 * HID).rearrange("p (u c n) -> p u c n", u=2, c=HC)
        x4T = part(QT, 0, CH * SN).rearrange("p (c n) -> p c n", c=CH)
        sil = part(QT, 0, 2 * HID).rearrange("p (u n) -> p u n", u=2)
        yrow = part(O, 0, 2 * DM).rearrange("p (u d) -> p u d", u=2)
        back = [part(m, 0, TILES * DM).rearrange("p (t d) -> p t d", t=TILES) for m in (M1s, M2s)]

        def stats(n):
            return {k: sb(f"{k}_{n}", s) for k, s in dict(
                st=[P, TS, 6], mv=[P, TS, 2], ve=[P, TS], rstd=[P, TS], bs=[P, 2, TS], bv=[P, 2, TS], bve=[P, TS],
                rsb=[P, TS], am=[P, TS], sa=[P, TS], s=[P, TS], sw=[P, 4, TS]).items()}

        SB1, SD, SE = stats("in"), stats("att"), stats("ssm")
        SR = SB1
        mx = sb("mx", [P, 2, NH])
        rec = sb("rec", [P, TS, NH])
        vec = sb("vec", [P, 6, CH])
        sv = sb("sv", [P, 20, CH])
        CT = sb("CT", [P, CH, L + 1])
        ST = sb("ST", [P, CH, L + 1])
        Wr = sb("Wr", [P, CH, L])
        Wi = sb("Wi", [P, CH, L])
        tmpT = sb("tmpT", [P, 4, CH, L])
        lg = sb("lg", [P, TILES, E])
        rs = sb("rs", [P, 10, TILES])
        cum = sb("cum", [P, 2, E, TILES])
        mask_b = sb("mask_b", [P, TILES, E], BF16)
        slot_of = sb("slot_of", [P, 3, 2, TILES])
        src_f = sb("src_f", [P, 3, SLOTS])
        silu_ready = sb("silu_ready", [P, 1])
        src_i = sb("src_i", [P, SLOTS], I32)
        dst_i = sb("dst_i", [P, SLOTS], I32)
        tb = sb("tb", [P, 4, E])
        exf = sb("exf", [P, SLOTS])
        exi = sb("exi", [P, SLOTS], I32)

        psum = ctx.enter_context(nc.psum_tensor("psum", [P, 8, 512], F32))
        bank = [psum[:, i, :] for i in range(8)]

        def banks(i):
            return psum[:, i:i + 2, :].rearrange("p a b -> p (a b)")

        d_w1, d_x0, d_x1, d_w2, d_b, d_att = (
            sem(n) for n in "d_w1 d_x0 d_x1 d_w2 d_b d_att".split())
        d_we, d_vec, d_moe, d_m3, d_vp, d_xs = (
            sem(n) for n in "d_we d_vec d_moe d_m3 d_vp d_xs".split())
        d_out, d_fetch0, d_fetch1, d_deliver0, d_deliver1 = (
            sem(n) for n in "d_out d_fetch0 d_fetch1 d_deliver0 d_deliver1".split())
        g_const, g_pow, g_input_im, g_turned, g_embed, g_expert_bias = (
            sem(n) for n in "g_const g_pow g_input_im g_turned g_embed g_expert_bias".split())
        g_decay, g_tile = (
            sem(n) for n in "g_decay g_tile".split())
        v_chain, v_ask, v_batch_in, v_xq_rows, v_batch_att, v_oq_rows = (
            sem(n) for n in "v_chain v_ask v_batch_in v_xq_rows v_batch_att v_oq_rows".split())
        v_att_added, v_norm2, v_scales, v_qk, v_less_max, v_probsT = (
            sem(n) for n in "v_att_added v_norm2 v_scales v_qk v_less_max v_probsT".split())
        v_att_rows, v_abs_sum, v_ternary, v_state_re, v_ssm_out, v_mask = (
            sem(n) for n in "v_att_rows v_abs_sum v_ternary v_state_re v_ssm_out v_mask".split())
        v_mask2, v_slot_expert, v_exp, v_gated, v_gate_in, v_final = (
            sem(n) for n in "v_mask2 v_slot_expert v_exp v_gated v_gate_in v_final".split())
        v_logit_gap, v_norm_in, v_state_im, v_hot, v_row, v_src = (
            sem(n) for n in "v_logit_gap v_norm_in v_state_im v_hot v_row v_src".split())
        p_abs_sum, p_ternaryT, p_layer1, p_layer2, p_batch_in, p_xqT = (
            sem(n) for n in "p_abs_sum p_ternaryT p_layer1 p_layer2 p_batch_in p_xqT".split())
        p_qkv, p_scores, p_values, p_batch_att, p_oqT, p_proj = (
            sem(n) for n in "p_qkv p_scores p_values p_batch_att p_oqT p_proj".split())
        p_norm2T, p_expert, p_places, p_places2, p_norm3T, p_ssm_rows = (
            sem(n) for n in "p_norm2T p_expert p_places p_places2 p_norm3T p_ssm_rows".split())
        p_norm4T, p_logits, p_slotT, p_up_h, p_up_g, p_actT = (
            sem(n) for n in "p_norm4T p_logits p_slotT p_up_h p_up_g p_actT".split())
        p_down, p_table = (
            sem(n) for n in "p_down p_table".split())
        a_norm3, a_norm4, a_ternaryT, a_pad, a_hidden, a_xqT = (
            sem(n) for n in "a_norm3 a_norm4 a_ternaryT a_pad a_hidden a_xqT".split())
        a_qkv, a_exp, a_oqT, a_norm2T, a_norm3T, a_norm4T = (
            sem(n) for n in "a_qkv a_exp a_oqT a_norm2T a_norm3T a_norm4T".split())
        a_pair_gate, a_gate, a_decay, a_slotT, a_silu, a_actT = (
            sem(n) for n in "a_pair_gate a_gate a_decay a_slotT a_silu a_actT".split())
        a_slot_out, a_embed, a_expert, a_k_masked, a_part = (
            sem(n) for n in "a_slot_out a_embed a_expert a_k_masked a_part".split())

        d_back = [sem(f"d_back{t}") for t in range(STEPS)]

        block = ctx.enter_context(nc.Block())

        def wait(eng, s, n):
            if n > 0:
                eng.wait_ge(s, n)

        def done(slot, lag):
            return max(0, min(STEPS, slot - lag + 1))

        def step_of(slot, lag):
            i = slot - lag
            return i if 0 <= i < STEPS else None

        A_LAG, B_LAG, C_LAG, D_LAG = 0, 1, 2, 3
        SLOTS_OF_STEPS = STEPS + D_LAG
        N_LAG, S_LAG, R_LAG, L_LAG = 0, 1, 2, 3

        @block.sync
        def _(sp):
            w1_v = W1.rearrange("(v s r) d -> s v r d", s=2, r=STRIDE)
            xv = x.rearrange("b v t -> v b t")

            def load_x(i):
                s_x = (d_x0, d_x1)[i % 2]
                sp.dma_start(xin[0:64, i % 2], xv[:, SB * i:SB * (i + 1), :]).then_inc(s_x, 16)
                sp.dma_start(xin[64:128, i % 2, :, 0:T_IN - STRIDE],
                             xv[:, SB * i:SB * (i + 1), STRIDE:T_IN]).then_inc(s_x, 16)

            for s in range(2):
                sp.dma_start(W1s[64 * s:64 * s + 64], w1_v[s]).then_inc(d_w1, 16)
            load_x(0)
            for n, w in enumerate((w_q, w_k, w_v, w_o)):
                sp.dma_start(wraw[:, n, :].rearrange("p (c i) -> p c i", c=CH),
                             w.rearrange("(c p) i -> p c i", p=P)).then_inc(d_att, 16)
            sp.dma_start(W2s[:], W2.rearrange("(c p) d -> p c d", p=P)).then_inc(d_w2, 16)
            load_x(1)
            sp.dma_start(WE[:, :, 0:DM], w_expert.rearrange("(c p) d -> p c d", p=P)).then_inc(d_we, 16)
            sp.dma_start(WE[:, :, DM:], w_gate.rearrange("(c p) d -> p c d", p=P)).then_inc(d_we, 16)
            sp.dma_start(Wgs[:], Wg.rearrange("(c p) d -> p c d", p=P)).then_inc(d_we, 16)
            for i in range(2, STEPS):
                sp.wait_ge(p_layer1, CH * (i - 1))
                load_x(i)
            sp.wait_ge(g_const, 20)
            for i in range(STEPS):
                sp.wait_ge(a_qkv, TS * (i + 1))
                if i > 0:
                    sp.wait_ge(p_values, BT * i)
                for b in range(BT):
                    for t in range(TS):
                        sp.dma_start(Vx[32 * t:32 * t + 32, b, t].rearrange("k h n -> k (h n)"),
                                     vtok[32 * b:32 * b + 32, t].rearrange("k h n -> k (h n)")).then_inc(d_vp, 16)
                if i == 1:
                    sp.dma_start(M2s[:], M2.rearrange("e (c p) h -> p e c h", p=P)).then_inc(d_moe, 16)
            sp.wait_ge(p_values, BT * STEPS)
            sp.dma_start(M1s[:], M1.rearrange("e (c p) h -> p e c h", p=P)).then_inc(d_moe, 16)
            sp.wait_ge(p_layer1, CH * STEPS)
            sp.dma_start(M3s[:], M3.rearrange("e (c p) d -> p e c d", p=P)).then_inc(d_m3, 16)
            for i in range(STEPS):
                sp.wait_ge(a_norm4, TS * (i + 1))
                sp.dma_start(xs_tiles[:, TS * i:TS * (i + 1), :], X4[:, TS * i:TS * (i + 1), 0:DM]).then_inc(d_xs, 16)
            sp.wait_ge(d_deliver0, 16 * ((SLOTS + 1) // 2))
            sp.wait_ge(d_deliver1, 16 * (SLOTS // 2))
            sp.wait_ge(p_down, SLOTS)
            for i in range(STEPS):
                for k in range(2):
                    sp.dma_start(back[k][:, TS * i:TS * (i + 1), :], ys_tiles[:, k, TS * i:TS * (i + 1), :]
                                 ).then_inc(d_back[i], 16)
            for t in range(TILES):
                sp.wait_ge(v_final, t + 1)
                sp.dma_start(out_rows[:, t, :], H[:, t, :]).then_inc(d_out, 16)
            sp.wait_ge(d_out, 16 * TILES)

        @block.gpsimd
        def _(pool):
            gp = nc.gpsimd
            gp.iota(row_no[:], pattern=[[1, P]], base=0, channel_multiplier=0,
                    allow_small_or_imprecise_dtypes=True).then_inc(g_const, 1)
            for t, v in ((ident_b, 0.0), (ident, 0.0), (tri_b, 1.0), (batch_mean, 1.0 / L), (ones_e, 1.0),
                         (ones, 1.0), (ones_b, 1.0), (mhalf, -0.5), (reset_t, 1.0)):
                gp.memset(t[:], v).then_inc(g_const, 1)
            gp.iota(rank_w[:], pattern=[[-1, E]], base=E, channel_multiplier=0,
                    allow_small_or_imprecise_dtypes=True).then_inc(g_const, 1)
            gp.iota(slot_no[:], pattern=[[1, SLOTS]], base=0, channel_multiplier=0,
                    allow_small_or_imprecise_dtypes=True).then_inc(g_const, 1)
            pool.wait_ge(g_const, 12)
            for t in (ident_b, ident):
                gp.affine_select(out=t[:], in_=t[:], compare_op=ALU.not_equal, fill=1.0, base=0,
                                 pattern=[[-1, P]], channel_multiplier=1).then_inc(g_const, 1)
            gp.affine_select(out=tri_b[:], in_=tri_b[:], compare_op=ALU.is_ge, fill=0.0, base=0,
                             pattern=[[1, P]], channel_multiplier=-1).then_inc(g_const, 1)
            bm = batch_mean[:].rearrange("p (a b) -> p a b", b=L)
            gp.affine_select(out=bm, in_=bm, compare_op=ALU.is_ge, fill=0.0, base=0,
                             pattern=[[-L, BT], [0, L]], channel_multiplier=1).then_inc(g_const, 1)
            pool.wait_ge(g_const, 16)
            gp.affine_select(out=bm, in_=bm, compare_op=ALU.is_ge, fill=0.0, base=L - 1,
                             pattern=[[L, BT], [0, L]], channel_multiplier=-1).then_inc(g_const, 1)
            gp.memset(reset_t[:, :, 0:1], 0.0).then_inc(g_const, 1)
            gp.memset(vtok[:], 1.0).then_inc(g_const, 1)
            gp.memset(Vx, 0.0).then_inc(g_const, 1)
            gp.iota(row_p[:], pattern=[[0, 1]], base=0, channel_multiplier=1,
                    allow_small_or_imprecise_dtypes=True).then_inc(g_const, 1)
            gp.iota(tile_no[:], pattern=[[TILES, 2], [1, TILES]], base=1, channel_multiplier=0,
                    allow_small_or_imprecise_dtypes=True).then_inc(g_const, 1)
            gp.iota(unread[:], pattern=[[P, SLOTS]], base=2 * NTOK + P, channel_multiplier=1,
                    allow_small_or_imprecise_dtypes=True).then_inc(g_const, 1)

            asked = [0]

            def power(dst, src):
                asked[0] += 1
                pool.wait_ge(v_ask, asked[0])
                gp.tensor_tensor(dst, src, mhalf[:, 0:src.shape[-1]], ALU.pow).then_inc(g_pow, 1)

            power(sv[:, 3, :], sv[:, 2, :])
            def expert_bias(i):
                pool.wait_ge(a_expert, TS * (i + 1))
                rows = EO[:, TS * i:TS * (i + 1), 0:DM]
                gp.tensor_tensor(rows, rows, bE[:].rearrange("p (t d) -> p t d", t=1).to_broadcast([P, TS, DM]),
                                 ALU.add).then_inc(g_expert_bias, 1)

            for slot in range(SLOTS_OF_STEPS):
                iA, iB, iC, iD = (step_of(slot, lag) for lag in (A_LAG, B_LAG, C_LAG, D_LAG))
                if iB is not None:
                    power(SB1["rstd"][:], SB1["ve"][:])
                if iD is not None:
                    power(SD["rsb"][:], SD["bve"][:])
                if iB is not None:
                    power(SB1["rsb"][:], SB1["bve"][:])
                if iA is not None:
                    pool.wait_ge(a_embed, iA + 1)
                    rows = H[:, TS * iA:TS * (iA + 1), :]
                    gp.tensor_tensor(rows, rows, b2r[:].rearrange("p (t d) -> p t d", t=1).to_broadcast([P, TS, DM]),
                                     ALU.add).then_inc(g_embed, 1)
                if iD is not None:
                    power(SD["rstd"][:], SD["ve"][:])
                if slot > D_LAG:
                    expert_bias(slot - 1 - D_LAG)
                if slot == STEPS + B_LAG:
                    pool.wait_ge(v_qk, STEPS)
                    pool.wait_ge(a_decay, 1)
                    gp.memset(RT, 0.0).then_inc(g_decay, 1)
                    pool.wait_ge(g_decay, 1)
                    rt = RT.rearrange("p (c b l) -> p c b l", c=CH, l=L)
                    for c in range(CH):
                        gp.tensor_scalar(rt[:, c, :, 1:L], rt[:, c, :, 1:L], sv[:, 4, c:c + 1], None, ALU.add
                                         ).then_inc(g_decay, 1)

            expert_bias(STEPS - 1)
            def cbl(u):
                return u.rearrange("p (c b l) -> p c b l", c=CH, l=L)

            def table(a):
                return a.rearrange("p c (a l) -> p c a l", a=1).to_broadcast([P, CH, SB, L])

            for slot in range(STEPS + R_LAG):
                iN, iS, iR = (step_of(slot, lag) for lag in (N_LAG, S_LAG, R_LAG))
                if iN is not None:
                    wait(pool, a_norm3, TS * iN)
                    power(SE["rstd"][:], SE["ve"][:])
                if iS is not None:
                    uRs, uIs = uR[iS % 2], uI[iS % 2]
                    pool.wait_ge(a_norm3T, iS + 1)
                    wait(pool, v_ssm_out, iS - 1)
                    gp.tensor_tensor(cbl(uIs), xT.rearrange("p c (b l) -> p c b l", l=L), table(Wi[:]), ALU.mult
                                     ).then_inc(g_input_im, 1)
                    pool.wait_ge(v_state_re, iS + 1)
                    gp.tensor_tensor(cbl(uRs), cbl(uRs), table(CT[:, :, 0:L]), ALU.mult).then_inc(g_turned, 1)
                if iR is not None:
                    wait(pool, a_norm4, TS * iR)
                    power(SR["rstd"][:], SR["ve"][:])
                if iS is not None:
                    pool.wait_ge(v_state_im, iS + 1)
                    gp.tensor_tensor(cbl(uIs), cbl(uIs), table(ST[:, :, 0:L]), ALU.mult).then_inc(g_turned, 1)
            pool.wait_ge(v_hot, 1)
            gp.tensor_tensor(in_tile, in_slot,
                             tile_no[:].rearrange("p k (t a) -> p k t a", a=1).to_broadcast([P, 2, TILES, SLOTS]),
                             ALU.mult).then_inc(g_tile, 1)
            pool.wait_ge(d_xs, 16 * STEPS)
            pool.wait_ge(v_src, 1)

            def fetch(j):
                wait(pool, p_slotT, j - 1)
                gp.indirect_dma_start(xrow[:, j % 2, :], None, xs,
                                      bass.IndirectOffsetOnAxis(ap=src_i[:, j:j + 1], axis=0)
                                      ).then_inc((d_fetch0, d_fetch1)[j % 2], 16)

            def deliver(j):
                pool.wait_ge(a_slot_out, j + 1)
                gp.indirect_dma_start(ys, bass.IndirectOffsetOnAxis(ap=dst_i[:, j:j + 1], axis=0),
                                      yrow[:, j % 2, :], None).then_inc((d_deliver0, d_deliver1)[j % 2], 16)

            for j in range(3):
                fetch(j)
            for j in range(SLOTS):
                if j + 3 < SLOTS:
                    fetch(j + 3)
                deliver(j)

        @block.scalar
        def _(act):
            a = nc.scalar
            def pad(i):
                act.wait_ge((d_x0, d_x1)[i % 2], 32 * (i // 2 + 1))
                a.activation(xin[64:128, i % 2, :, T_IN - STRIDE:T_IN],
                             xin[64:128, i % 2, :, T_IN - STRIDE - 1:T_IN - STRIDE].to_broadcast([64, SB, STRIDE]),
                             ACT.Copy).then_inc(a_pad, 1)

            for n, v in enumerate((ph_re, ph_im, pi_re, pi_im, lc_re, lc_im)):
                act.dma_start(vec[:, n, :], v.rearrange("(c p) -> p c", p=P),
                              allow_slow_non_contiguous=True).then_inc(d_vec, 16)
            act.dma_start(b1c[:], b1.rearrange("(c p) -> p c", p=P), allow_slow_non_contiguous=True).then_inc(d_b, 16)
            act.dma_start(b2r[:], b2.partition_broadcast(P)).then_inc(d_b, 16)
            act.dma_start(bE[:], b_expert.partition_broadcast(P)).then_inc(d_b, 16)
            pad(0)
            act.wait_ge(v_exp, 1)
            a.activation(sv[:, 4, :], sv[:, 5, :], ACT.Exp, scale=-1.0).then_inc(a_decay, 1)
            for c in range(CH):
                act.wait_ge(p_ternaryT, c + 1)
                a.activation(WT[:, c].rearrange("p w d -> p (w d)"), bank[4 + c].bitcast(BF16), ACT.Copy
                             ).then_inc(a_ternaryT, 1)
            act.wait_ge(d_b, 48)

            def exps(i, batches):
                for b in batches:
                    act.wait_ge(v_less_max, BT * i + b + 1)
                    a.activation(Eb[:, b % 2], Eb[:, b % 2], ACT.Exp).then_inc(a_exp, 1)

            for slot in range(SLOTS_OF_STEPS):
                iA, iB, iC, iD = (step_of(slot, lag) for lag in (A_LAG, B_LAG, C_LAG, D_LAG))
                if iA is not None:
                    for c in range(CH):
                        act.wait_ge(p_layer1, CH * iA + c + 1)
                        wait(act, p_layer2, TS * iA)
                        a.activation(h1T[:, c, :], bank[c], ACT.Relu, bias=b1c[:, c:c + 1]).then_inc(a_hidden, 1)
                    if iA + 1 < STEPS:
                        pad(iA + 1)
                if iA is not None:
                    for k in range(2):
                        act.wait_ge(p_layer2, TS * iA + 2 * (k + 1))
                        r = a.activation(H[:, TS * iA + 2 * k:TS * iA + 2 * k + 2, :].rearrange("p t d -> p (t d)"),
                                         bank[6 + k], ACT.Copy)
                    r.then_inc(a_embed, 1)
                if iD is not None:
                    act.wait_ge(p_oqT, iD + 1)
                    wait(act, p_proj, TS * iD)
                    a.activation(oqT[:].rearrange("p c n -> p (c n)"), bank[3].bitcast(BF16), ACT.Copy).then_inc(a_oqT, 1)
                if iB is not None:
                    act.wait_ge(p_xqT, iB + 1)
                    wait(act, p_qkv, TS * iB)
                    a.activation(xqT[:].rearrange("p c n -> p (c n)"), bank[4].bitcast(BF16), ACT.Copy).then_inc(a_xqT, 1)
                if iC is not None:
                    exps(iC, range(0, 2))
                if iB is not None:
                    act.wait_ge(v_scales, iB + 1)
                    wait(act, v_qk, iB)
                    wait(act, d_vp, 16 * BT * TS * iB)
                    if iB == 0:
                        act.wait_ge(g_const, 19)
                    for t in range(TS):
                        act.wait_ge(p_qkv, TS * iB + t + 1)
                        qk = bank[(3, 5)[t % 2]]
                        a.activation(qtok[:, t, :], qk[:, 0:DM], ACT.Copy, scale=SB1["sw"][:, 0, t:t + 1])
                        a.activation(ktok[:, 0, DM * t:DM * (t + 1)], qk[:, DM:2 * DM], ACT.Copy,
                                     scale=SB1["sw"][:, 1, t:t + 1])
                        a.activation(vtok[:, t, :, 0:HD],
                                     bank[(2, 4)[t % 2]][:, 0:DM].rearrange("p (h d) -> p h d", d=HD),
                                     ACT.Copy, scale=SB1["sw"][:, 2, t:t + 1]).then_inc(a_qkv, 1)
                if iC is not None:
                    exps(iC, range(2, BT))
                if iD is not None:
                    act.wait_ge(p_norm2T, iD + 1)
                    wait(act, v_xq_rows, done(slot, B_LAG))
                    a.activation(xT.rearrange("p c n -> p (c n)"), banks(0), ACT.Copy).then_inc(a_norm2T, 1)
                if iD is not None:
                    for t in range(TS):
                        act.wait_ge(p_expert, TS * iD + t + 1)
                        a.activation(EO[:, TS * iD + t, :], bank[6 + t % 2][:, 0:DE], ACT.Copy).then_inc(a_expert, 1)
                if iB is not None:
                    act.wait_ge(v_qk, iB + 1)
                    kT = ktok[:, 1, :].rearrange("p (t n k) -> p t n k", t=TS, n=DBLK)
                    for h in range(2):
                        r = a.activation(KT[:, :, :, 32 * h:32 * (h + 1)], kT, ACT.Copy, scale=head_mask[:, h:h + 1])
                    r.then_inc(a_k_masked, 1)
            act.wait_ge(v_gate_in, 1)
            a.activation(ra[:, 5], ra[:, 3], ACT.Exp).then_inc(a_gate, 1)
            norms = [0]

            def norm(S, i, rows, signal):
                norms[0] += 1
                act.wait_ge(v_norm_in, norms[0])
                for t in range(TS):
                    a.activation(rows(t), H[:, TS * i + t, :], ACT.Identity, bias=S["am"][:, t:t + 1],
                                 scale=S["rstd"][:, t:t + 1]).then_inc(signal, 1)

            for slot in range(STEPS + L_LAG):
                iN, iS, iR, iL = (step_of(slot, lag) for lag in (N_LAG, S_LAG, R_LAG, L_LAG))
                if iN is not None:
                    wait(act, p_norm3T, iN)
                    norm(SE, iN, lambda t: O[:, t, :], a_norm3)
                    act.wait_ge(p_norm3T, iN + 1)
                    wait(act, v_state_re, iN)
                    wait(act, g_input_im, iN)
                    a.activation(xT.rearrange("p c n -> p (c n)"), banks(0), ACT.Copy).then_inc(a_norm3T, 1)
                if iL is not None:
                    act.wait_ge(p_norm4T, iL + 1)
                    wait(act, p_logits, iL)
                    a.activation(x4T.rearrange("p c n -> p (c n)"), banks(4), ACT.Copy).then_inc(a_norm4T, 1)
                if iR is not None:
                    norm(SR, iR, lambda t: X4[:, TS * iR + t, 0:DM], a_norm4)
            act.wait_ge(v_logit_gap, 1)
            a.activation(rs[:, 4, :], rs[:, 3, :], ACT.Exp).then_inc(a_pair_gate, 1)
            act.wait_ge(v_hot, 1)
            a.activation(in_part, in_slot, ACT.Copy, scale=row_p[:, 0:1]).then_inc(a_part, 1)
            a.activation(silu_ready[:], row_p[:], ACT.Silu)

            def slot_rows(j, u):
                act.wait_ge(p_slotT, j + 1)
                a.activation(xrT[:, u].rearrange("p c n -> p (c n)"), bank[u][:, 0:DM], ACT.Copy).then_inc(a_slotT, 1)

            def slot_silu(j, u):
                act.wait_ge(p_up_h, j + 1)
                a.activation(sil[:, u, :], bank[2], ACT.Silu).then_inc(a_silu, 1)

            def slot_act(j, u):
                act.wait_ge(p_actT, j + 1)
                a.activation(actT[:, u].rearrange("p c n -> p (c n)"), bank[4 + u], ACT.Copy).then_inc(a_actT, 1)

            def slot_out(j, u, stored):
                act.wait_ge(p_down, j + 1)
                if stored is not None:
                    act.wait_ge((d_deliver0, d_deliver1)[u], stored)
                a.activation(yrow[:, u, :], bank[6 + u][:, 0:DM], ACT.Copy).then_inc(a_slot_out, 1)

            def slot_step(j, u, stored):
                slot_act(j, u)
                if not isinstance(j, int) or j + 2 < SLOTS:
                    slot_rows(j + 2, u)
                if not isinstance(j, int) or j + 1 < SLOTS:
                    slot_silu(j + 1, 1 - u)
                slot_out(j, u, stored)

            slot_rows(0, 0)
            slot_rows(1, 1)
            slot_silu(0, 0)
            for j in range(PEEL):
                slot_step(j, j % 2, 16 * (j // 2) or None)
            with act.Fori(0, (SLOTS - 2 - PEEL) // 2) as t:
                slot_step(2 * t + PEEL, 1, 16 * t + 16)
                slot_step(2 * t + PEEL + 1, 0, 16 * t + 32)
            for j in range(SLOTS - 2, SLOTS):
                slot_step(j, j % 2, 16 * (j // 2))

        @block.vector
        def _(dve):
            v = nc.vector
            chain = [0]

            def ln(ins):
                chain[0] += 1
                ins.then_inc(v_chain, 1)

            def own():
                dve.wait_ge(v_chain, chain[0])

            asked = [0]

            def ask(ins):
                asked[0] += 1
                ins.then_inc(v_ask, 1)

            def answered(later=0):
                dve.wait_ge(g_pow, asked[0] - later)

            dve.wait_ge(g_const, 16)
            ln(v.tensor_reduce(head_sum[:], ident[:].rearrange("p (b d) -> p b d", d=HD), AX, ALU.add))
            own()
            ln(v.tensor_reduce(head_mask[:], head_sum[:].rearrange("p (n h) -> p h n", h=2), AX, ALU.add))
            dve.wait_ge(d_att, 64)
            v.tensor_reduce(wsum[:], wraw, AX, ALU.add, apply_absolute_value=True).then_inc(v_abs_sum, 1)
            dve.wait_ge(d_vec, 96)
            pr, pim = vec[:, 0, :], vec[:, 1, :]
            t = [sv[:, k, :] for k in range(20)]
            ln(v.tensor_tensor(t[5], pr, pr, ALU.mult))
            ln(v.tensor_tensor(t[6], pim, pim, ALU.mult))
            ln(v.tensor_scalar(t[7], pr, -1.0, None, ALU.mult))
            ln(v.tensor_scalar(t[8], pim, -1.0, None, ALU.mult))
            own()
            v.tensor_tensor(t[5], t[5], t[6], ALU.add).then_inc(v_exp, 1)
            ln(v.tensor_tensor(t[7], t[7], pr, ALU.max))
            ln(v.tensor_tensor(t[8], t[8], pim, ALU.max))
            own()
            ln(v.tensor_tensor(t[9], t[7], t[8], ALU.max))
            own()
            ln(v.tensor_scalar(t[10], t[9], 0.0, None, ALU.is_equal))
            own()
            ln(v.tensor_tensor(t[9], t[9], t[10], ALU.add))
            own()
            ln(v.reciprocal(t[11], t[9]))
            own()
            ln(v.tensor_tensor(t[12], pr, t[11], ALU.mult))
            ln(v.tensor_tensor(t[13], pim, t[11], ALU.mult))
            own()
            ln(v.tensor_tensor(t[12], t[12], t[10], ALU.add))
            own()
            ln(v.tensor_tensor(t[14], t[12], t[12], ALU.mult))
            ln(v.tensor_tensor(t[15], t[13], t[13], ALU.mult))
            own()
            ask(v.tensor_tensor(t[2], t[14], t[15], ALU.add))
            dve.wait_ge(p_abs_sum, 1)
            ln(v.tensor_scalar(wm[:], bank[6][:, 0:4], 1.0 / (DM * DM), 1e-5, ALU.mult, ALU.max))
            own()
            ln(v.reciprocal(wmi[:], wm[:]))
            own()
            for w in range(4):
                ln(v.tensor_scalar(wraw[:, w, :], wraw[:, w, :], wmi[:, w:w + 1], MAGIC, ALU.mult, ALU.add))
            own()
            allw = wraw.rearrange("p w n -> p (w n)")
            ln(v.tensor_scalar(allw, allw, MAGIC, 1.0, ALU.subtract, ALU.min))
            own()
            v.tensor_scalar(wter.rearrange("p w c n -> p (w c n)"), allw, -1.0, None, ALU.max).then_inc(v_ternary, 1)
            answered()
            ln(v.memset(CT[:, :, 0:1], 1.0))
            ln(v.memset(ST[:, :, 0:1], 0.0))
            one = lambda a_: a_.rearrange("p (c a) -> p c a", a=1)
            ln(v.tensor_tensor(CT[:, :, 1:2], one(t[12]), one(t[3]), ALU.mult))
            ln(v.tensor_tensor(ST[:, :, 1:2], one(t[13]), one(t[3]), ALU.mult))
            own()
            n = 1
            while n < L:
                cn = CT[:, :, n:n + 1].to_broadcast([P, CH, n])
                sn = ST[:, :, n:n + 1].to_broadcast([P, CH, n])
                q = [tmpT[:, k, :, 0:n] for k in range(4)]
                ln(v.tensor_tensor(q[0], CT[:, :, 1:n + 1], cn, ALU.mult))
                ln(v.tensor_tensor(q[1], ST[:, :, 1:n + 1], sn, ALU.mult))
                ln(v.tensor_tensor(q[2], CT[:, :, 1:n + 1], sn, ALU.mult))
                ln(v.tensor_tensor(q[3], ST[:, :, 1:n + 1], cn, ALU.mult))
                own()
                ln(v.tensor_tensor(CT[:, :, n + 1:2 * n + 1], q[0], q[1], ALU.subtract))
                ln(v.tensor_tensor(ST[:, :, n + 1:2 * n + 1], q[2], q[3], ALU.add))
                own()
                n *= 2
            q = [tmpT[:, k] for k in range(4)]
            bc = lambda k: one(vec[:, k, :]).to_broadcast([P, CH, L])
            ln(v.tensor_tensor(q[0], CT[:, :, 0:L], bc(2), ALU.mult))
            ln(v.tensor_tensor(q[1], ST[:, :, 0:L], bc(3), ALU.mult))
            ln(v.tensor_tensor(q[2], CT[:, :, 0:L], bc(3), ALU.mult))
            ln(v.tensor_tensor(q[3], ST[:, :, 0:L], bc(2), ALU.mult))
            own()
            ln(v.tensor_tensor(Wr[:], q[0], q[1], ALU.add))
            ln(v.tensor_tensor(Wi[:], q[3], q[2], ALU.subtract))
            own()
            c1, s1 = CT[:, :, 1:2], ST[:, :, 1:2]
            ln(v.tensor_tensor(one(t[14]), one(vec[:, 4, :]), c1, ALU.mult))
            ln(v.tensor_tensor(one(t[15]), one(vec[:, 5, :]), s1, ALU.mult))
            ln(v.tensor_tensor(one(t[16]), one(vec[:, 4, :]), s1, ALU.mult))
            ln(v.tensor_tensor(one(t[17]), one(vec[:, 5, :]), c1, ALU.mult))
            own()
            ln(v.tensor_tensor(t[14], t[14], t[15], ALU.subtract))
            ln(v.tensor_tensor(t[16], t[16], t[17], ALU.add))
            own()
            dve.wait_ge(a_decay, 1)
            ln(v.tensor_tensor(t[18], t[14], t[4], ALU.mult))
            ln(v.scalar_tensor_tensor(t[19], t[16], -1.0, t[4], ALU.mult, ALU.mult))

            def norm_stats(S, rows):
                for t_ in range(TS):
                    ln(v.bn_stats(S["st"][:, t_, :], rows(t_)))
                own()
                for t_ in range(TS):
                    ln(v.bn_aggr(S["mv"][:, t_, :], S["st"][:, t_, :]))
                own()

            def ask_rstd(S):
                ask(v.tensor_scalar(S["ve"][:], S["mv"][:, :, 1], EPS, None, ALU.add))

            def minus_mean(S):
                v.scalar_tensor_tensor(S["am"][:], S["mv"][:, :, 0], -1.0, S["rstd"][:], ALU.mult, ALU.mult
                                       ).then_inc(v_norm_in, 1)

            def scales(S, rows, weights):
                ln(v.tensor_reduce(S["am"][:], rows, AX, ALU.max, apply_absolute_value=True))
                answered()
                own()
                ln(v.tensor_tensor(S["am"][:], S["am"][:], S["rsb"][:], ALU.mult))
                own()
                ln(v.tensor_scalar(S["sa"][:], S["am"][:], 1e-5, 1.0 / 127.0, ALU.max, ALU.mult))
                own()
                ln(v.reciprocal(S["s"][:], S["sa"][:]))
                for n_, (w_, extra) in enumerate(weights):
                    ln(v.tensor_scalar(S["sw"][:, n_, :], S["sa"][:], wm[:, w_:w_ + 1], extra, ALU.mult, ALU.mult))
                own()
                ln(v.tensor_tensor(S["s"][:], S["s"][:], S["rsb"][:], ALU.mult))
                own()

            def minus_max(i, b):
                m = mx[:, b % 2, :]
                s_ = bank[b % 2].rearrange("p (h k) -> p h k", k=32)
                dve.wait_ge(p_scores, BT * i + b + 1)
                ln(v.tensor_reduce(m, s_, AX, ALU.max))
                own()
                wait(dve, v_probsT, BT * i + b - 1)
                v.tensor_tensor(Eb[:, b % 2], s_, m.rearrange("p (h a) -> p h a", a=1).to_broadcast([P, NH, 32]),
                                ALU.subtract).then_inc(v_less_max, 1)

            def turn(i, b):
                dve.wait_ge(a_exp, BT * i + b + 1)
                wait(dve, p_values, BT * i + b - 1)
                v.transpose(PT[:, b % 2].rearrange("p h k -> p (h k)"), Eb[:, b % 2].rearrange("p h k -> p (h k)")
                            ).then_inc(v_probsT, 1)

            for slot in range(SLOTS_OF_STEPS):
                iA, iB, iC, iD = (step_of(slot, lag) for lag in (A_LAG, B_LAG, C_LAG, D_LAG))
                if iD is not None:
                    norm_stats(SD, lambda t_: O[:, t_, :])
                    mean, var = SD["mv"][:, :, 0], SD["mv"][:, :, 1]
                    ln(v.tensor_copy(SD["bs"][:, 0, :], mean))
                    ln(v.tensor_tensor(SD["st"][:, :, 0], mean, mean, ALU.mult))
                    own()
                    v.tensor_tensor(SD["bs"][:, 1, :], SD["st"][:, :, 0], var, ALU.add).then_inc(v_batch_att, 1)
                if iB is not None:
                    i = iB
                    dve.wait_ge(g_embed, i + 1)
                    wait(dve, p_expert, TS * done(slot - 1, D_LAG))
                    norm_stats(SB1, lambda t_: H[:, TS * i + t_, :])
                    ask_rstd(SB1)

                    def batch_var(later=0):
                        answered(later)
                        ln(v.tensor_tensor(SB1["bs"][:, 1, :], SB1["mv"][:, :, 1], SB1["rstd"][:], ALU.mult))
                        own()
                        v.tensor_tensor(SB1["bs"][:, 0, :], SB1["bs"][:, 1, :], SB1["rstd"][:], ALU.mult
                                        ).then_inc(v_batch_in, 1)

                if iD is not None:
                    dve.wait_ge(p_batch_att, iD + 1)
                    ln(v.tensor_copy(SD["bv"][:].rearrange("p a t -> p (a t)"), bank[3][:, 0:2 * TS]))
                    own()
                    mu, e2 = SD["bv"][:, 0, :], SD["bv"][:, 1, :]
                    ln(v.tensor_tensor(SD["am"][:], mu, mu, ALU.mult))
                    own()
                    ln(v.tensor_tensor(e2, e2, SD["am"][:], ALU.subtract))
                    own()
                    ask(v.tensor_scalar(SD["bve"][:], e2, 0.0, EPS, ALU.max, ALU.add))
                    for t_ in range(TS):
                        ln(v.tensor_scalar(O[:, t_, :], O[:, t_, :], mu[:, t_:t_ + 1], None, ALU.subtract))
                    if iB is not None:
                        batch_var(later=1)
                    own()
                    scales(SD, O[:], [(3, 1.0)])
                    for t_ in range(TS):
                        ln(v.tensor_scalar(O[:, t_, :], O[:, t_, :], SD["s"][:, t_:t_ + 1], MAGIC, ALU.mult, ALU.add))
                    own()
                    wait(dve, p_oqT, iD)
                    v.tensor_scalar(oq[:], O[:], MAGIC, 127.0, ALU.subtract, ALU.min).then_inc(v_oq_rows, 1)
                if iB is not None:
                    mean, r_ = SB1["mv"][:, :, 0], SB1["rstd"]
                    if iD is None:
                        batch_var()
                    for t_ in range(TS):
                        ln(v.tensor_scalar(x1[:, t_, :], H[:, TS * iB + t_, :], mean[:, t_:t_ + 1], r_[:, t_:t_ + 1],
                                           ALU.subtract, ALU.mult))
                    dve.wait_ge(p_batch_in, iB + 1)
                    ask(v.tensor_scalar(SB1["bve"][:], bank[2][:, 0:TS], EPS, None, ALU.add))
                    own()
                    wait(dve, a_qkv, TS * iB)
                    scales(SB1, x1[:], [(0, HD ** -0.5), (1, 1.0), (2, 1.0)])
                    for t_ in range(TS):
                        ln(v.tensor_scalar(x1[:, t_, :], x1[:, t_, :], SB1["s"][:, t_:t_ + 1], MAGIC, ALU.mult, ALU.add))
                    own()
                    v.engine_nop().then_inc(v_scales, 1)
                    wait(dve, p_xqT, iB)
                    v.tensor_scalar(xq[:], x1[:], MAGIC, 127.0, ALU.subtract, ALU.min).then_inc(v_xq_rows, 1)
                if iC is not None:
                    minus_max(iC, 0)
                    minus_max(iC, 1)
                if iC is not None:
                    turn(iC, 0)
                    turn(iC, 1)
                if iD is not None:
                    for t_ in range(TS):
                        dve.wait_ge(p_proj, TS * iD + 2 * (t_ // 2) + 2)
                        hrow = H[:, TS * iD + t_, :]
                        ln(v.scalar_tensor_tensor(hrow, bank[6 + t_ // 2][:, DM * (t_ % 2):DM * (t_ % 2 + 1)],
                                                  SD["sw"][:, 0, t_:t_ + 1], hrow, ALU.mult, ALU.add))
                    own()
                    v.engine_nop().then_inc(v_att_added, 1)
                    norm_stats(SD, lambda t_: H[:, TS * iD + t_, :])
                    ask_rstd(SD)
                if iC is not None:
                    minus_max(iC, 2)
                    minus_max(iC, 3)
                if iD is not None:
                    answered()
                    for t_ in range(TS):
                        r = v.tensor_scalar(O[:, t_, :], H[:, TS * iD + t_, :], SD["mv"][:, t_, 0:1],
                                            SD["rstd"][:, t_:t_ + 1], ALU.subtract, ALU.mult)
                    r.then_inc(v_norm2, 1)
                if iC is not None:
                    turn(iC, 2)
                    turn(iC, 3)
                if iB is not None:
                    dve.wait_ge(a_qkv, TS * (iB + 1))
                    wait(dve, p_scores, BT * iB)
                    wait(dve, a_k_masked, iB)
                    if iB == 0:
                        dve.wait_ge(p_ternaryT, CH)
                    v.transpose(QT[:].rearrange("p t n k -> p (t n k)"), qtok[:].rearrange("p t d -> p (t d)"))
                    v.transpose(ktok[:, 1, :], ktok[:, 0, :]).then_inc(v_qk, 1)
                if iC is not None:
                    dve.wait_ge(p_values, BT * (iC + 1))
                    wait(dve, p_norm2T, done(slot, D_LAG))
                    HB = NH // 4
                    rows = [bank[2 + k][:, 0:HB * TS * VW].rearrange("p (h t n) -> p h t n", h=HB, t=TS)
                            for k in range(4)]
                    recs = [rec[:, :, HB * k:HB * (k + 1)].rearrange("p t (h a) -> p h t a", a=1) for k in range(4)]
                    for k in range(4):
                        ln(v.reciprocal(recs[k], rows[k][:, :, :, HD:VW]))
                    own()
                    for k in range(4):
                        ln(v.tensor_tensor(O[:, :, HB * HD * k:HB * HD * (k + 1)].rearrange("p t (h d) -> p h t d", d=HD),
                                           rows[k][:, :, :, 0:HD], recs[k].to_broadcast([P, HB, TS, HD]), ALU.mult))
                    own()
                    v.engine_nop().then_inc(v_att_rows, 1)

            te = lambda a_: a_.rearrange("p (t a) -> p t a", a=1).to_broadcast([P, TILES, E])
            rw = rank_w[:].rearrange("p (a e) -> p a e", a=1).to_broadcast([P, TILES, E])

            def best(logits, m, tie, oh, s1_, s2_):
                ln(v.tensor_reduce(m, logits, AX, ALU.max))
                own()
                ln(v.tensor_tensor(s1_, logits, te(m), ALU.is_equal))
                own()
                ln(v.tensor_tensor(s2_, s1_, rw, ALU.mult))
                own()
                ln(v.tensor_reduce(tie, s2_, AX, ALU.max))
                own()
                ln(v.tensor_tensor(oh, s2_, te(tie), ALU.is_equal))
                own()

            def queue_places(ready):
                dve.wait_ge(ready, 1)
                ct = cum[:, 0]
                ln(v.tensor_copy(ct, bank[7][:, 0:TILES * E].rearrange("p (t e) -> p e t", e=E)))
                own()
                ln(v.tensor_tensor_scan(cum[:, 1].rearrange("p e t -> p (e t)"), reset_t[:].rearrange("p e t -> p (e t)"),
                                        ct.rearrange("p e t -> p (e t)"), 0.0, ALU.mult, ALU.add))
                own()
                ln(v.tensor_tensor(ct, cum[:, 1], ct, ALU.subtract))
                own()
                ln(v.tensor_tensor(ra[:, 7], bank[6][:, 0:TILES * E].rearrange("p (t e) -> p t e", e=E),
                                   ct.rearrange("p e t -> p t e"), ALU.add))
                own()

            dve.wait_ge(a_expert, TILES)
            dve.wait_ge(v_probsT, BT * STEPS)
            dve.wait_ge(g_const, 23)
            ln(v.tensor_copy(lg[:], EO[:, :, DM:DE]))
            own()
            best(lg[:], rs[:, 0, :], rs[:, 1, :], ra[:, 0], ra[:, 1], ra[:, 2])
            v.tensor_copy(mask_b[:], ra[:, 0]).then_inc(v_mask, 1)
            ln(v.tensor_tensor(ra[:, 3], lg[:], te(rs[:, 0, :]), ALU.subtract))
            own()
            v.engine_nop().then_inc(v_gate_in, 1)
            queue_places(p_places)
            ln(v.tensor_scalar(ra[:, 4], ra[:, 7], float(CAPACITY), None, ALU.is_le))
            own()
            ln(v.tensor_tensor(ra[:, 4], ra[:, 4], ra[:, 0], ALU.mult))
            own()
            ln(v.tensor_reduce(rs[:, 2, :], ra[:, 4], AX, ALU.add))
            dve.wait_ge(a_gate, 1)
            ln(v.tensor_reduce(rs[:, 5, :], ra[:, 5], AX, ALU.add))
            own()
            ln(v.reciprocal(rs[:, 6, :], rs[:, 5, :]))
            own()
            ln(v.tensor_tensor(rs[:, 7, :], rs[:, 6, :], rs[:, 2, :], ALU.mult))
            own()
            dve.wait_ge(g_decay, 1 + CH)
            cbl = lambda a_: a_.rearrange("p (c b l) -> p c b l", c=CH, l=L)
            tab = lambda a_: a_.rearrange("p c (a l) -> p c a l", a=1).to_broadcast([P, CH, SB, L])
            for slot in range(STEPS + R_LAG):
                iN, iS, iR = (step_of(slot, lag) for lag in (N_LAG, S_LAG, R_LAG))
                if iN is not None:
                    dve.wait_ge(g_expert_bias, iN + 1)
                    for t_ in range(TS):
                        n = TS * iN + t_
                        ln(v.scalar_tensor_tensor(H[:, n, :], EO[:, n, 0:DM], rs[:, 7, n:n + 1], H[:, n, :],
                                                  ALU.mult, ALU.add))
                    own()
                    norm_stats(SE, lambda t_: H[:, TS * iN + t_, :])
                    ask_rstd(SE)
                if iR is not None:
                    dve.wait_ge(g_turned, 2 * (iR + 1))
                    v.tensor_tensor(uR[iR % 2], uR[iR % 2], uI[iR % 2], ALU.add).then_inc(v_ssm_out, 1)
                if iN is not None:
                    answered()
                    minus_mean(SE)
                if iS is not None:
                    uRs, uIs = uR[iS % 2], uI[iS % 2]
                    dve.wait_ge(a_norm3T, iS + 1)
                    wait(dve, p_ssm_rows, iS - 1)
                    ln(v.tensor_tensor(cbl(uRs), xT.rearrange("p c (b l) -> p c b l", l=L), tab(Wr[:]), ALU.mult))
                    own()
                    for c in range(CH):
                        ln(v.tensor_scalar(cbl(uRs)[:, c, :, 0], cbl(uRs)[:, c, :, 0], t[18][:, c:c + 1], None, ALU.add))
                    own()
                    v.tensor_tensor_scan(uRs, RT, uRs, 0.0, ALU.mult, ALU.add).then_inc(v_state_re, 1)
                if iR is not None:
                    dve.wait_ge(p_ssm_rows, iR + 1)
                    hh = H[:, TS * iR:TS * (iR + 1), :].rearrange("p t d -> p (t d)")
                    ln(v.tensor_tensor(hh, hh, banks(2), ALU.add))
                    own()
                    norm_stats(SR, lambda t_: H[:, TS * iR + t_, :])
                    ask_rstd(SR)
                if iS is not None:
                    dve.wait_ge(g_input_im, iS + 1)
                    for c in range(CH):
                        ln(v.tensor_scalar(cbl(uIs)[:, c, :, 0], cbl(uIs)[:, c, :, 0], t[19][:, c:c + 1], None, ALU.add))
                    own()
                    v.tensor_tensor_scan(uIs, RT, uIs, 0.0, ALU.mult, ALU.add).then_inc(v_state_im, 1)
                if iR is not None:
                    answered()
                    minus_mean(SR)

            dve.wait_ge(p_logits, STEPS)
            ln(v.tensor_copy(lg[:], bank[6][:, 0:TILES * E].rearrange("p (t e) -> p t e", e=E)))
            own()
            best(lg[:], rs[:, 0, :], rs[:, 1, :], ra[:, 0], ra[:, 1], ra[:, 2])
            ln(v.scalar_tensor_tensor(ra[:, 3], ra[:, 0], -1e30, lg[:], ALU.mult, ALU.add))
            own()
            best(ra[:, 3], rs[:, 2, :], rs[:, 1, :], ra[:, 4], ra[:, 1], ra[:, 2])
            v.tensor_tensor(mask_b[:], ra[:, 0], ra[:, 4], ALU.add).then_inc(v_mask2, 1)
            v.tensor_tensor(rs[:, 3, :], rs[:, 2, :], rs[:, 0, :], ALU.subtract).then_inc(v_logit_gap, 1)
            queue_places(p_places2)
            cnt = cum[:, 1, :, TILES - 1]
            ln(v.tensor_scalar(tb[:, 0, :], cnt, float(P - 1), 1.0 / P, ALU.add, ALU.mult))
            own()
            ln(v.tensor_scalar(tb[:, 0, :], tb[:, 0, :], 0.5 - 1.0 / (2 * P), MAGIC, ALU.subtract, ALU.add))
            own()
            ln(v.tensor_scalar(tb[:, 0, :], tb[:, 0, :], MAGIC, None, ALU.subtract))
            own()
            ln(v.tensor_tensor_scan(tb[:, 1, :], ones_e[:], tb[:, 0, :], 0.0, ALU.mult, ALU.add))
            own()
            ln(v.tensor_tensor(tb[:, 2, :], tb[:, 1, :], tb[:, 0, :], ALU.subtract))
            own()
            ln(v.tensor_scalar(tb[:, 3, :], tb[:, 2, :], float(P), -1.0, ALU.mult, ALU.add))
            own()
            eb = lambda a_, n_: a_.rearrange("p (a e) -> p a e", a=1).to_broadcast([P, n_, E])
            ln(v.tensor_tensor(ra[:, 7], ra[:, 7], eb(tb[:, 3, :], TILES), ALU.add))
            own()
            for k, oh in enumerate((ra[:, 0], ra[:, 4])):
                ln(v.tensor_tensor(ra[:, 5 + k], ra[:, 7], oh, ALU.mult))
            own()
            for k in range(2):
                ln(v.tensor_reduce(rs[:, 5 + k, :], ra[:, 5 + k], AX, ALU.add))
            own()
            place, tile_of, row_of = (slot_of[:, n] for n in range(3))
            ln(v.tensor_scalar(place, rs[:, 5:7, :], (P - 1) / 2, 1.0 / P, ALU.subtract, ALU.mult))
            own()
            ln(v.tensor_scalar(place, place, MAGIC, None, ALU.add))
            own()
            ln(v.tensor_scalar(tile_of, place, MAGIC, None, ALU.subtract))
            own()
            kt = lambda a_, n_: a_.rearrange("p k (t a) -> p k t a", a=1).to_broadcast([P, 2, TILES, n_])
            v.tensor_tensor(in_slot, kt(tile_of, SLOTS),
                            slot_no[:].rearrange("p (k t s) -> p k t s", k=1, t=1).to_broadcast([P, 2, TILES, SLOTS]),
                            ALU.is_equal).then_inc(v_hot, 1)
            ln(v.scalar_tensor_tensor(row_of, tile_of, -float(P), rs[:, 5:7, :], ALU.mult, ALU.add))
            own()
            for k in range(2):
                v.tensor_tensor(in_row[:, k], kt(row_of, P)[:, k],
                                row_no[:].rearrange("p (t s) -> p t s", t=1).to_broadcast([P, TILES, P]),
                                ALU.is_equal).then_inc(v_row, 1)
            ln(v.tensor_tensor(cmp, eb(tb[:, 1, :], SLOTS),
                               slot_no[:].rearrange("p (s a) -> p s a", a=1).to_broadcast([P, SLOTS, E]), ALU.is_le))
            own()
            ln(v.tensor_reduce(exf[:], cmp, AX, ALU.add))
            own()
            v.tensor_scalar(exi[:], exf[:], float(E - 1), None, ALU.min).then_inc(v_slot_expert, 1)
            dve.wait_ge(p_table, 1)
            tile1, row = (bank[5 - n][:, 0:SLOTS] for n in range(2))
            f = [src_f[:, n, :] for n in range(3)]
            ln(v.tensor_scalar(f[0], tile1, float(P), -float(P), ALU.mult, ALU.add))
            ln(v.tensor_scalar(f[1], tile1, TILES + 0.5, -float(NTOK), ALU.is_gt, ALU.mult))
            ln(v.scalar_tensor_tensor(f[2], tile1, 0.5, unread[:], ALU.is_lt, ALU.mult))
            own()
            ln(v.tensor_tensor(f[0], f[0], row, ALU.add))
            own()
            ln(v.tensor_tensor(f[1], f[1], f[0], ALU.add))
            ln(v.tensor_tensor(f[2], f[2], f[0], ALU.add))
            own()
            ln(v.tensor_scalar(src_i[:], f[1], 0.0, None, ALU.max))
            ln(v.tensor_copy(dst_i[:], f[2]))
            own()
            v.engine_nop().then_inc(v_src, 1)
            dve.wait_ge(a_pair_gate, 1)
            ln(v.tensor_scalar(rs[:, 7, :], rs[:, 4, :], 1.0, None, ALU.add))
            own()
            ln(v.reciprocal(rs[:, 8, :], rs[:, 7, :]))
            own()
            ln(v.tensor_tensor(rs[:, 9, :], rs[:, 8, :], rs[:, 4, :], ALU.mult))
            own()

            def slot_gate(j, u):
                dve.wait_ge(a_silu, j + 1)
                dve.wait_ge(p_up_g, j + 1)
                v.tensor_tensor(sil[:, u, :], sil[:, u, :], bank[3], ALU.mult).then_inc(v_gated, 1)

            slot_gate(0, 0)
            with dve.Fori(0, (SLOTS - 1) // 2) as t_:
                slot_gate(2 * t_ + 1, 1)
                slot_gate(2 * t_ + 2, 0)
            for i in range(STEPS):
                dve.wait_ge(d_back[i], 32)
                for n in range(TS * i, TS * (i + 1)):
                    ln(v.scalar_tensor_tensor(H[:, n, :], back[0][:, n, :], rs[:, 8, n:n + 1], H[:, n, :],
                                              ALU.mult, ALU.add))
                own()
                for n in range(TS * i, TS * (i + 1)):
                    v.scalar_tensor_tensor(H[:, n, :], back[1][:, n, :], rs[:, 9, n:n + 1], H[:, n, :],
                                           ALU.mult, ALU.add).then_inc(v_final, 1)

        @block.tensor
        def _(pe):
            mm = nc.tensor.matmul
            tr = nc.tensor.transpose
            def layer1(i, c):
                if c == 0:
                    if i == 0:
                        pe.wait_ge(d_w1, 32)
                    pe.wait_ge(a_pad, i + 1)
                    pe.wait_ge((d_x0, d_x1)[i % 2], 32 * (i // 2 + 1))
                wait(pe, a_hidden, CH * (i - 1) + c + 1)
                wait(pe, v_less_max, BT * done(i - 1, C_LAG))
                wait(pe, a_norm2T, done(i - 1, D_LAG))
                for r in range(STRIDE):
                    last = mm(bank[c], W1s[:, r, P * c:P * (c + 1)],
                              xin[:, i % 2].rearrange("p b (l s) -> p b l s", s=STRIDE)[:, :, :, r],
                              start=(r == 0), stop=(r == STRIDE - 1))
                last.then_inc(p_layer1, 1)

            def layer2(i, slot):
                pe.wait_ge(a_hidden, CH * (i + 1))
                if i == 0:
                    pe.wait_ge(d_w2, 16)
                    pe.wait_ge(v_ternary, 1)
                wait(pe, a_embed, i)
                wait(pe, a_expert, TS * done(slot - 1, D_LAG))
                for t in range(TS):
                    for c in range(CH):
                        last = mm(bank[6 + t // 2][:, DM * (t % 2):DM * (t % 2 + 1)], h1T[:, c, P * t:P * (t + 1)],
                                  W2s[:, c, :], start=(c == 0), stop=(c == CH - 1))
                    last.then_inc(p_layer2, 1)

            def scores(i, slot, batches):
                pe.wait_ge(a_k_masked, i + 1)
                pe.wait_ge(a_hidden, CH * done(slot, A_LAG))
                wait(pe, a_norm2T, done(slot - 1, D_LAG))
                for b in batches:
                    wait(pe, v_less_max, BT * i + b - 1)
                    for n in range(DBLK):
                        for t in range(TS):
                            last = mm(bank[b % 2][32 * t:32 * t + 32, 64 * n:64 * n + 64],
                                      QT[32 * b:32 * b + 32, t, n, :], KT[32 * b:32 * b + 32, t, n, :],
                                      start=True, stop=True)
                    last.then_inc(p_scores, 1)

            def values(i, slot, batches):
                pe.wait_ge(d_vp, 16 * BT * TS * (i + 1))
                wait(pe, a_qkv, TS * done(slot, B_LAG))
                for b in batches:
                    pe.wait_ge(v_probsT, BT * i + b + 1)
                    for h in range(NH):
                        w = TS * VW
                        last = mm(bank[2 + h // 4][32 * b:32 * b + 32, w * (h % 4):w * (h % 4 + 1)],
                                  PT[:, b % 2, h, :], Vx[:, b, :, h, :], start=True, stop=True)
                    last.then_inc(p_values, 1)

            for slot in range(SLOTS_OF_STEPS):
                iA, iB, iC, iD = (step_of(slot, lag) for lag in (A_LAG, B_LAG, C_LAG, D_LAG))
                if iA is not None:
                    layer1(iA, 0)
                if iA == 0:
                    pe.wait_ge(g_const, 19)
                    pe.wait_ge(v_abs_sum, 1)
                    mm(bank[6][:, 0:4], ones[:], wsum[:], start=True, stop=True).then_inc(p_abs_sum, 1)
                if iD is not None:
                    pe.wait_ge(v_batch_att, iD + 1)
                    pe.wait_ge(v_att_rows, done(slot - 1, C_LAG))
                    mm(bank[3][:, 0:2 * TS], batch_mean[:], SD["bs"][:].rearrange("p a t -> p (a t)"),
                       start=True, stop=True).then_inc(p_batch_att, 1)
                if iC is not None and iA is None:
                    scores(iC, slot, range(0, 2))
                if iA is not None:
                    layer1(iA, 1)
                if iB is not None:
                    pe.wait_ge(v_batch_in, iB + 1)
                    wait(pe, v_att_rows, done(slot - 1, C_LAG))
                    mm(bank[2][:, 0:TS], batch_mean[:], SB1["bs"][:, 0, :], start=True, stop=True).then_inc(p_batch_in, 1)
                if iA == 0:
                    pe.wait_ge(v_ternary, 1)
                    for c in range(CH):
                        for w in range(4):
                            for o in range(CH):
                                last = tr(bank[4 + c].bitcast(BF16)[:, DM * w + P * o:DM * w + P * (o + 1)],
                                          wter[:, w, o, P * c:P * (c + 1)], ident_b[:])
                        last.then_inc(p_ternaryT, 1)
                if iA is not None:
                    layer2(iA, slot)
                    if iC is not None:
                        scores(iC, slot, range(0, 2))
                if iD is not None:
                    pe.wait_ge(v_oq_rows, iD + 1)
                    for c in range(CH):
                        for t in range(TS):
                            last = tr(bank[3].bitcast(BF16)[:, SN * c + P * t:SN * c + P * (t + 1)],
                                      oq[:, t, P * c:P * (c + 1)], ident_b[:])
                    last.then_inc(p_oqT, 1)
                if iB is not None:
                    pe.wait_ge(v_xq_rows, iB + 1)
                    for c in range(CH):
                        for t in range(TS):
                            last = tr(bank[4].bitcast(BF16)[:, SN * c + P * t:SN * c + P * (t + 1)],
                                      xq[:, t, P * c:P * (c + 1)], ident_b[:])
                    last.then_inc(p_xqT, 1)
                if iD is not None:
                    pe.wait_ge(a_oqT, iD + 1)
                    wait(pe, a_embed, done(slot, A_LAG))
                    wait(pe, a_expert, TS * done(slot - 1, D_LAG))
                    for t in range(TS):
                        for c in range(CH):
                            last = mm(bank[6 + t // 2][:, DM * (t % 2):DM * (t % 2 + 1)], oqT[:, c, P * t:P * (t + 1)],
                                      WT[:, c, 3, :], start=(c == 0), stop=(c == CH - 1))
                        last.then_inc(p_proj, 1)
                if iB is not None:
                    if iB == 0:
                        pe.wait_ge(a_ternaryT, CH)
                    pe.wait_ge(a_xqT, iB + 1)
                    wait(pe, a_oqT, done(slot, D_LAG))
                    pe.wait_ge(v_xq_rows, iB + 1)
                    for t in range(TS):
                        wait(pe, a_qkv, TS * iB + t - 1)
                        for c in range(CH):
                            mm(bank[(3, 5)[t % 2]], xqT[:, c, P * t:P * (t + 1)],
                               WT[:, c, 0:2, :].rearrange("p w d -> p (w d)"), start=(c == 0), stop=(c == CH - 1))
                        for c in range(CH):
                            last = mm(bank[(2, 4)[t % 2]][:, 0:DM], xqT[:, c, P * t:P * (t + 1)],
                                      WT[:, c, 2, :], start=(c == 0), stop=(c == CH - 1))
                        last.then_inc(p_qkv, 1)
                if iC is not None:
                    scores(iC, slot, range(2, BT))
                if iC is not None:
                    values(iC, slot, range(0, 2))
                if iD is not None:
                    pe.wait_ge(v_norm2, iD + 1)
                    wait(pe, v_less_max, BT * done(slot, C_LAG))
                    for c in range(CH):
                        for t in range(TS):
                            last = tr(bank[c][:, P * t:P * (t + 1)], O[:, t, P * c:P * (c + 1)], ident[:])
                    last.then_inc(p_norm2T, 1)
                if iC is not None:
                    values(iC, slot, range(2, BT))
                if iD is not None:
                    pe.wait_ge(a_norm2T, iD + 1)
                    if iD == 0:
                        pe.wait_ge(d_we, 48)
                    pe.wait_ge(v_att_added, iD + 1)
                    for t in range(TS):
                        wait(pe, a_expert, TS * iD + t - 1)
                        for c in range(CH):
                            last = mm(bank[6 + t % 2][:, 0:DE], xT[:, c, P * t:P * (t + 1)], WE[:, c, :],
                                      start=(c == 0), stop=(c == CH - 1))
                        last.then_inc(p_expert, 1)

            def places(ready, signal):
                pe.wait_ge(ready, 1)
                mk = mask_b[:].rearrange("p t e -> p (t e)")
                mm(bank[6][:, 0:TILES * E], tri_b[:], mk, start=True, stop=True)
                mm(bank[7][:, 0:TILES * E], ones_b[:], mk, start=True, stop=True).then_inc(signal, 1)

            pe.wait_ge(a_expert, TILES)
            places(v_mask, p_places)
            for slot in range(STEPS + L_LAG):
                iN, iS, iR, iL = (step_of(slot, lag) for lag in (N_LAG, S_LAG, R_LAG, L_LAG))
                if iR is not None:
                    pe.wait_ge(v_ssm_out, iR + 1)
                    for t in range(TS):
                        for c in range(CH):
                            last = tr(banks(2)[:, DM * t + P * c:DM * t + P * (c + 1)],
                                      uR[iR % 2][:, SN * c + P * t:SN * c + P * (t + 1)], ident[:])
                    last.then_inc(p_ssm_rows, 1)
                if iN is not None:
                    wait(pe, a_norm3T, iN)
                    for t in range(TS):
                        pe.wait_ge(a_norm3, TS * iN + t + 1)
                        for c in range(CH):
                            last = tr(bank[c][:, P * t:P * (t + 1)], O[:, t, P * c:P * (c + 1)], ident[:])
                    last.then_inc(p_norm3T, 1)
                if iL is not None:
                    for t in range(TS):
                        pe.wait_ge(a_norm4, TS * iL + t + 1)
                        for c in range(CH):
                            last = tr(bank[4 + c][:, P * t:P * (t + 1)], X4[:, TS * iL + t, P * c:P * (c + 1)], ident[:])
                    last.then_inc(p_norm4T, 1)
                    pe.wait_ge(a_norm4T, iL + 1)
                    for t in range(TS):
                        for c in range(CH):
                            last = mm(bank[6][:, E * (TS * iL + t):E * (TS * iL + t + 1)], x4T[:, c, P * t:P * (t + 1)], Wgs[:, c, :],
                                      start=(c == 0), stop=(c == CH - 1))
                    last.then_inc(p_logits, 1)
            places(v_mask2, p_places2)
            pe.wait_ge(g_tile, 1)
            pe.wait_ge(a_part, 1)
            for k in range(2):
                pe.wait_ge(v_row, k + 1)
                for t in range(TILES):
                    for n, what in enumerate((in_tile, in_part)):
                        last = mm(bank[5 - n][:, 0:SLOTS], in_row[:, k, t, :], what[:, k, t, :],
                                  start=(k == 0 and t == 0), stop=(k == 1 and t == TILES - 1))
            last.then_inc(p_table, 1)
            pe.wait_ge(v_slot_expert, 1)
            pe.wait_ge(d_moe, 32)
            pe.wait_ge(d_m3, 16)
            slot_in = (d_fetch0, d_fetch1)

            def slot_rows(j, u, loads):
                pe.wait_ge(slot_in[u], loads)
                for c in range(CH):
                    last = tr(bank[u][:, P * c:P * (c + 1)], xrow[:, u, P * c:P * (c + 1)], ident[:])
                last.then_inc(p_slotT, 1)

            def slot_up(j, u):
                e = pe.value_load(exi[0:1, bass.ds(j, 1)], min_val=0, max_val=E - 1)
                pe.wait_ge(a_slotT, j + 1)
                for w, z, signal in ((M1s, bank[2], p_up_h), (M2s, bank[3], p_up_g)):
                    for c in range(CH):
                        last = mm(z, xrT[:, u, c, :], w[:, bass.ds(e, 1), c, :].rearrange("p a h -> p (a h)"),
                                  start=(c == 0), stop=(c == CH - 1))
                    last.then_inc(signal, 1)

            def slot_act(j, u):
                pe.wait_ge(v_gated, j + 1)
                for c in range(HC):
                    last = tr(bank[4 + u][:, P * c:P * (c + 1)], sil[:, u, P * c:P * (c + 1)], ident[:])
                last.then_inc(p_actT, 1)

            def slot_down(j, u):
                e = pe.value_load(exi[0:1, bass.ds(j, 1)], min_val=0, max_val=E - 1)
                pe.wait_ge(a_actT, j + 1)
                if not (isinstance(j, int) and j < 2):
                    pe.wait_ge(a_slot_out, j - 1)
                for c in range(HC):
                    last = mm(bank[6 + u][:, 0:DM], actT[:, u, c, :],
                              M3s[:, bass.ds(e, 1), c, :].rearrange("p a d -> p (a d)"),
                              start=(c == 0), stop=(c == HC - 1))
                last.then_inc(p_down, 1)

            def slot_step(j, u, loads):
                slot_act(j, u)
                if not isinstance(j, int) or j + 2 < SLOTS:
                    slot_rows(j + 2, u, loads)
                if not isinstance(j, int) or j + 1 < SLOTS:
                    slot_up(j + 1, 1 - u)
                slot_down(j, u)

            slot_rows(0, 0, 16)
            slot_rows(1, 1, 16)
            slot_up(0, 0)
            for j in range(PEEL):
                slot_step(j, j % 2, 16 * ((j + 2) // 2 + 1))
            with pe.Fori(0, (SLOTS - 2 - PEEL) // 2) as t:
                slot_step(2 * t + PEEL, 1, 16 * t + 48)
                slot_step(2 * t + PEEL + 1, 0, 16 * t + 64)
            for j in range(SLOTS - 2, SLOTS):
                slot_step(j, j % 2, None)


_INS = ['x', 'L0_tok_W1', 'L0_tok_b1', 'L0_tok_W2', 'L0_tok_b2', 'L0_attn_w_q', 'L0_attn_w_k', 'L0_attn_w_v',
        'L0_attn_w_o', 'L0_ffn_w_gate', 'L0_ffn_w_expert', 'L0_ffn_b_expert', 'L1_attn_phazor_real',
        'L1_attn_phazor_imag', 'L1_attn_phazor_init_real', 'L1_attn_phazor_init_imag', 'L1_attn_last_conv_real',
        'L1_attn_last_conv_imag', 'L1_ffn_Wg', 'L1_ffn_W1', 'L1_ffn_W2', 'L1_ffn_W3']
_OUTS = [((64, 32, 256), 'float32')]


def kernel(**inputs):
    import numpy as _np
    import concourse.bacc as _bacc
    from concourse import mybir as _mybir
    from concourse.bass_utils import run_bass_kernel_spmd as _run

    nc = _bacc.Bacc("TRN2", target_bir_lowering=False, num_devices=1)
    arrays, args = {}, []
    for name in _INS:
        a = _np.ascontiguousarray(inputs[name])
        arrays[f"in_{name}_dram"] = a
        args.append(nc.dram_tensor(f"in_{name}_dram", a.shape, _mybir.dt.from_np(a.dtype), kind="ExternalInput").ap())
    for i, (shape, dtype) in enumerate(_OUTS):
        dt = _mybir.dt.from_np(_np.dtype(dtype))
        args.append(nc.dram_tensor(f"out_{i}_dram", shape, dt, kind="ExternalOutput").ap())
    audio_tower_kernel(nc, *args)
    r = _run(nc, [arrays], core_ids=[0])
    got = tuple(r.results[0][f"out_{i}_dram"] for i in range(len(_OUTS)))
    return got[0]
```
